# Optimizing a Trainium2 kernel written in Bass

```python
import numpy as np
import jax
import jax.numpy as jnp

def _softmax(x, axis=-1):
    return jax.nn.softmax(x, axis=axis)

def _gelu(x):
    return jax.nn.gelu(x, approximate=True)

def _silu(x):
    return jax.nn.silu(x)

def _sigmoid(x):
    return jax.nn.sigmoid(x)

def _layernorm(x, axis=-1, eps=1e-05):
    m = jnp.mean(x, axis=axis, keepdims=True)
    v = jnp.var(x, axis=axis, keepdims=True)
    return (x - m) / jnp.sqrt(v + eps)

def _scatter_add(tgt, idx, src, axis=0):
    return tgt.at[idx].add(src)

def _segment_sum(src, seg, n):
    return jax.ops.segment_sum(src, seg, n)
kernel_name = 'mk_flamingo_gated_d1_seqx_r8_f01f62'

def setup_inputs(seed: int=0):
    np.random.seed(seed)
    _w = jnp.asarray

    def _rec_inputs():
        import jax
        import jax.numpy as jnp
        _rk = jax.random.key(seed)
        x = -0.000125 + 0.9999 * jax.random.normal(jax.random.fold_in(_rk, 1), (4, 256, 256), jnp.float32)
        _lenS = 256 - jax.random.randint(jax.random.fold_in(_rk, 7), (4,), 0, max(1, 256 // 4) + 1, jnp.int32)
        _lenS2 = 256 - jax.random.randint(jax.random.fold_in(_rk, 8), (4,), 0, max(1, 256 // 4) + 1, jnp.int32)
        fside_BxS2xS2_0 = -3.05549e-07 + 0.0199987 * jax.random.normal(jax.random.fold_in(_rk, 11), (4, 256, 256), jnp.float32)
        _ctx_1024P = jax.random.normal(jax.random.fold_in(_rk, 12), (4, 16, 128), jnp.float32)
        _ctx_1024c = jax.random.dirichlet(jax.random.fold_in(_rk, 512), 0.3 * jnp.ones((16,), jnp.float32), (4, 256))
        _ctx_1024t = jnp.einsum('bsk,bkd->bsd', _ctx_1024c, _ctx_1024P)
        _ctx_1024t = _ctx_1024t * jax.lax.rsqrt(jnp.mean(jnp.square(_ctx_1024t)) + 1e-12) * 0.953939
        ctx_1024 = 6.82029e-06 + 0.0200006 * (_ctx_1024t + 0.3 * jax.random.normal(jax.random.fold_in(_rk, 612), (4, 256, 128), jnp.float32))
        _g = jax.random.normal(jax.random.fold_in(_rk, 9001), (2, 1), jnp.float32)
        _g = jnp.sign(_g) * jnp.maximum(jnp.abs(_g), 1.0) + (_g == 0) * 1.0
        g_xattn = _g[0]
        g_ffn = _g[1]
        return (x, fside_BxS2xS2_0, ctx_1024, g_xattn, g_ffn)
    x, fside_BxS2xS2_0, ctx_1024, g_xattn, g_ffn = _rec_inputs()

    def _L0_xattn_setup():
        import jax, jax.numpy as jnp
        import numpy as np
        EPS = 1e-06
        QMAX = 127.0

        def _smooth_quant_linear(x, w):
            amax_x = jnp.max(jnp.abs(x), axis=0)
            amax_w = jnp.max(jnp.abs(w), axis=0)
            s = jnp.sqrt(jnp.maximum(amax_x, EPS) / jnp.maximum(amax_w, EPS))
            s = jnp.maximum(s, EPS)
            xs = x / s
            ws = w * s
            x_scale = jnp.maximum(jnp.max(jnp.abs(xs), axis=-1, keepdims=True), EPS) / QMAX
            w_scale = jnp.maximum(jnp.max(jnp.abs(ws), axis=-1, keepdims=True), EPS) / QMAX
            x_q = jnp.clip(jnp.round(xs / x_scale), -QMAX, QMAX)
            w_q = jnp.clip(jnp.round(ws / w_scale), -QMAX, QMAX)
            return x_q @ w_q.T * x_scale * w_scale.T

        def _expert_forward(xe, guw, dw):
            h = _smooth_quant_linear(xe, guw)
            gate, up = jnp.split(h, 2, axis=-1)
            a = jax.nn.silu(gate) * up
            return _smooth_quant_linear(a, dw)
        key = jax.random.key(seed)
        k1, k2, k3 = jax.random.split(key, 3)
        E, T, D, I = (8, 256, 256, 128)
        x = jax.random.normal(k1, (E, T, D), dtype=jnp.float32)
        gate_up_weight = jax.random.normal(k2, (E, 2 * I, D), dtype=jnp.float32) * 0.02
        down_weight = jax.random.normal(k3, (E, D, I), dtype=jnp.float32) * 0.02
        return {'x': x, 'gate_up_weight': gate_up_weight, 'down_weight': down_weight}
    _L0_xattn_all = _L0_xattn_setup()
    _L0_xattn_in = {k: v for k, v in _L0_xattn_all.items() if k in ()}
    del _L0_xattn_all

    def _L0_ffn_setup():
        import jax, jax.numpy as jnp
        import numpy as np
        B, S, H, I, E, K, R = (4, 128, 256, 896, 8, 2, 64)
        SCALING = 16.0 / 64.0
        key = jax.random.key(seed)
        ks = jax.random.split(key, 14)
        rn = lambda k, shape, sc: jax.random.normal(k, shape, jnp.float32) * sc
        x = rn(ks[0], (B, S, H), 1.0)
        expert_wealth = jnp.full((E,), 100.0, jnp.float32)
        conf_W = rn(ks[1], (E, H), 0.02)
        conf_b = ((jnp.arange(E) - E / 2.0) * 0.1).astype(jnp.float32)
        base_gate = rn(ks[2], (H, I), H ** (-0.5))
        base_up = rn(ks[3], (H, I), H ** (-0.5))
        base_down = rn(ks[4], (I, H), I ** (-0.5))
        gate_A = rn(ks[5], (E, H, R), H ** (-0.5))
        gate_B = rn(ks[6], (E, R, I), 0.01)
        up_A = rn(ks[7], (E, H, R), H ** (-0.5))
        up_B = rn(ks[8], (E, R, I), 0.01)
        down_A = rn(ks[9], (E, I, R), I ** (-0.5))
        down_B = rn(ks[10], (E, R, H), 0.01)
        return {'hidden_states': x, 'expert_wealth': expert_wealth, 'conf_W': conf_W, 'conf_b': conf_b, 'base_gate': base_gate, 'base_up': base_up, 'base_down': base_down, 'gate_A': gate_A, 'gate_B': gate_B, 'up_A': up_A, 'up_B': up_B, 'down_A': down_A, 'down_B': down_B}
    _L0_ffn_all = _L0_ffn_setup()
    _L0_ffn_in = {k: v for k, v in _L0_ffn_all.items() if k in ('expert_wealth', 'conf_W', 'conf_b', 'base_gate', 'base_up', 'base_down', 'gate_A', 'gate_B', 'up_A', 'up_B', 'down_A', 'down_B')}
    del _L0_ffn_all
    return {'x': x, 'fside_BxS2xS2_0': fside_BxS2xS2_0, 'ctx_1024': ctx_1024, 'g_xattn': g_xattn, 'g_ffn': g_ffn, 'L0_ffn_expert_wealth': _L0_ffn_in['expert_wealth'], 'L0_ffn_conf_W': _L0_ffn_in['conf_W'], 'L0_ffn_conf_b': _L0_ffn_in['conf_b'], 'L0_ffn_base_gate': _L0_ffn_in['base_gate'], 'L0_ffn_base_up': _L0_ffn_in['base_up'], 'L0_ffn_base_down': _L0_ffn_in['base_down'], 'L0_ffn_gate_A': _L0_ffn_in['gate_A'], 'L0_ffn_gate_B': _L0_ffn_in['gate_B'], 'L0_ffn_up_A': _L0_ffn_in['up_A'], 'L0_ffn_up_B': _L0_ffn_in['up_B'], 'L0_ffn_down_A': _L0_ffn_in['down_A'], 'L0_ffn_down_B': _L0_ffn_in['down_B']}

def reference(x, fside_BxS2xS2_0, ctx_1024, g_xattn, g_ffn, L0_ffn_expert_wealth, L0_ffn_conf_W, L0_ffn_conf_b, L0_ffn_base_gate, L0_ffn_base_up, L0_ffn_base_down, L0_ffn_gate_A, L0_ffn_gate_B, L0_ffn_up_A, L0_ffn_up_B, L0_ffn_down_A, L0_ffn_down_B):
    import jax
    import jax.numpy as jnp

    def _L0_xattn_ref(x, gate_up_weight, down_weight):
        import jax, jax.numpy as jnp
        import numpy as np
        EPS = 1e-06
        QMAX = 127.0

        def _smooth_quant_linear(x, w):
            amax_x = jnp.max(jnp.abs(x), axis=0)
            amax_w = jnp.max(jnp.abs(w), axis=0)
            s = jnp.sqrt(jnp.maximum(amax_x, EPS) / jnp.maximum(amax_w, EPS))
            s = jnp.maximum(s, EPS)
            xs = x / s
            ws = w * s
            x_scale = jnp.maximum(jnp.max(jnp.abs(xs), axis=-1, keepdims=True), EPS) / QMAX
            w_scale = jnp.maximum(jnp.max(jnp.abs(ws), axis=-1, keepdims=True), EPS) / QMAX
            x_q = jnp.clip(jnp.round(xs / x_scale), -QMAX, QMAX)
            w_q = jnp.clip(jnp.round(ws / w_scale), -QMAX, QMAX)
            return x_q @ w_q.T * x_scale * w_scale.T

        def _expert_forward(xe, guw, dw):
            h = _smooth_quant_linear(xe, guw)
            gate, up = jnp.split(h, 2, axis=-1)
            a = jax.nn.silu(gate) * up
            return _smooth_quant_linear(a, dw)
        return jax.vmap(_expert_forward)(x, gate_up_weight, down_weight)

    def _L0_ffn_ref(hidden_states, expert_wealth, conf_W, conf_b, base_gate, base_up, base_down, gate_A, gate_B, up_A, up_B, down_A, down_B):
        import jax, jax.numpy as jnp
        import numpy as np
        B, S, H, I, E, K, R = (4, 128, 256, 896, 8, 2, 64)
        SCALING = 16.0 / 64.0
        x = hidden_states
        conf = jax.nn.sigmoid(jnp.einsum('bsh,eh->bse', x, conf_W) + conf_b)
        bids = conf * expert_wealth
        top_bids, sel = jax.lax.top_k(bids, K)
        routing = jax.nn.softmax(top_bids, axis=-1)
        base_g = jnp.einsum('bsh,hi->bsi', x, base_gate)
        base_u = jnp.einsum('bsh,hi->bsi', x, base_up)
        out = jnp.zeros_like(x)
        for e in range(E):
            g = base_g + x @ gate_A[e] @ gate_B[e] * SCALING
            u = base_u + x @ up_A[e] @ up_B[e] * SCALING
            h = jax.nn.silu(g) * u
            oe = h @ base_down + h @ down_A[e] @ down_B[e] * SCALING
            we = jnp.sum(routing * (sel == e), axis=-1)
            out = out + we[..., None] * oe
        return out
    x = x + jnp.tanh(g_xattn[0]) * _L0_xattn_ref(_layernorm(x, axis=-1), fside_BxS2xS2_0, ctx_1024)
    x = x + jnp.tanh(g_ffn[0]) * _L0_ffn_ref(_layernorm(x, axis=-1), L0_ffn_expert_wealth, L0_ffn_conf_W, L0_ffn_conf_b, L0_ffn_base_gate, L0_ffn_base_up, L0_ffn_base_down, L0_ffn_gate_A, L0_ffn_gate_B, L0_ffn_up_A, L0_ffn_up_B, L0_ffn_down_A, L0_ffn_down_B)
    return x

_drawn_inputs = setup_inputs


def setup_inputs(seed=0):
    import zlib

    import numpy as np

    out = dict(_drawn_inputs(seed))
    spreads = {'L0_ffn_expert_wealth': (100.0, 0.6)}
    factors = {'fside_BxS2xS2_0': 5.904,
     'ctx_1024': 5.792,
     'L0_ffn_conf_W': 7.166,
     'L0_ffn_conf_b': 4.886,
     'L0_ffn_gate_A': 5.682,
     'L0_ffn_gate_B': 5.668,
     'L0_ffn_up_A': 5.858,
     'L0_ffn_up_B': 5.821,
     'L0_ffn_down_A': 5.927,
     'L0_ffn_down_B': 5.881}
    for name, (base, spread) in spreads.items():
        noise = np.random.default_rng([zlib.crc32(name.encode()), seed]).standard_normal(out[name].shape)
        drawn = base * np.exp(spread * noise) if base else spread * noise
        out[name] = jnp.asarray(drawn.astype(out[name].dtype))
    for name, factor in factors.items():
        out[name] = (out[name] * factor).astype(out[name].dtype)
    return out
```

```python
from contextlib import ExitStack

import concourse.bass as bass
from concourse import mybir

ALU = mybir.AluOpType
ACT = mybir.ActivationFunctionType
F32 = mybir.dt.float32
F32R = mybir.dt.float32r
BF16 = mybir.dt.bfloat16
AX_X = mybir.AxisListType.X

P = 128
EPS = 1e-6
LN_EPS = 1e-5
QMAX = 127.0
ROUND = 1.5 * 2.0 ** 23
BIG = 3.0e38


def build(nc, x, fside, ctxw, g_xattn, g_ffn, wealth, conf_W, conf_b,
          base_gate, base_up, base_down, gate_A, gate_B, up_A, up_B, down_A, down_B, out):
    NB, S, H = x.shape
    I2 = ctxw.shape[2]
    E, _, R = gate_A.shape
    I = base_gate.shape[1]
    ER = E * R
    SCALING = 16.0 / 64.0
    TB = S // P
    NT = NB * TB
    HC, EC, IC = H // P, ER // P, I // P
    IH = I // 2
    assert TB == 2 and HC == 2 and I2 == P and ER == 512 and IH <= 512 and fside.shape[1] == S

    stack = ExitStack()
    with stack:
        def sem(name):
            return stack.enter_context(nc.semaphore(name))

        def sb(name, shape, dt=F32, scope=stack):
            return scope.enter_context(nc.sbuf_tensor(name, shape, dt))

        def ps(name, shape, dt=F32, scope=stack):
            return scope.enter_context(nc.psum_tensor(name, shape, dt))

        xs_all = sb("x_resid", [P, NT, H])
        x2T = sb("x2T", [P, HC, NT, P])
        ident = sb("ident", [P, P])
        identb = sb("identb", [P, P], BF16)
        Wbase_hi = sb("Wbase_hi", [P, 2, HC, I], F32R)
        Wbase_lo = sb("Wbase_lo", [P, 2, HC, I], F32R)
        WB_hi = sb("WB_hi", [P, 2, EC, I], F32R)
        WB_lo = sb("WB_lo", [P, 2, EC, I], F32R)
        WdA_hi = sb("WdA_hi", [P, IC, ER], F32R)
        WdA_lo = sb("WdA_lo", [P, IC, ER], F32R)
        WA = sb("WA", [P, 2, HC, ER])
        Wbd = sb("Wbd", [P, IC, H])
        WdB = sb("WdB", [P, EC, H])
        picks = sb("picks", [P, NT, 2, E])
        pcur = sb("pcur", [P, 2, E])
        share = sb("share", [P, 2, NT])
        gates = sb("gates", [P, 2])
        raw = sb("raw", [P, 2, I])

        part1 = ExitStack()
        with part1:
            def s1(name, shape, dt=F32):
                return sb(name, shape, dt, part1)
            q1 = s1("q1", [P, NB, 4, H])
            q1i = s1("q1i", [P, 2, 4, H], BF16)
            q1T = s1("q1T", [P, 2, 2, HC, S], BF16)
            ones = s1("ones", [P, P])
            q2 = s1("q2", [P, NB, 4, I2])
            q2i = s1("q2i", [P, 2, 4, I2], BF16)
            q2T = s1("q2T", [P, 2, 2, S], BF16)
            bst = s1("bst", [P, NT, 6])
            mv = s1("mv", [P, NT, 2])
            rstd = s1("rstd", [P, NT])
            amx = s1("amx", [P, 2, NB, HC])
            s_rs = s1("s_rs", [P, 2, NB, HC])
            tmp8 = s1("tmp8", [P, NB, HC])
            diag = s1("diag", [P, 4, P])
            am1 = s1("am1", [P, NB, 4])
            inv1 = s1("inv1", [P, NB, 4])
            sc1 = s1("sc1", [P, NB, 4])
            wrow = s1("wrow", [P, 2, S])
            hq = s1("hq", [P, 2, TB, S])
            amx2 = s1("amx2", [P, 2, NB])
            s_rs2 = s1("s_rs2", [P, 2, NB])
            tmp4 = s1("tmp4", [P, NB])
            am2 = s1("am2", [P, NB, 4])
            inv2 = s1("inv2", [P, NB, 4])
            sc2 = s1("sc2", [P, NB, 4])
            sc2g = s1("sc2g", [P, NB, TB])
            bst2 = s1("bst2", [P, NT, 6])
            mv2 = s1("mv2", [P, NT, 2])
            rstd2 = s1("rstd2", [P, NT])
            cW = s1("cW", [E, H])
            cWT = s1("cWT", [P, HC, E])
            rows = s1("rows", [P, 2, E])
            gin = s1("gin", [P, 2])
            bids = s1("bids", [P, NT, E])
            eq = s1("eq", [P, NT, E])
            best = s1("best", [P, 2, NT])
            key = s1("key", [P, NT])
            down = s1("down", [P, E])
            dif = s1("dif", [P, NT])
        part2 = ExitStack()
        with part2:
            def s2(name, shape, dt=F32):
                return sb(name, shape, dt, part2)
            x2c = s2("x2c", [P, HC, P])
            x2h = s2("x2h", [P, HC, P], F32R)
            x2l = s2("x2l", [P, HC, P], F32R)
            base = s2("base", [P, 2, I])
            xA = s2("xA", [P, 2, ER])
            xm = s2("xm", [P, 2, ER])
            xmT_hi = s2("xmT_hi", [P, 2, EC, P], F32R)
            xmT_lo = s2("xmT_lo", [P, 2, EC, P], F32R)
            hbuf = s2("hbuf", [P, 2, I])
            ubuf = s2("ubuf", [P, I])
            hT_hi = s2("hT_hi", [P, IC, P], F32R)
            hT_lo = s2("hT_lo", [P, IC, P], F32R)
            hsumT = s2("hsumT", [P, IC, P])
            zs = s2("zs", [P, ER])
            zT = s2("zT", [P, EC, P])

        psum = ExitStack()
        with psum:
            A = [ps(f"bank{i}", [P, 512], F32, psum) for i in range(8)]
        psum = ExitStack()
        with psum:
            Ab = [ps(f"bankb{i}", [P, 1024], BF16, psum) for i in range(8)]
        psum = ExitStack()
        with psum:
            pG = ps("pG", [P, 2, 512], F32, psum)
            pU = ps("pU", [P, 2, 512], F32, psum)
            pZ = ps("pZ", [P, 2, 512], F32, psum)
            pT = ps("pT", [P, 2, 512], F32, psum)

        d_c, d_small = sem("d_c"), sem("d_small")
        d_x, d_w = [sem(f"d_x{b}") for b in range(NB)], [sem(f"d_w{b}") for b in range(NB)]
        d_WA, d_Wbd, d_WdB = sem("d_WA"), sem("d_Wbd"), sem("d_WdB")
        d_raw = [sem(f"d_raw{i}") for i in range(2)]
        s_ident, s_identb, s_ones, s_down = sem("s_ident"), sem("s_identb"), sem("s_ones"), sem("s_down")
        s_ident0 = sem("s_ident0")
        s_whi, s_wlo = sem("s_whi"), sem("s_wlo")
        s_stat, s_var, s_std, s_rstd, s_xn = sem("s_stat"), sem("s_var"), sem("s_std"), sem("s_rstd"), sem("s_xn")
        s_wT, s_xT1, s_cT, s_aT = sem("s_wT"), sem("s_xT1"), sem("s_cT"), sem("s_aT")
        s_wamax, s_xamax, s_camax, s_aamax = sem("s_wamax"), sem("s_xamax"), sem("s_camax"), sem("s_aamax")
        s_ratio, s_sq, s_srs = sem("s_ratio"), sem("s_sq"), sem("s_srs")
        s_diag, s_bc, s_smooth, s_am1, s_inv1 = sem("s_diag"), sem("s_bc"), sem("s_smooth"), sem("s_am1"), sem("s_inv1")
        s_scaled, s_clip, s_q1i, s_q1Tp, s_q1T = sem("s_scaled"), sem("s_clip"), sem("s_q1i"), sem("s_q1Tp"), sem("s_q1T")
        s_diagw, s_wbc, s_wrow, s_mm1, s_deq1 = sem("s_diagw"), sem("s_wbc"), sem("s_wrow"), sem("s_mm1"), sem("s_deq1")
        s_sg, s_a = sem("s_sg"), sem("s_a")
        s_ratio2, s_sq2, s_srs2 = sem("s_ratio2"), sem("s_sq2"), sem("s_srs2")
        s_diag2, s_bc2, s_smooth2, s_am2, s_inv2 = sem("s_diag2"), sem("s_bc2"), sem("s_smooth2"), sem("s_am2"), sem("s_inv2")
        s_scaled2, s_clip2, s_q2i, s_q2Tp, s_q2T = sem("s_scaled2"), sem("s_clip2"), sem("s_q2i"), sem("s_q2Tp"), sem("s_q2T")
        s_diagc, s_cbc, s_crow, s_mm2, s_deq2, s_x1 = sem("s_diagc"), sem("s_cbc"), sem("s_crow"), sem("s_mm2"), sem("s_deq2"), sem("s_x1")
        s_gate = sem("s_gate")
        s_stat2, s_var2, s_std2, s_rstd2, s_x2 = sem("s_stat2"), sem("s_var2"), sem("s_std2"), sem("s_rstd2"), sem("s_x2")
        s_x2Tp, s_x2T, s_cWTp, s_cWT, s_conf = sem("s_x2Tp"), sem("s_x2T"), sem("s_cWTp"), sem("s_cWT"), sem("s_conf")
        s_logit, s_sig, s_bids, s_route, s_dif, s_share = sem("s_logit"), sem("s_sig"), sem("s_bids"), sem("s_route"), sem("s_dif"), sem("s_share")
        s_zero = sem("s_zero")
        s_x2hi, s_x2lo = sem("s_x2hi"), sem("s_x2lo")
        s_xA, s_xAc, s_xm = sem("s_xA"), sem("s_xAc"), sem("s_xm")
        s_bg, s_bu, s_bgc, s_buc = sem("s_bg"), sem("s_bu"), sem("s_bgc"), sem("s_buc")
        s_xT, s_xhi, s_xlo = sem("s_xT"), sem("s_xhi"), sem("s_xlo")
        s_Bg, s_Bu, s_gadd, s_silu, s_uadd, s_h = sem("s_Bg"), sem("s_Bu"), sem("s_gadd"), sem("s_silu"), sem("s_uadd"), sem("s_h")
        s_hT, s_hhi, s_hlo, s_hs0, s_hs1 = sem("s_hT"), sem("s_hhi"), sem("s_hlo"), sem("s_hs0"), sem("s_hs1")
        s_z, s_zm, s_zs, s_zT, s_zTc = sem("s_z"), sem("s_zm"), sem("s_zs"), sem("s_zT"), sem("s_zTc")
        s_y, s_yo, s_out, s_pcur = sem("s_y"), sem("s_yo"), sem("s_out"), sem("s_pcur")

        chunks = []
        for gu, w in enumerate((base_gate, base_up)):
            for c in range(HC):
                chunks.append((w[c * P:(c + 1) * P, :], Wbase_hi[:, gu, c, :], Wbase_lo[:, gu, c, :], I))
        for gu, w in enumerate((gate_B, up_B)):
            wf = w.rearrange("e r i -> (e r) i")
            for c in range(EC):
                chunks.append((wf[c * P:(c + 1) * P, :], WB_hi[:, gu, c, :], WB_lo[:, gu, c, :], I))
        for c in range(IC):
            chunks.append((down_A[:, c * P:(c + 1) * P, :].rearrange("e i r -> i e r"),
                           WdA_hi[:, c, :], WdA_lo[:, c, :], ER))
        NCH = len(chunks)
        CH_BASE, CH_B = 2 * HC, 2 * HC + 2 * EC

        block = stack.enter_context(nc.Block())

        @block.sync
        def _(sp):
            xv = x.rearrange("b (j p) h -> p (b j) h", p=P)
            for b in range(NB):
                sp.dma_start(xs_all[:, 2 * b:2 * b + 2, :], xv[:, 2 * b:2 * b + 2, :]).then_inc(d_x[b], 16)
            for gu, w in enumerate((gate_A, up_A)):
                for c in range(HC):
                    sp.dma_start(WA[:, gu, c, :].rearrange("p (e r) -> p e r", e=E),
                                 w[:, c * P:(c + 1) * P, :].rearrange("e h r -> h e r")).then_inc(d_WA, 16)
            for n, (src, _, _, width) in enumerate(chunks):
                if n >= 2:
                    sp.wait_ge(s_wlo, n - 1)
                dst = raw[:, n % 2, 0:width]
                if width == ER:
                    dst = dst.rearrange("p (e r) -> p e r", e=E)
                sp.dma_start(dst, src).then_inc(d_raw[n % 2], 16)
            sp.dma_start(Wbd[:, :, :], base_down.rearrange("(c p) h -> p c h", p=P)).then_inc(d_Wbd, 16)
            sp.dma_start(WdB[:, :, :], down_B.rearrange("e r h -> (e r) h").rearrange("(c p) h -> p c h", p=P)).then_inc(d_WdB, 16)
            ov = out.rearrange("b (j p) h -> (b j) p h", p=P)
            with sp.Fori(0, NT) as t:
                sp.wait_ge(s_yo, t + 1)
                sp.dma_start(ov[bass.ds(t, 1), :, :].rearrange("a p h -> p a h"),
                             xs_all[:, bass.ds(t, 1), :]).then_inc(s_out, 16)
            sp.wait_ge(s_out, 16 * NT)

        @block.gpsimd
        def _(pool):
            g = nc.gpsimd
            g.memset(ident[:, :], 0.0).then_inc(s_zero, 1)
            g.memset(ones[:, :], 1.0).then_inc(s_ones, 1)
            pool.wait_ge(s_zero, 1)
            g.affine_select(out=ident[:, :], in_=ident[:, :], compare_op=ALU.not_equal, fill=1.0, base=0,
                            pattern=[[-1, P]], channel_multiplier=1).then_inc(s_ident, 1)
            pool.wait_ge(s_ident, 1)
            g.tensor_copy(identb[:, :], ident[:, :]).then_inc(s_identb, 1)
            for e in range(E):
                g.memset(down[:, e:e + 1], float(E - e)).then_inc(s_down, 1)
            for n, (_, hi, lo, width) in enumerate(chunks):
                pool.wait_ge(s_whi, n + 1)
                g.tensor_tensor(lo, raw[:, n % 2, 0:width], hi, ALU.subtract).then_inc(s_wlo, 1)

            pool.wait_ge(s_share, 2)
            pool.wait_ge(s_route, 1)

            def mask(t, k, gu, first=False):
                pool.wait_ge(s_xAc, 2 * t + gu + 1)
                pool.wait_ge(s_pcur, t + 1)
                if not (first and k == 0):
                    pool.wait_ge(s_xT, 4 * t + 2 * k + gu - 1)
                g.tensor_tensor(xm[:, gu, :].rearrange("p (e r) -> p e r", e=E),
                                xA[:, gu, :].rearrange("p (e r) -> p e r", e=E),
                                pcur[:, k, :].unsqueeze(2).to_broadcast([P, E, R]),
                                ALU.mult).then_inc(s_xm, 1)

            def x2_lo(t):
                pool.wait_ge(s_x2hi, 2 * t + 2)
                g.tensor_tensor(x2l[:, :, :], x2c[:, :, :], x2h[:, :, :], ALU.subtract).then_inc(s_x2lo, 1)

            def hsum_first(t, first=False):
                pool.wait_ge(s_hlo, 2 * t + 1)
                if not first:
                    pool.wait_ge(s_y, t)
                g.tensor_tensor(hsumT[:, :, :], hT_hi[:, :, :], hT_lo[:, :, :], ALU.add).then_inc(s_hs0, 1)

            def tile(t, first=False, last=False):
                mask(t, 0, 1, first)
                mask(t, 1, 0)
                mask(t, 1, 1)
                hsum_first(t, first)
                if not last:
                    x2_lo(t + 1)
                    mask(t + 1, 0, 0)

            x2_lo(0)
            mask(0, 0, 0, True)
            tile(0, first=True)
            with pool.Fori(1, NT - 1) as t:
                tile(t)
            tile(NT - 1, last=True)

        @block.scalar
        def _(act):
            a = nc.scalar
            wv = fside.rearrange("b (j p) h -> p b j h", p=P)
            cv = ctxw.rearrange("b (j p) h -> p b j h", p=P)
            for b in range(NB):
                a.dma_start(q1[:, b, 2:4, :], wv[:, b]).then_inc(d_w[b], 16)
            for b in range(NB):
                a.dma_start(q2[:, b, 2:4, :], cv[:, b]).then_inc(d_c, 16)
            a.dma_start(cW[:, :], conf_W).then_inc(d_small, 16)
            a.dma_start(rows[:, 0, :], conf_b.rearrange("(a e) -> a e", a=1).to_broadcast([P, E])).then_inc(d_small, 16)
            a.dma_start(rows[:, 1, :], wealth.rearrange("(a e) -> a e", a=1).to_broadcast([P, E])).then_inc(d_small, 16)
            a.dma_start(gin[:, 0:1], g_xattn.rearrange("(a e) -> a e", a=1).to_broadcast([P, 1])).then_inc(d_small, 16)
            a.dma_start(gin[:, 1:2], g_ffn.rearrange("(a e) -> a e", a=1).to_broadcast([P, 1])).then_inc(d_small, 16)

            split = [0]

            def split_hi(count):
                for _ in range(count):
                    n = split[0]
                    act.wait_ge(d_raw[n % 2], 16 * (n // 2 + 1))
                    a.copy(chunks[n][1], raw[:, n % 2, 0:chunks[n][3]]).then_inc(s_whi, 1)
                    split[0] += 1

            act.wait_ge(d_small, 80)
            a.activation(gates[:, :], gin[:, :], ACT.Tanh).then_inc(s_gate, 1)
            act.wait_ge(s_var, 1)
            a.activation(rstd[:, :], mv[:, :, 1], ACT.Sqrt).then_inc(s_std, 1)
            split_hi(2)
            act.wait_ge(s_ratio, 1)
            a.activation(s_rs[:, 1], tmp8[:, :, :], ACT.Sqrt).then_inc(s_sq, 1)
            split_hi(2)
            for b in range(NB):
                for i in range(4):
                    act.wait_ge(s_inv1, b + 1)
                    a.activation(q1[:, b, i, :], q1[:, b, i, :], ACT.Copy, scale=inv1[:, b, i:i + 1]).then_inc(s_scaled, 1)
                if b >= 1:
                    act.wait_ge(s_q1Tp, b)
                    if b >= 3:
                        act.wait_ge(s_mm1, b - 2)
                    a.copy(q1T[:, (b - 1) % 2].rearrange("p a c s -> p (a c s)"), Ab[(b - 1) % 2][:, :]).then_inc(s_q1T, 1)
                    act.wait_ge(s_wbc, b)
                    if b >= 3:
                        act.wait_ge(s_deq1, b - 2)
                    a.copy(wrow[:, (b - 1) % 2, :], A[2 + (b - 1) % 2][:, 0:S]).then_inc(s_wrow, 1)
            for b in (NB - 1,):
                act.wait_ge(s_q1Tp, b + 1)
                act.wait_ge(s_mm1, b - 1)
                a.copy(q1T[:, b % 2].rearrange("p a c s -> p (a c s)"), Ab[b % 2][:, :]).then_inc(s_q1T, 1)
                act.wait_ge(s_wbc, b + 1)
                act.wait_ge(s_deq1, b - 1)
                a.copy(wrow[:, b % 2, :], A[2 + b % 2][:, 0:S]).then_inc(s_wrow, 1)
            for b in range(NB):
                act.wait_ge(s_deq1, b + 1)
                a.activation(hq[:, b % 2, :, 0:I2], hq[:, b % 2, :, 0:I2], ACT.Silu).then_inc(s_sg, 1)
            split_hi(1)
            act.wait_ge(s_ratio2, 1)
            a.activation(s_rs2[:, 1], tmp4[:, :], ACT.Sqrt).then_inc(s_sq2, 1)
            split_hi(1)
            for b in range(NB):
                for i in range(4):
                    act.wait_ge(s_inv2, b + 1)
                    a.activation(q2[:, b, i, :], q2[:, b, i, :], ACT.Copy, scale=inv2[:, b, i:i + 1]).then_inc(s_scaled2, 1)
            for b in range(NB):
                act.wait_ge(s_q2Tp, b + 1)
                if b >= 2:
                    act.wait_ge(s_mm2, b - 1)
                a.copy(q2T[:, b % 2].rearrange("p a s -> p (a s)"), Ab[b % 2][:, 0:2 * S]).then_inc(s_q2T, 1)
                act.wait_ge(s_cbc, b + 1)
                if b >= 2:
                    act.wait_ge(s_deq2, b - 1)
                a.copy(wrow[:, b % 2, :], A[2 + b % 2][:, 0:S]).then_inc(s_crow, 1)
            act.wait_ge(s_var2, 1)
            a.activation(rstd2[:, :], mv2[:, :, 1], ACT.Sqrt).then_inc(s_std2, 1)
            for b in range(NB):
                act.wait_ge(s_x2Tp, b + 1)
                a.copy(x2T[:, :, 2 * b:2 * b + 2, :], A[b][:, :].rearrange("p (c j q) -> p c j q", c=HC, j=TB)).then_inc(s_x2T, 1)
            act.wait_ge(s_logit, 1)
            a.activation(bids[:, :, :], bids[:, :, :], ACT.Sigmoid).then_inc(s_sig, 1)
            act.wait_ge(s_dif, 1)
            a.activation(share[:, 0, :], dif[:, :], ACT.Sigmoid).then_inc(s_share, 1)
            a.activation(share[:, 1, :], dif[:, :], ACT.Sigmoid, scale=-1.0).then_inc(s_share, 1)

            act.wait_ge(s_route, 1)

            def x2_hi(t, first=False):
                src = x2T[:, :, t, :] if first else x2T[:, :, bass.ds(t, 1), :].rearrange("p c a q -> p c (a q)")
                if not first:
                    act.wait_ge(s_bu, t)
                a.copy(x2c[:, :, :], src).then_inc(s_x2hi, 1)
                if not first:
                    act.wait_ge(s_xm, 4 * t)
                a.copy(pcur[:, :, :], picks[:, t, :, :] if isinstance(t, int) else
                       picks[:, bass.ds(t, 1), :, :].rearrange("p a k e -> p (a k) e")).then_inc(s_pcur, 1)
                act.wait_ge(s_x2hi, 2 * t + 1)
                a.copy(x2h[:, :, :], x2c[:, :, :]).then_inc(s_x2hi, 1)

            def copy_xA(t, first=False):
                act.wait_ge(s_xA, t + 1)
                for gu in range(2):
                    if not first:
                        act.wait_ge(s_xm, 4 * t - 1 + gu)
                    a.copy(xA[:, gu, :], pT[:, gu, :]).then_inc(s_xAc, 1)

            def copy_base(t, gu, first=False):
                act.wait_ge((s_bg, s_bu)[gu], t + 1)
                if not first:
                    act.wait_ge((s_gadd, s_uadd)[gu], 2 * t)
                a.copy(base[:, gu, :].rearrange("p (a i) -> p a i", a=2), (pG, pU)[gu][:, :, 0:IH]).then_inc((s_bgc, s_buc)[gu], 1)

            def x_hi(t, k, gu, first=False):
                act.wait_ge(s_xT, 4 * t + 2 * k + gu + 1)
                if not (first and k == 0):
                    act.wait_ge((s_Bg, s_Bu)[gu], 2 * t + k)
                a.copy(xmT_hi[:, gu].rearrange("p c q -> p (c q)"), pT[:, gu, :]).then_inc(s_xhi, 1)

            def silu(t, k):
                act.wait_ge(s_gadd, 2 * t + k + 1)
                a.activation(hbuf[:, k, :], hbuf[:, k, :], ACT.Silu).then_inc(s_silu, 1)

            def h_hi(t, k, first=False):
                act.wait_ge(s_hT, 2 * t + k + 1)
                if k == 1:
                    act.wait_ge(s_hs0, t + 1)
                if not (first and k == 0):
                    act.wait_ge(s_z, 2 * t + k)
                a.copy(hT_hi[:, :, :].rearrange("p c q -> p (c q)"),
                       pT[:, :, :].rearrange("p a q -> p (a q)")[:, 0:I]).then_inc(s_hhi, 1)

            def copy_zT(t, first=False):
                act.wait_ge(s_zT, t + 1)
                if not first:
                    act.wait_ge(s_y, t)
                a.copy(zT[:, :, :].rearrange("p c q -> p (c q)"), pZ[:, 0, :]).then_inc(s_zTc, 1)

            def tile(t, first=False, last=False, second=False):
                x_hi(t, 0, 1, first)
                silu(t, 0)
                x_hi(t, 1, 0)
                if not first:
                    h_hi(t - 1, 1)
                silu(t, 1)
                x_hi(t, 1, 1)
                if not first:
                    copy_zT(t - 1, second)
                h_hi(t, 0, first)
                if not last:
                    x2_hi(t + 1)
                    copy_xA(t + 1)
                    copy_base(t + 1, 0)
                    x_hi(t + 1, 0, 0)
                    copy_base(t + 1, 1)

            x2_hi(0, True)
            copy_xA(0, True)
            split_hi(NCH - split[0])
            copy_base(0, 0, True)
            x_hi(0, 0, 0, True)
            copy_base(0, 1, True)
            tile(0, first=True)
            tile(1, second=True)
            with act.Fori(2, NT - 1) as t:
                tile(t)
            tile(NT - 1, last=True)
            h_hi(NT - 1, 1)
            copy_zT(NT - 1)

        @block.vector
        def _(dve):
            v = nc.vector

            chains = [0]
            s_chain = sem("s_chain")

            def link(ins):
                ins.then_inc(s_chain, 1)
                chains[0] += 1
                dve.wait_ge(s_chain, chains[0])

            for t in range(NT):
                dve.wait_ge(d_x[t // TB], 16)
                v.bn_stats(bst[:, t, :], xs_all[:, t, :]).then_inc(s_stat, 1)
            for t in range(NT):
                dve.wait_ge(s_stat, t + 1)
                ins = v.bn_aggr(mv[:, t, :], bst[:, t, :])
            link(ins)
            v.tensor_scalar(mv[:, :, 1], mv[:, :, 1], LN_EPS, None, ALU.add).then_inc(s_var, 1)
            for b in range(NB):
                dve.wait_ge(s_wT, b + 1)
                v.tensor_reduce(amx[:, 1, b, :], A[4 + b][:, :].rearrange("p (c s) -> p c s", c=HC), AX_X, ALU.max,
                                apply_absolute_value=True).then_inc(s_wamax, 1)
            dve.wait_ge(s_std, 1)
            v.reciprocal(rstd[:, :], rstd[:, :]).then_inc(s_rstd, 1)
            dve.wait_ge(s_rstd, 1)
            for t in range(NT):
                v.tensor_scalar(q1[:, t // TB, t % TB, :], xs_all[:, t, :], mv[:, t, 0:1], rstd[:, t:t + 1],
                                ALU.subtract, ALU.mult).then_inc(s_xn, 1)
            for b in range(NB):
                dve.wait_ge(s_xT1, b + 1)
                v.tensor_reduce(amx[:, 0, b, :], A[b][:, :].rearrange("p (c s) -> p c s", c=HC), AX_X, ALU.max,
                                apply_absolute_value=True).then_inc(s_xamax, 1)
            dve.wait_ge(s_xamax, NB)
            dve.wait_ge(s_wamax, NB)
            v.tensor_scalar(amx[:, :, :, :], amx[:, :, :, :], EPS, None, ALU.max).then_inc(s_srs, 1)
            dve.wait_ge(s_srs, 1)
            v.reciprocal(tmp8[:, :, :], amx[:, 1]).then_inc(s_srs, 1)
            dve.wait_ge(s_srs, 2)
            v.tensor_tensor(tmp8[:, :, :], amx[:, 0], tmp8[:, :, :], ALU.mult).then_inc(s_ratio, 1)
            dve.wait_ge(s_sq, 1)
            v.tensor_scalar(s_rs[:, 1], s_rs[:, 1], EPS, None, ALU.max).then_inc(s_srs, 1)
            dve.wait_ge(s_srs, 3)
            v.reciprocal(s_rs[:, 0], s_rs[:, 1]).then_inc(s_srs, 1)
            dve.wait_ge(s_srs, 4)

            def smooth(b):
                dve.wait_ge(s_bc, b + 1)
                for w in range(2):
                    dve.wait_ge(s_xn, NT) if w == 0 else dve.wait_ge(d_w[b], 16)
                    qv = q1[:, b, 2 * w:2 * w + 2, :]
                    v.tensor_tensor(qv, qv, A[b][:, w * H:(w + 1) * H].unsqueeze(1).to_broadcast([P, 2, H]),
                                    ALU.mult).then_inc(s_smooth, 1)
                dve.wait_ge(s_smooth, 2 * b + 2)
                v.tensor_reduce(am1[:, b, :], q1[:, b], AX_X, ALU.max, apply_absolute_value=True).then_inc(s_am1, 1)
                dve.wait_ge(s_am1, b + 1)
                scales(am1[:, b, :], inv1[:, b, :], sc1[:, b, :], s_inv1, b)

            def scales(am, inv, sc, s_inv, b):
                link(v.tensor_scalar(am, am, EPS, None, ALU.max))
                v.tensor_scalar(sc, am, 1.0 / QMAX, None, ALU.mult)
                link(v.reciprocal(inv, am))
                v.tensor_scalar(inv, inv, QMAX, None, ALU.mult).then_inc(s_inv, 1)

            for b in range(NB):
                if b >= 1:
                    dve.wait_ge(s_bc, b)
                v.tensor_tensor(diag[:, :, :].rearrange("p (w c) q -> p w c q", w=2),
                                ident[:, :].unsqueeze(1).unsqueeze(1).to_broadcast([P, 2, HC, P]),
                                s_rs[:, :, b, :].unsqueeze(3).to_broadcast([P, 2, HC, P]), ALU.mult).then_inc(s_diag, 1)
                if b >= 1:
                    smooth(b - 1)
            smooth(NB - 1)
            for b in range(NB):
                dve.wait_ge(s_scaled, 4 * b + 4)
                qf = q1[:, b].rearrange("p i h -> p (i h)")
                link(v.tensor_scalar(qf, qf, ROUND, ROUND, ALU.add, ALU.subtract))
                if b >= 2:
                    dve.wait_ge(s_q1Tp, b - 1)
                v.tensor_scalar(q1i[:, b % 2].rearrange("p i h -> p (i h)"), qf, QMAX, -QMAX, ALU.min, ALU.max).then_inc(s_q1i, 1)
                if b >= 1:
                    dve.wait_ge(s_wbc, b)
                v.tensor_tensor(diag[:, 0:2, :], ident[:, :].unsqueeze(1).to_broadcast([P, 2, P]),
                                sc1[:, b, 2:4].unsqueeze(2).to_broadcast([P, 2, P]), ALU.mult).then_inc(s_diagw, 1)
            def deq1(b):
                dve.wait_ge(s_mm1, b + 1)
                dve.wait_ge(s_wrow, b + 1)
                if b >= 2:
                    dve.wait_ge(s_a, b - 1)
                for j in range(TB):
                    ins = v.scalar_tensor_tensor(out=hq[:, b % 2, j, :], in0=A[4 + b % 2][:, j * S:(j + 1) * S],
                                                 scalar=sc1[:, b, j:j + 1], in1=wrow[:, b % 2, :], op0=ALU.mult, op1=ALU.mult)
                ins.then_inc(s_deq1, 1)

            def a_mul(b):
                dve.wait_ge(s_sg, b + 1)
                v.tensor_tensor(q2[:, b, 0:2, :], hq[:, b % 2, :, 0:I2], hq[:, b % 2, :, I2:2 * I2], ALU.mult).then_inc(s_a, 1)

            for b in range(NB):
                deq1(b)
                if b >= 1:
                    a_mul(b - 1)
            a_mul(NB - 1)
            for b in range(NB):
                dve.wait_ge(s_cT, b // 2 + 1)
                v.tensor_reduce(amx2[:, 1, b:b + 1], A[6 + b // 2][:, (b % 2) * S:(b % 2 + 1) * S], AX_X, ALU.max,
                                apply_absolute_value=True)
            for b in range(NB):
                dve.wait_ge(s_aT, b + 1)
                ins = v.tensor_reduce(amx2[:, 0, b:b + 1], A[b][:, 0:S], AX_X, ALU.max, apply_absolute_value=True)
            link(ins)
            link(v.tensor_scalar(amx2[:, :, :], amx2[:, :, :], EPS, None, ALU.max))
            link(v.reciprocal(tmp4[:, :], amx2[:, 1]))
            v.tensor_tensor(tmp4[:, :], amx2[:, 0], tmp4[:, :], ALU.mult).then_inc(s_ratio2, 1)
            dve.wait_ge(s_sq2, 1)
            link(v.tensor_scalar(s_rs2[:, 1], s_rs2[:, 1], EPS, None, ALU.max))
            link(v.reciprocal(s_rs2[:, 0], s_rs2[:, 1]))

            def smooth2(b):
                dve.wait_ge(s_bc2, b + 1)
                dve.wait_ge(d_c, 16 * NB)
                link(v.tensor_tensor(q2[:, b].rearrange("p (w j) q -> p w j q", w=2), q2[:, b].rearrange("p (w j) q -> p w j q", w=2),
                                     A[b][:, 0:2 * I2].rearrange("p (w q) -> p w q", w=2).unsqueeze(2).to_broadcast([P, 2, 2, I2]),
                                     ALU.mult))
                link(v.tensor_reduce(am2[:, b, :], q2[:, b], AX_X, ALU.max, apply_absolute_value=True))
                scales(am2[:, b, :], inv2[:, b, :], sc2[:, b, :], s_inv2, b)

            dve.wait_ge(s_a, NB)
            for b in range(NB):
                if b >= 1:
                    dve.wait_ge(s_bc2, b)
                v.tensor_tensor(diag[:, 0:2, :], ident[:, :].unsqueeze(1).to_broadcast([P, 2, P]),
                                s_rs2[:, :, b].unsqueeze(2).to_broadcast([P, 2, P]), ALU.mult).then_inc(s_diag2, 1)
                if b >= 1:
                    smooth2(b - 1)
            smooth2(NB - 1)
            dve.wait_ge(s_gate, 1)
            dve.wait_ge(s_inv2, NB)
            link(v.tensor_scalar(sc2g[:, :, :], sc2[:, :, 0:2], gates[:, 0:1], None, ALU.mult))
            for b in range(NB):
                dve.wait_ge(s_scaled2, 4 * b + 4)
                qf = q2[:, b].rearrange("p i h -> p (i h)")
                link(v.tensor_scalar(qf, qf, ROUND, ROUND, ALU.add, ALU.subtract))
                if b >= 2:
                    dve.wait_ge(s_q2Tp, b - 1)
                v.tensor_scalar(q2i[:, b % 2].rearrange("p i h -> p (i h)"), qf, QMAX, -QMAX, ALU.min, ALU.max).then_inc(s_q2i, 1)
                if b >= 1:
                    dve.wait_ge(s_cbc, b)
                v.tensor_tensor(diag[:, 0:2, :], ident[:, :].unsqueeze(1).to_broadcast([P, 2, P]),
                                sc2[:, b, 2:4].unsqueeze(2).to_broadcast([P, 2, P]), ALU.mult).then_inc(s_diagc, 1)
            for b in range(NB):
                dve.wait_ge(s_mm2, b + 1)
                dve.wait_ge(s_crow, b + 1)
                for j in range(TB):
                    ins = v.scalar_tensor_tensor(out=hq[:, b % 2, j, :], in0=A[4 + b % 2][:, j * H:(j + 1) * H],
                                                 scalar=sc2g[:, b, j:j + 1], in1=wrow[:, b % 2, :], op0=ALU.mult, op1=ALU.mult)
                ins.then_inc(s_deq2, 1)
                dve.wait_ge(s_deq2, b + 1)
                xv_ = xs_all[:, 2 * b:2 * b + 2, :]
                v.tensor_tensor(xv_, xv_, hq[:, b % 2], ALU.add).then_inc(s_x1, 1)
            for t in range(NT):
                dve.wait_ge(s_x1, t // TB + 1)
                v.bn_stats(bst2[:, t, :], xs_all[:, t, :]).then_inc(s_stat2, 1)
            for t in range(NT):
                dve.wait_ge(s_stat2, t + 1)
                ins = v.bn_aggr(mv2[:, t, :], bst2[:, t, :])
            link(ins)
            v.tensor_scalar(mv2[:, :, 1], mv2[:, :, 1], LN_EPS, None, ALU.add).then_inc(s_var2, 1)
            dve.wait_ge(s_std2, 1)
            link(v.reciprocal(rstd2[:, :], rstd2[:, :]))
            for t in range(NT):
                v.tensor_scalar(q1[:, t // TB, t % TB, :], xs_all[:, t, :], mv2[:, t, 0:1], rstd2[:, t:t + 1],
                                ALU.subtract, ALU.mult).then_inc(s_x2, 1)
            dve.wait_ge(s_cWTp, 1)
            v.tensor_copy(cWT[:, :, :], A[5][:, 0:HC * E].rearrange("p (c e) -> p c e", c=HC)).then_inc(s_cWT, 1)

            def row(r):
                return rows[:, r, :].unsqueeze(1).to_broadcast([P, NT, E])

            def per_tile(ap):
                return ap.unsqueeze(2).to_broadcast([P, NT, E])
            dve.wait_ge(s_conf, 1)
            dve.wait_ge(d_small, 80)
            v.tensor_tensor(bids[:, :, :], A[4][:, 0:NT * E].rearrange("p (t e) -> p t e", t=NT), row(0), ALU.add).then_inc(s_logit, 1)
            dve.wait_ge(s_sig, 1)
            dve.wait_ge(s_down, E)
            link(v.tensor_tensor(bids[:, :, :], bids[:, :, :], row(1), ALU.mult))
            for k in range(2):
                link(v.tensor_reduce(best[:, k, :], bids[:, :, :], AX_X, ALU.max))
                link(v.tensor_tensor(eq[:, :, :], bids[:, :, :], per_tile(best[:, k, :]), ALU.is_equal))
                link(v.tensor_tensor(eq[:, :, :], eq[:, :, :], down[:, :].unsqueeze(1).to_broadcast([P, NT, E]), ALU.mult))
                link(v.tensor_reduce(key[:, :], eq[:, :, :], AX_X, ALU.max))
                link(v.tensor_tensor(eq[:, :, :], down[:, :].unsqueeze(1).to_broadcast([P, NT, E]), per_tile(key[:, :]), ALU.is_equal))
                if k == 0:
                    link(v.scalar_tensor_tensor(out=bids[:, :, :], in0=eq[:, :, :], scalar=-BIG, in1=bids[:, :, :],
                                                op0=ALU.mult, op1=ALU.add))
                    link(v.tensor_scalar(picks[:, :, k, :], eq[:, :, :], SCALING, None, ALU.mult))
                else:
                    v.tensor_tensor(dif[:, :], best[:, 0, :], best[:, 1, :], ALU.subtract).then_inc(s_dif, 1)
                    v.tensor_scalar(picks[:, :, k, :], eq[:, :, :], SCALING, None, ALU.mult).then_inc(s_route, 1)

            dve.wait_ge(s_route, 1)
            dve.wait_ge(s_share, 2)

            def x_lo(t, k, gu):
                dve.wait_ge(s_xhi, 4 * t + 2 * k + gu + 1)
                v.tensor_tensor(xmT_lo[:, gu].rearrange("p c q -> p (c q)"), pT[:, gu, :],
                                xmT_hi[:, gu].rearrange("p c q -> p (c q)"), ALU.subtract).then_inc(s_xlo, 1)

            def gate_sum(t, k, first=False):
                dve.wait_ge(s_Bg, 2 * t + k + 1)
                dve.wait_ge(s_bgc, t + 1)
                if not first:
                    dve.wait_ge(s_hT, 2 * t + k - 1)
                v.tensor_tensor(hbuf[:, k, :].rearrange("p (a i) -> p a i", a=2), pG[:, :, 0:IH],
                                base[:, 0, :].rearrange("p (a i) -> p a i", a=2), ALU.add).then_inc(s_gadd, 1)

            def up_sum(t, k):
                dve.wait_ge(s_Bu, 2 * t + k + 1)
                dve.wait_ge(s_buc, t + 1)
                v.tensor_tensor(ubuf[:, :].rearrange("p (a i) -> p a i", a=2), pU[:, :, 0:IH],
                                base[:, 1, :].rearrange("p (a i) -> p a i", a=2), ALU.add).then_inc(s_uadd, 1)

            def h_mul(t, k):
                dve.wait_ge(s_silu, 2 * t + k + 1)
                dve.wait_ge(s_uadd, 2 * t + k + 1)
                sh = share[:, k, t:t + 1] if isinstance(t, int) else share[:, k, bass.ds(t, 1)]
                v.scalar_tensor_tensor(out=hbuf[:, k, :], in0=hbuf[:, k, :], scalar=sh, in1=ubuf[:, :],
                                       op0=ALU.mult, op1=ALU.mult).then_inc(s_h, 1)

            def h_lo(t, k):
                dve.wait_ge(s_hhi, 2 * t + k + 1)
                v.tensor_tensor(hT_lo[:, :, :].rearrange("p c q -> p (c q)"),
                                pT[:, :, :].rearrange("p a q -> p (a q)")[:, 0:I],
                                hT_hi[:, :, :].rearrange("p c q -> p (c q)"), ALU.subtract).then_inc(s_hlo, 1)

            def hsum_second(t):
                dve.wait_ge(s_hs0, t + 1)
                v.tensor_tensor(hsumT[:, :, :].rearrange("p c q -> p (c q)"),
                                pT[:, :, :].rearrange("p a q -> p (a q)")[:, 0:I],
                                hsumT[:, :, :].rearrange("p c q -> p (c q)"), ALU.add).then_inc(s_hs1, 1)

            def z_mask(t, k, first=False):
                dve.wait_ge(s_z, 2 * t + k + 1)
                if k == 0 and not first:
                    dve.wait_ge(s_zT, t)
                pk = picks[:, t, k, :] if isinstance(t, int) else picks[:, bass.ds(t, 1), k, :].rearrange("p a e -> p (a e)")
                v.tensor_tensor((zs[:, :], pZ[:, 1, :])[k].rearrange("p (e r) -> p e r", e=E), pZ[:, k, :].rearrange("p (e r) -> p e r", e=E),
                                pk.unsqueeze(2).to_broadcast([P, E, R]), ALU.mult).then_inc(s_zm, 1)
                if k == 1:
                    dve.wait_ge(s_zm, 2 * t + 2)
                    v.tensor_tensor(zs[:, :], pZ[:, 1, :], zs[:, :], ALU.add).then_inc(s_zs, 1)

            def output(t):
                dve.wait_ge(s_y, t + 1)
                xt = xs_all[:, t:t + 1, :] if isinstance(t, int) else xs_all[:, bass.ds(t, 1), :]
                v.scalar_tensor_tensor(out=xt.rearrange("p a h -> p (a h)"), in0=pZ[:, 1, 0:H], scalar=gates[:, 1:2],
                                       in1=xt.rearrange("p a h -> p (a h)"), op0=ALU.mult, op1=ALU.add).then_inc(s_yo, 1)

            def tile(t, first=False, last=False, second=False):
                x_lo(t, 0, 1)
                gate_sum(t, 0, first)
                x_lo(t, 1, 0)
                up_sum(t, 0)
                h_mul(t, 0)
                if not first:
                    h_lo(t - 1, 1)
                    hsum_second(t - 1)
                gate_sum(t, 1, first)
                x_lo(t, 1, 1)
                if not first:
                    z_mask(t - 1, 1, second)
                up_sum(t, 1)
                h_mul(t, 1)
                h_lo(t, 0)
                if not first:
                    output(t - 1)
                z_mask(t, 0, first)
                if not last:
                    x_lo(t + 1, 0, 0)

            x_lo(0, 0, 0)
            tile(0, first=True)
            tile(1, second=True)
            with dve.Fori(2, NT - 1) as t:
                tile(t)
            tile(NT - 1, last=True)
            h_lo(NT - 1, 1)
            hsum_second(NT - 1)
            z_mask(NT - 1, 1)
            output(NT - 1)

        @block.tensor
        def _(pe):
            m = nc.tensor
            pe.wait_ge(s_ident, 1)
            pe.wait_ge(s_identb, 1)
            pe.wait_ge(s_ones, 1)
            for b in range(NB):
                pe.wait_ge(d_w[b], 16)
                for c in range(HC):
                    for j in range(TB):
                        ins = m.transpose(A[4 + b][:, c * S + j * P:c * S + (j + 1) * P], q1[:, b, 2 + j, c * P:(c + 1) * P], ident[:, :])
                ins.then_inc(s_wT, 1)
            for b in range(NB):
                pe.wait_ge(s_xn, TB * (b + 1))
                for c in range(HC):
                    for j in range(TB):
                        ins = m.transpose(A[b][:, c * S + j * P:c * S + (j + 1) * P], q1[:, b, j, c * P:(c + 1) * P], ident[:, :])
                ins.then_inc(s_xT1, 1)
            for b in range(NB):
                pe.wait_ge(d_c, 16 * NB)
                pe.wait_ge(s_wamax, NB)
                for j in range(TB):
                    ins = m.transpose(A[6 + b // 2][:, (b % 2) * S + j * P:(b % 2) * S + (j + 1) * P], q2[:, b, 2 + j, :], ident[:, :])
                if b % 2:
                    ins.then_inc(s_cT, 1)
            pe.wait_ge(s_xamax, NB)
            for b in range(NB):
                pe.wait_ge(s_diag, b + 1)
                m.matmul(A[b][:, :], ones[:, :], diag[:, :, :].rearrange("p a q -> p (a q)"), start=True, stop=True).then_inc(s_bc, 1)
            pe.wait_ge(s_smooth, 2 * NB)

            def products1(b):
                pe.wait_ge(s_q1T, b + 1)
                if b >= 2:
                    pe.wait_ge(s_deq1, b - 1)
                for j in range(TB):
                    for c in range(HC):
                        ins = m.matmul(A[4 + b % 2][:, j * S:(j + 1) * S], q1T[:, b % 2, 0, c, j * P:(j + 1) * P],
                                       q1T[:, b % 2, 1, c, :], start=(c == 0), stop=(c == HC - 1))
                ins.then_inc(s_mm1, 1)

            for b in range(NB):
                pe.wait_ge(s_q1i, b + 1)
                if b >= 2:
                    pe.wait_ge(s_q1T, b - 1)
                for w in range(2):
                    for c in range(HC):
                        for j in range(TB):
                            o = ((w * HC + c) * TB + j) * P
                            ins = m.transpose(Ab[b % 2][:, o:o + P], q1i[:, b % 2, 2 * w + j, c * P:(c + 1) * P], identb[:, :])
                ins.then_inc(s_q1Tp, 1)
                pe.wait_ge(s_diagw, b + 1)
                if b >= 2:
                    pe.wait_ge(s_wrow, b - 1)
                m.matmul(A[2 + b % 2][:, 0:S], ones[:, :], diag[:, 0:2, :].rearrange("p a q -> p (a q)"), start=True, stop=True).then_inc(s_wbc, 1)
                if b >= 1:
                    products1(b - 1)
            products1(NB - 1)
            pe.wait_ge(s_wrow, NB)
            for b in range(NB):
                pe.wait_ge(s_a, b + 1)
                for j in range(TB):
                    ins = m.transpose(A[b][:, j * P:(j + 1) * P], q2[:, b, j, :], ident[:, :])
                ins.then_inc(s_aT, 1)
            for b in range(NB):
                pe.wait_ge(s_diag2, b + 1)
                m.matmul(A[b][:, 0:2 * I2], ones[:, :], diag[:, 0:2, :].rearrange("p a q -> p (a q)"), start=True, stop=True).then_inc(s_bc2, 1)
            pe.wait_ge(s_inv2, NB)

            def products2(b):
                pe.wait_ge(s_q2T, b + 1)
                if b >= 2:
                    pe.wait_ge(s_deq2, b - 1)
                for j in range(TB):
                    ins = m.matmul(A[4 + b % 2][:, j * H:(j + 1) * H], q2T[:, b % 2, 0, j * P:(j + 1) * P], q2T[:, b % 2, 1, :],
                                   start=True, stop=True)
                ins.then_inc(s_mm2, 1)

            for b in range(NB):
                pe.wait_ge(s_q2i, b + 1)
                if b >= 2:
                    pe.wait_ge(s_q2T, b - 1)
                for i in range(4):
                    ins = m.transpose(Ab[b % 2][:, i * P:(i + 1) * P], q2i[:, b % 2, i, :], identb[:, :])
                ins.then_inc(s_q2Tp, 1)
                pe.wait_ge(s_diagc, b + 1)
                if b >= 2:
                    pe.wait_ge(s_crow, b - 1)
                m.matmul(A[2 + b % 2][:, 0:S], ones[:, :], diag[:, 0:2, :].rearrange("p a q -> p (a q)"), start=True, stop=True).then_inc(s_cbc, 1)
                if b >= 1:
                    products2(b - 1)
            products2(NB - 1)
            pe.wait_ge(s_deq2, NB)
            pe.wait_ge(s_crow, NB)
            pe.wait_ge(d_small, 80)
            for c in range(HC):
                ins = m.transpose(A[5][:, c * E:(c + 1) * E], cW[:, c * P:(c + 1) * P], ident[0:E, 0:E])
            ins.then_inc(s_cWTp, 1)
            for b in range(NB):
                pe.wait_ge(s_x2, TB * (b + 1))
                for c in range(HC):
                    for j in range(TB):
                        ins = m.transpose(A[b][:, (c * TB + j) * P:(c * TB + j + 1) * P], q1[:, b, j, c * P:(c + 1) * P], ident[:, :])
                ins.then_inc(s_x2Tp, 1)
            pe.wait_ge(s_cWT, 1)
            for t in range(NT):
                pe.wait_ge(s_x2T, t // TB + 1)
                for c in range(HC):
                    ins = m.matmul(A[4][:, t * E:(t + 1) * E], x2T[:, c, t, :], cWT[:, c, :], start=(c == 0), stop=(c == HC - 1))
            ins.then_inc(s_conf, 1)

            pe.wait_ge(d_WA, 64)
            pe.wait_ge(s_logit, 1)

            def split_product(outs, hi, lo, whi, wlo, first, last):
                n = len(outs)
                for j in range(n):
                    m.matmul(outs[j], hi, whi[j], start=first, stop=False)
                for j in range(n):
                    m.matmul(outs[j], hi, wlo[j], start=False, stop=False)
                for j in range(n):
                    ins = m.matmul(outs[j], lo, whi[j], start=False, stop=last)
                return ins

            def project_A(t, first=False):
                pe.wait_ge(s_x2hi, 2 * t + 1)
                if not first:
                    pe.wait_ge(s_hlo, 2 * t - 1)
                for gu in range(2):
                    for c in range(HC):
                        ins = m.matmul(pT[:, gu, :], x2c[:, c, :], WA[:, gu, c, :], start=(c == 0), stop=(c == HC - 1))
                ins.then_inc(s_xA, 1)

            def project_base(t, gu, first=False):
                if gu == 0:
                    pe.wait_ge(s_x2lo, t + 1)
                if first:
                    pe.wait_ge(s_wlo, HC * (gu + 1))
                else:
                    pe.wait_ge((s_gadd, s_uadd)[gu], 2 * t)
                pp = (pG, pU)[gu]
                for c in range(HC):
                    ins = split_product([pp[:, a, 0:IH] for a in range(2)], x2h[:, c, :], x2l[:, c, :],
                                        [Wbase_hi[:, gu, c, a * IH:(a + 1) * IH] for a in range(2)],
                                        [Wbase_lo[:, gu, c, a * IH:(a + 1) * IH] for a in range(2)], c == 0, c == HC - 1)
                ins.then_inc((s_bg, s_bu)[gu], 1)

            def mask_T(t, k, gu):
                pe.wait_ge(s_xm, 4 * t + 2 * k + gu + 1)
                pe.wait_ge(s_xAc, 2 * t + 1 + gu)
                for c in range(EC):
                    ins = m.transpose(pT[:, gu, c * P:(c + 1) * P], xm[:, gu, c * P:(c + 1) * P], ident[:, :])
                ins.then_inc(s_xT, 1)

            def expand_B(t, k, gu, first=False):
                pe.wait_ge(s_xlo, 4 * t + 2 * k + gu + 1)
                if k == 0:
                    pe.wait_ge((s_bgc, s_buc)[gu], t + 1)
                else:
                    pe.wait_ge((s_gadd, s_uadd)[gu], 2 * t + 1)
                pp = (pG, pU)[gu]
                for c in range(EC):
                    if first:
                        pe.wait_ge(s_wlo, CH_BASE + gu * EC + c + 1)
                    ins = split_product([pp[:, a, 0:IH] for a in range(2)], xmT_hi[:, gu, c, :], xmT_lo[:, gu, c, :],
                                        [WB_hi[:, gu, c, a * IH:(a + 1) * IH] for a in range(2)],
                                        [WB_lo[:, gu, c, a * IH:(a + 1) * IH] for a in range(2)], c == 0, c == EC - 1)
                ins.then_inc((s_Bg, s_Bu)[gu], 1)

            def h_T(t, k):
                pe.wait_ge(s_h, 2 * t + k + 1)
                for c in range(IC):
                    ins = m.transpose(pT[:, c // 4, (c % 4) * P:(c % 4 + 1) * P], hbuf[:, k, c * P:(c + 1) * P], ident[:, :])
                ins.then_inc(s_hT, 1)

            def down_products(t, k, first=False):
                pe.wait_ge(s_hlo, 2 * t + k + 1)
                for c in range(IC):
                    if first:
                        pe.wait_ge(s_wlo, CH_B + c + 1)
                    ins = split_product([pZ[:, k, :]], hT_hi[:, c, :], hT_lo[:, c, :], [WdA_hi[:, c, :]], [WdA_lo[:, c, :]],
                                        c == 0, c == IC - 1)
                ins.then_inc(s_z, 1)

            def z_T(t):
                pe.wait_ge(s_zs, t + 1)
                for c in range(EC):
                    ins = m.transpose(pZ[:, 0, c * P:(c + 1) * P], zs[:, c * P:(c + 1) * P], ident[:, :])
                ins.then_inc(s_zT, 1)

            def down_out(t):
                pe.wait_ge(s_hs1, t + 1)
                pe.wait_ge(s_zs, t + 1)
                for c in range(IC):
                    m.matmul(pZ[:, 1, 0:H], hsumT[:, c, :], Wbd[:, c, :], start=(c == 0), stop=False)
                pe.wait_ge(s_zTc, t + 1)
                for c in range(EC):
                    ins = m.matmul(pZ[:, 1, 0:H], zT[:, c, :], WdB[:, c, :], start=False, stop=(c == EC - 1))
                ins.then_inc(s_y, 1)

            def tile(t, first=False, last=False, second=False):
                mask_T(t, 0, 1)
                expand_B(t, 0, 0, first)
                pe.wait_ge(s_xlo, 4 * t + 1)
                mask_T(t, 1, 0)
                expand_B(t, 0, 1, first)
                if not first:
                    pe.wait_ge(s_xlo, 4 * t + 3)
                    h_T(t - 1, 1)
                expand_B(t, 1, 0)
                if not first:
                    pe.wait_ge(s_hlo, 2 * t)
                    pe.wait_ge(s_hs1, t)
                mask_T(t, 1, 1)
                if not first:
                    if not second:
                        pe.wait_ge(s_yo, t - 1)
                    down_products(t - 1, 1)
                expand_B(t, 1, 1)
                if not first:
                    z_T(t - 1)
                h_T(t, 0)
                if not first:
                    down_out(t - 1)
                down_products(t, 0, first)
                if not last:
                    project_A(t + 1)
                    project_base(t + 1, 0)
                    mask_T(t + 1, 0, 0)
                    project_base(t + 1, 1)

            pe.wait_ge(s_route, 1)
            project_A(0, True)
            project_base(0, 0, True)
            mask_T(0, 0, 0)
            project_base(0, 1, True)
            tile(0, first=True)
            pe.wait_ge(d_Wbd, 16)
            pe.wait_ge(d_WdB, 16)
            tile(1, second=True)
            with pe.Fori(2, NT - 1) as t:
                tile(t)
            tile(NT - 1, last=True)
            h_T(NT - 1, 1)
            pe.wait_ge(s_yo, NT - 1)
            down_products(NT - 1, 1)
            z_T(NT - 1)
            down_out(NT - 1)


_INS = ['x', 'fside_BxS2xS2_0', 'ctx_1024', 'g_xattn', 'g_ffn', 'L0_ffn_expert_wealth', 'L0_ffn_conf_W', 'L0_ffn_conf_b',
        'L0_ffn_base_gate', 'L0_ffn_base_up', 'L0_ffn_base_down', 'L0_ffn_gate_A', 'L0_ffn_gate_B', 'L0_ffn_up_A',
        'L0_ffn_up_B', 'L0_ffn_down_A', 'L0_ffn_down_B']


def kernel(**inputs):
    import numpy as _np
    import concourse.bacc as _bacc
    from concourse import mybir as _mybir
    from concourse.bass_utils import run_bass_kernel_spmd as _run

    nc = _bacc.Bacc("TRN2", target_bir_lowering=False, num_devices=1)
    arrays, args = {}, []
    for name in _INS:
        a = _np.ascontiguousarray(inputs[name])
        arrays[f"in_{name}_dram"] = a
        args.append(nc.dram_tensor(f"in_{name}_dram", a.shape, _mybir.dt.from_np(a.dtype), kind="ExternalInput").ap())
    shape = inputs['x'].shape
    args.append(nc.dram_tensor("out_0_dram", shape, _mybir.dt.from_np(_np.dtype('float32')), kind="ExternalOutput").ap())
    build(nc, *args)
    r = _run(nc, [arrays], core_ids=[0])
    return r.results[0]["out_0_dram"]
```

```python
from contextlib import ExitStack

import concourse.bass as bass
from concourse import mybir

ALU = mybir.AluOpType
ACT = mybir.ActivationFunctionType
F32 = mybir.dt.float32
F32R = mybir.dt.float32r
I32 = mybir.dt.int32
U32 = mybir.dt.uint32
BF16 = mybir.dt.bfloat16
AX_X = mybir.AxisListType.X

P = 128
EPS = 1e-6
LN_EPS = 1e-5
QMAX = 127.0
ROUND = 1.5 * 2.0 ** 23
BIG = 3.0e38


GE = 2


def pair_tiles(pairs, groups):
    return (pairs + groups * (P - 1)) // P


def build(nc, x, fside, ctxw, g_xattn, g_ffn, wealth, conf_W, conf_b,
          base_gate, base_up, base_down, gate_A, gate_B, up_A, up_B, down_A, down_B, xn, yg, out):
    NB, S, H = x.shape
    I2 = ctxw.shape[2]
    E, _, R = gate_A.shape
    I = base_gate.shape[1]
    ER = E * R
    SCALING = 16.0 / 64.0
    TB = S // P
    NT = NB * TB
    HC, EC, IC = H // P, ER // P, I // P
    IH = I // 2
    K = 2
    NG = K * NT
    PAIRS = NG * P
    G = E // GE
    GR = GE * R
    PT = pair_tiles(PAIRS, G)
    assert yg.shape[0] == PAIRS + PT * P and GR == P and NG * P == 2 * NB * S
    assert TB == 2 and HC == 2 and I2 == P and ER == 512 and IH <= 512 and fside.shape[1] == S

    stack = ExitStack()
    with stack:
        def sem(name):
            return stack.enter_context(nc.semaphore(name))

        def sb(name, shape, dt=F32, scope=stack):
            return scope.enter_context(nc.sbuf_tensor(name, shape, dt))

        def ps(name, shape, dt=F32, scope=stack):
            return scope.enter_context(nc.psum_tensor(name, shape, dt))

        xs_all = sb("x_resid", [P, NT, H])
        ident = sb("ident", [P, P])
        identb = sb("identb", [P, P], BF16)
        Wbase_hi = sb("Wbase_hi", [P, 2, HC, I], F32R)
        Wbase_lo = sb("Wbase_lo", [P, 2, HC, I], F32R)
        WB_hi = sb("WB_hi", [P, 2, G, I], F32R)
        WB_lo = sb("WB_lo", [P, 2, G, I], F32R)
        WA_hi = sb("WA_hi", [P, HC, 2, G, GR], F32R)
        WA_lo = sb("WA_lo", [P, HC, 2, G, GR], F32R)
        WdA_hi = sb("WdA_hi", [P, IC, G, GR], F32R)
        WdA_lo = sb("WdA_lo", [P, IC, G, GR], F32R)
        WdB_hi = sb("WdB_hi", [P, G, H], F32R)
        WdB_lo = sb("WdB_lo", [P, G, H], F32R)
        raw = sb("raw", [P, 2, 1024])
        gid = sb("gid", [1, PT], I32)
        dest = sb("dest", [P, PT], I32)
        tok = sb("tok", [P, PT], I32)
        mask = sb("mask", [P, PT, GE])
        share = sb("share", [P, K, NT])
        gates = sb("gates", [P, 2])

        part1 = ExitStack()
        with part1:
            def s1(name, shape, dt=F32):
                return sb(name, shape, dt, part1)
            q1 = s1("q1", [P, NB, 4, H])
            q1i = s1("q1i", [P, 2, 4, H], BF16)
            q1T = s1("q1T", [P, 2, 2, HC, S], BF16)
            ones = s1("ones", [P, P])
            q2 = s1("q2", [P, NB, 4, I2])
            q2i = q1i[:, :, 0:2, :].rearrange("p r i (a q) -> p r (i a) q", a=2)
            q2T = q1T[:, :, :, 0, :]
            bst = s1("bst", [P, NT, 6])
            mv = s1("mv", [P, NT, 2])
            rstd = s1("rstd", [P, NT])
            amx = s1("amx", [P, 2, NB, HC])
            s_rs = s1("s_rs", [P, 2, NB, HC])
            tmp8 = s1("tmp8", [P, NB, HC])
            diag = s1("diag", [P, 4, P])
            am1 = s1("am1", [P, NB, 4])
            inv1 = s1("inv1", [P, NB, 4])
            sc1 = s1("sc1", [P, NB, 4])
            wrow = s1("wrow", [P, 2, S])
            hq = s1("hq", [P, 2, TB, S])
            amx2 = s1("amx2", [P, 2, NB])
            s_rs2 = s1("s_rs2", [P, 2, NB])
            tmp4 = s1("tmp4", [P, NB])
            am2 = s1("am2", [P, NB, 4])
            inv2 = s1("inv2", [P, NB, 4])
            sc2 = s1("sc2", [P, NB, 4])
            sc2g = s1("sc2g", [P, NB, TB])
            bst2 = s1("bst2", [P, NT, 6])
            mv2 = s1("mv2", [P, NT, 2])
            rstd2 = s1("rstd2", [P, NT])
            cW = s1("cW", [E, H])
            x2T = q1[:, :, 2:4, :]
            cWT = s1("cWT", [P, HC, E])
            rows = s1("rows", [P, 2, E])
            gin = s1("gin", [P, 2])
            bids = s1("bids", [P, NT, E])
            eq = s1("eq", [P, NT, E])
            pick = s1("pick", [P, K, NT, E])
            pickb = s1("pickb", [P, NG, G], BF16)
            gp = s1("gp", [P, NG, G])
            par = s1("par", [P, NG])
            before = s1("before", [P, P])
            beforeb = s1("beforeb", [P, P], BF16)
            onesb = s1("onesb", [P, P], BF16)
            place = s1("place", [P, NG, G])
            placef = s1("placef", [P, NG])
            ptile = s1("ptile", [P, NG])
            prow = s1("prow", [P, NG])
            csum = s1("csum", [P, 3, 2 * G])
            tiles_g = s1("tiles_g", [P, G])
            start_g = s1("start_g", [P, G])
            icol = s1("icol", [P, P], I32)
            irow = s1("irow", [P, 1], I32)
            ipad = s1("ipad", [P, PT], I32)
            fcol = s1("fcol", [P, P])
            frow = s1("frow", [P, 1])
            fpad = s1("fpad", [P, PT])
            atrow = q1i[:, :, :, :].rearrange("p r i h -> p (r i h)").rearrange("p (g q) -> p g q", g=NG)
            attile = s1("attile", [P, NG, PT])
            attrib = s1("attrib", [P, NG, 4, PT], BF16)
            sorted_ = s1("sorted", [P, 4, PT])
            destf = s1("destf", [P, PT])
            past = s1("past", [1, PT, G])
            gidf = s1("gidf", [1, PT])
            best = s1("best", [P, 2, NT])
            key = s1("key", [P, NT])
            down = s1("down", [P, E])
            dif = s1("dif", [P, NT])
        part2 = ExitStack()
        with part2:
            def s2(name, shape, dt=F32):
                return sb(name, shape, dt, part2)
            Wd_hi = s2("Wd_hi", [P, IC, H + GR], F32R)
            Wd_lo = s2("Wd_lo", [P, IC, H + GR], F32R)
            xin = s2("xin", [P, H])
            xT_hi = s2("xT_hi", [P, HC, P], F32R)
            xT_lo = s2("xT_lo", [P, HC, P], F32R)
            xa = s2("xa", [P, 2, GE, R])
            xaT_hi = s2("xaT_hi", [P, 2, P], F32R)
            xaT_lo = s2("xaT_lo", [P, 2, P], F32R)
            sg = s2("sg", [P, I])
            hbuf = s2("hbuf", [P, I])
            hT_hi = s2("hT_hi", [P, IC, P], F32R)
            hT_lo = s2("hT_lo", [P, IC, P], F32R)
            zb = s2("zb", [P, GE, R])
            zT_hi = s2("zT_hi", [P, P], F32R)
            zT_lo = s2("zT_lo", [P, P], F32R)
            yb = s2("yb", [P, H])
        part3 = ExitStack()
        with part3:
            yr = sb("yr", [P, K, NT, H], F32, part3)

        psum = ExitStack()
        with psum:
            A = [ps(f"bank{i}", [P, 512], F32, psum) for i in range(8)]
        psum = ExitStack()
        with psum:
            Ab = [ps(f"bankb{i}", [P, 1024], BF16, psum) for i in range(8)]
        psum = ExitStack()
        with psum:
            pG = ps("pG", [P, 2, 512], F32, psum)
            pU = ps("pU", [P, 2, 512], F32, psum)
            pT = ps("pT", [P, 2, 512], F32, psum)
            pY = ps("pY", [P, 512], F32, psum)
            pX = ps("pX", [P, 512], F32, psum)

        d_c, d_small = sem("d_c"), sem("d_small")
        d_x, d_w = [sem(f"d_x{b}") for b in range(NB)], [sem(f"d_w{b}") for b in range(NB)]
        d_xn = sem("d_xn")
        d_raw = [sem(f"d_raw{i}") for i in range(2)]
        s_ident, s_identb, s_ones, s_down1 = sem("s_ident"), sem("s_identb"), sem("s_ones"), sem("s_down0")
        s_whi, s_wlo = sem("s_whi"), sem("s_wlo")
        s_stat, s_var, s_std, s_rstd, s_xn = sem("s_stat"), sem("s_var"), sem("s_std"), sem("s_rstd"), sem("s_xn")
        s_wT, s_xT1, s_cT, s_aT = sem("s_wT"), sem("s_xT1"), sem("s_cT"), sem("s_aT")
        s_wamax, s_xamax, s_camax, s_aamax = sem("s_wamax"), sem("s_xamax"), sem("s_camax"), sem("s_aamax")
        s_ratio, s_sq, s_srs = sem("s_ratio"), sem("s_sq"), sem("s_srs")
        s_diag, s_bc, s_smooth, s_am1, s_inv1 = sem("s_diag"), sem("s_bc"), sem("s_smooth"), sem("s_am1"), sem("s_inv1")
        s_scaled, s_clip, s_q1i, s_q1Tp, s_q1T = sem("s_scaled"), sem("s_clip"), sem("s_q1i"), sem("s_q1Tp"), sem("s_q1T")
        s_diagw, s_wbc, s_wrow, s_mm1, s_deq1 = sem("s_diagw"), sem("s_wbc"), sem("s_wrow"), sem("s_mm1"), sem("s_deq1")
        s_sg, s_a = sem("s_sg"), sem("s_a")
        s_ratio2, s_sq2, s_srs2 = sem("s_ratio2"), sem("s_sq2"), sem("s_srs2")
        s_diag2, s_bc2, s_smooth2, s_am2, s_inv2 = sem("s_diag2"), sem("s_bc2"), sem("s_smooth2"), sem("s_am2"), sem("s_inv2")
        s_scaled2, s_clip2, s_q2i, s_q2Tp, s_q2T = sem("s_scaled2"), sem("s_clip2"), sem("s_q2i"), sem("s_q2Tp"), sem("s_q2T")
        s_diagc, s_cbc, s_crow, s_mm2, s_deq2, s_x1 = sem("s_diagc"), sem("s_cbc"), sem("s_crow"), sem("s_mm2"), sem("s_deq2"), sem("s_x1")
        s_gate = sem("s_gate")
        s_stat2, s_var2, s_std2, s_rstd2, s_x2 = sem("s_stat2"), sem("s_var2"), sem("s_std2"), sem("s_rstd2"), sem("s_x2")
        s_x2Tp, s_x2T, s_cWTp, s_cWT, s_conf = sem("s_x2Tp"), sem("s_x2T"), sem("s_cWTp"), sem("s_cWT"), sem("s_conf")
        s_logit, s_sig, s_bids, s_route, s_dif, s_share = sem("s_logit"), sem("s_sig"), sem("s_bids"), sem("s_route"), sem("s_dif"), sem("s_share")
        s_zero = sem("s_zero")
        s_before, s_onesb, s_iota = sem("s_before"), sem("s_onesb"), sem("s_iota")
        s_before0 = sem("s_before0")
        s_pickb, s_rank, s_atrow, s_attrib, s_sorted, s_plan = (sem("s_pickb"), sem("s_rank"), sem("s_atrow"), sem("s_attrib"),
                                                               sem("s_sorted"), sem("s_plan"))
        d_xin, d_y = sem("d_xin"), sem("d_y")
        s_xT, s_xhi, s_xlo = sem("s_xT"), sem("s_xhi"), sem("s_xlo")
        s_A, s_xac, s_xaT, s_xahi, s_xalo = sem("s_A"), sem("s_xac"), sem("s_xaT"), sem("s_xahi"), sem("s_xalo")
        s_bu, s_g, s_u, s_silu, s_h = sem("s_bu"), sem("s_g"), sem("s_u"), sem("s_silu"), sem("s_h")
        s_hT, s_hhi, s_hlo = sem("s_hT"), sem("s_hhi"), sem("s_hlo")
        s_Wd = sem("s_Wd")
        s_down, s_zc, s_zT, s_zhi, s_zlo, s_y, s_yc = (sem("s_downp"), sem("s_zc"), sem("s_zT"), sem("s_zhi"), sem("s_zlo"),
                                                       sem("s_y"), sem("s_yc"))
        d_rows = [sem(f"d_rows{b}") for b in range(NB)]
        s_out1, s_outr, d_out = sem("s_out1"), sem("s_outr"), sem("d_out")

        chunks = []

        def view(n):
            return raw[:, n % 2, :]

        def add(moves, hi, lo, width):
            chunks.append((moves, hi, lo, width))

        for c in range(HC):
            n = len(chunks)
            add([(view(n)[:, gu * ER:(gu + 1) * ER].rearrange("p (e r) -> p e r", e=E),
                  w[:, c * P:(c + 1) * P, :].rearrange("e h r -> h e r")) for gu, w in enumerate((gate_A, up_A))],
                WA_hi[:, c].rearrange("p a g r -> p (a g r)"), WA_lo[:, c].rearrange("p a g r -> p (a g r)"), 2 * ER)
        CH_A = len(chunks)
        for gu, w in enumerate((base_gate, base_up)):
            for c in range(HC):
                add([(view(len(chunks))[:, 0:I], w[c * P:(c + 1) * P, :])], Wbase_hi[:, gu, c, :], Wbase_lo[:, gu, c, :], I)
        for gu, w in enumerate((gate_B, up_B)):
            for g in range(G):
                add([(view(len(chunks))[:, 0:I], w[GE * g:GE * (g + 1)].rearrange("e r i -> (e r) i"))],
                    WB_hi[:, gu, g, :], WB_lo[:, gu, g, :], I)
        CH_B = len(chunks)
        for c0 in range(0, IC, 2):
            n, c1 = len(chunks), min(c0 + 2, IC)
            add([(view(n)[:, (c - c0) * ER:(c - c0 + 1) * ER].rearrange("p (e r) -> p e r", e=E),
                  down_A[:, c * P:(c + 1) * P, :].rearrange("e i r -> i e r")) for c in range(c0, c1)],
                WdA_hi[:, c0:c1].rearrange("p c g r -> p (c g r)"), WdA_lo[:, c0:c1].rearrange("p c g r -> p (c g r)"), (c1 - c0) * ER)
        CH_DA = len(chunks)
        add([(view(CH_DA).rearrange("p (g h) -> p g h", g=G), down_B.rearrange("(g a) r h -> (a r) g h", a=GE))],
            WdB_hi[:, :, :].rearrange("p g h -> p (g h)"), WdB_lo[:, :, :].rearrange("p g h -> p (g h)"), G * H)
        CH_1 = len(chunks)
        for c0, c1 in ((0, 4), (4, IC)):
            w = (c1 - c0) * H
            add([(view(len(chunks))[:, 0:w].rearrange("p (c h) -> p c h", h=H),
                  base_down[c0 * P:c1 * P, :].rearrange("(c p) h -> p c h", p=P))],
                Wd_hi[:, c0:c1, 0:H], Wd_lo[:, c0:c1, 0:H], w)
        NCH = len(chunks)
        landed = []
        for n in range(NCH):
            landed.append((landed[n - 2] if n >= 2 else 0) + 16 * len(chunks[n][0]))

        def results(b, k):
            g0 = (k * NT + TB * b) * P
            return yg[g0:g0 + TB * P, :].rearrange("(t p) h -> p t h", p=P)

        block = stack.enter_context(nc.Block())

        @block.sync
        def _(sp):
            xv = x.rearrange("b (j p) h -> p (b j) h", p=P)
            for b in range(NB):
                sp.dma_start(xs_all[:, 2 * b:2 * b + 2, :], xv[:, 2 * b:2 * b + 2, :]).then_inc(d_x[b], 16)
            for n, (moves, _, _, _) in enumerate(chunks):
                if n >= 2:
                    sp.wait_ge(s_wlo, n - 1)
                for dst, src in moves:
                    sp.dma_start(dst, src).then_inc(d_raw[n % 2], 16)
            for b in range(NB):
                sp.wait_ge(s_x2, TB * (b + 1))
                sp.dma_start(xn[b * S:(b + 1) * S, :].rearrange("(t p) h -> p t h", p=P), q1[:, b, 0:2, :]).then_inc(d_xn, 16)
            sp.wait_ge(d_y, 16 * PT)
            for b in range(NB):
                for k in range(K):
                    sp.dma_start(yr[:, k, TB * b:TB * (b + 1), :], results(b, k)).then_inc(d_rows[b], 16)
            ov = out.rearrange("b (j p) h -> b p j h", p=P)
            for b in range(NB):
                sp.wait_ge(s_outr, TB * (b + 1))
                sp.dma_start(ov[b], xs_all[:, TB * b:TB * (b + 1), :]).then_inc(d_out, 16)
            sp.wait_ge(d_out, 16 * NB)

        @block.gpsimd
        def _(pool):
            g = nc.gpsimd
            g.memset(ident[:, :], 0.0).then_inc(s_zero, 1)
            g.memset(ones[:, :], 1.0).then_inc(s_ones, 1)
            pool.wait_ge(s_zero, 1)
            g.affine_select(out=ident[:, :], in_=ident[:, :], compare_op=ALU.not_equal, fill=1.0, base=0,
                            pattern=[[-1, P]], channel_multiplier=1).then_inc(s_ident, 1)
            pool.wait_ge(s_ident, 1)
            g.tensor_copy(identb[:, :], ident[:, :]).then_inc(s_identb, 1)
            g.memset(before[:, :], 1.0).then_inc(s_before0, 1)
            pool.wait_ge(s_before0, 1)
            g.affine_select(out=before[:, :], in_=before[:, :], compare_op=ALU.is_ge, fill=0.0, base=-1,
                            pattern=[[1, P]], channel_multiplier=-1).then_inc(s_before, 1)
            pool.wait_ge(s_before, 1)
            g.tensor_copy(beforeb[:, :], before[:, :]).then_inc(s_before, 1)
            g.memset(onesb[:, :], 1.0).then_inc(s_onesb, 1)
            for e in range(E):
                g.memset(down[:, e:e + 1], float(E - e)).then_inc(s_down1, 1)
            g.iota(icol[:, :], pattern=[[1, P]], base=0, channel_multiplier=0).then_inc(s_iota, 1)
            g.iota(irow[:, :], pattern=[[1, 1]], base=0, channel_multiplier=1).then_inc(s_iota, 1)
            g.iota(ipad[:, :], pattern=[[P, PT]], base=PAIRS, channel_multiplier=1).then_inc(s_iota, 1)

            def split_lo(n):
                _, hi, lo, width = chunks[n]
                src = raw[:, n % 2, 0:width]
                if n >= CH_1:
                    src = src.rearrange("p (c h) -> p c h", h=H)
                pool.wait_ge(s_whi, n + 1)
                g.tensor_tensor(lo, src, hi, ALU.subtract).then_inc(s_wlo, 1)

            for n in range(CH_1):
                split_lo(n)

            def gather(j):
                g.indirect_dma_start(out=xin[:, :], out_offset=None, in_=xn,
                                     in_offset=bass.IndirectOffsetOnAxis(ap=tok[:, j:j + 1], axis=0)).then_inc(d_xin, 16)

            def scatter(j):
                pool.wait_ge(s_yc, j + 1)
                g.indirect_dma_start(out=yg, out_offset=bass.IndirectOffsetOnAxis(ap=dest[:, j:j + 1], axis=0),
                                     in_=yb[:, :], in_offset=None).then_inc(d_y, 16)

            pool.wait_ge(s_plan, 1)
            pool.wait_ge(d_xn, 16 * NB)
            gather(0)
            for n in range(CH_1, NCH):
                split_lo(n)
            for j in range(1, PT + 4):
                if j >= 4:
                    scatter(j - 4)
                if j < PT:
                    pool.wait_ge(s_xT, j)
                    gather(j)

        @block.scalar
        def _(act):
            a = nc.scalar
            wv = fside.rearrange("b (j p) h -> p b j h", p=P)
            cv = ctxw.rearrange("b (j p) h -> p b j h", p=P)
            for b in range(NB):
                a.dma_start(q1[:, b, 2:4, :], wv[:, b]).then_inc(d_w[b], 16)
            for b in range(NB):
                a.dma_start(q2[:, b, 2:4, :], cv[:, b]).then_inc(d_c, 16)
            a.dma_start(cW[:, :], conf_W).then_inc(d_small, 16)
            a.dma_start(rows[:, 0, :], conf_b.rearrange("(a e) -> a e", a=1).to_broadcast([P, E])).then_inc(d_small, 16)
            a.dma_start(rows[:, 1, :], wealth.rearrange("(a e) -> a e", a=1).to_broadcast([P, E])).then_inc(d_small, 16)
            a.dma_start(gin[:, 0:1], g_xattn.rearrange("(a e) -> a e", a=1).to_broadcast([P, 1])).then_inc(d_small, 16)
            a.dma_start(gin[:, 1:2], g_ffn.rearrange("(a e) -> a e", a=1).to_broadcast([P, 1])).then_inc(d_small, 16)

            def split_hi(count):
                for n in range(done[0], done[0] + count):
                    _, hi, _, width = chunks[n]
                    src = raw[:, n % 2, 0:width]
                    if n >= CH_1:
                        src = src.rearrange("p (c h) -> p c h", h=H)
                    act.wait_ge(d_raw[n % 2], landed[n])
                    a.copy(hi, src).then_inc(s_whi, 1)
                done[0] += count

            done = [0]
            act.wait_ge(d_small, 80)
            a.activation(gates[:, :], gin[:, :], ACT.Tanh).then_inc(s_gate, 1)
            act.wait_ge(s_var, 1)
            a.activation(rstd[:, :], mv[:, :, 1], ACT.Sqrt).then_inc(s_std, 1)
            split_hi(3)
            act.wait_ge(s_ratio, 1)
            a.activation(s_rs[:, 1], tmp8[:, :, :], ACT.Sqrt).then_inc(s_sq, 1)
            split_hi(2)
            for b in range(NB):
                for i in range(4):
                    act.wait_ge(s_inv1, b + 1)
                    a.activation(q1[:, b, i, :], q1[:, b, i, :], ACT.Copy, scale=inv1[:, b, i:i + 1]).then_inc(s_scaled, 1)
                split_hi(1)
                if b >= 1:
                    act.wait_ge(s_q1Tp, b)
                    if b >= 3:
                        act.wait_ge(s_mm1, b - 2)
                    a.copy(q1T[:, (b - 1) % 2].rearrange("p a c s -> p (a c s)"), Ab[(b - 1) % 2][:, :]).then_inc(s_q1T, 1)
                    act.wait_ge(s_wbc, b)
                    if b >= 3:
                        act.wait_ge(s_deq1, b - 2)
                    a.copy(wrow[:, (b - 1) % 2, :], A[2 + (b - 1) % 2][:, 0:S]).then_inc(s_wrow, 1)
            for b in (NB - 1,):
                act.wait_ge(s_q1Tp, b + 1)
                act.wait_ge(s_mm1, b - 1)
                a.copy(q1T[:, b % 2].rearrange("p a c s -> p (a c s)"), Ab[b % 2][:, :]).then_inc(s_q1T, 1)
                act.wait_ge(s_wbc, b + 1)
                act.wait_ge(s_deq1, b - 1)
                a.copy(wrow[:, b % 2, :], A[2 + b % 2][:, 0:S]).then_inc(s_wrow, 1)
            for b in range(NB):
                act.wait_ge(s_deq1, b + 1)
                a.activation(hq[:, b % 2, :, 0:I2], hq[:, b % 2, :, 0:I2], ACT.Silu).then_inc(s_sg, 1)
                split_hi(1)
            act.wait_ge(s_ratio2, 1)
            a.activation(s_rs2[:, 1], tmp4[:, :], ACT.Sqrt).then_inc(s_sq2, 1)
            split_hi(2)
            for b in range(NB):
                for i in range(4):
                    act.wait_ge(s_inv2, b + 1)
                    a.activation(q2[:, b, i, :], q2[:, b, i, :], ACT.Copy, scale=inv2[:, b, i:i + 1]).then_inc(s_scaled2, 1)
            for b in range(NB):
                act.wait_ge(s_q2Tp, b + 1)
                if b >= 2:
                    act.wait_ge(s_mm2, b - 1)
                a.copy(q2T[:, b % 2], Ab[b % 2][:, 0:2 * S].rearrange("p (a s) -> p a s", a=2)).then_inc(s_q2T, 1)
                act.wait_ge(s_cbc, b + 1)
                if b >= 2:
                    act.wait_ge(s_deq2, b - 1)
                a.copy(wrow[:, b % 2, :], A[2 + b % 2][:, 0:S]).then_inc(s_crow, 1)
            split_hi(CH_1 - done[0])
            act.wait_ge(s_var2, 1)
            a.activation(rstd2[:, :], mv2[:, :, 1], ACT.Sqrt).then_inc(s_std2, 1)
            for b in range(NB):
                act.wait_ge(s_x2Tp, b + 1)
                a.copy(x2T[:, b], A[b][:, :].rearrange("p (c s) -> p c s", c=HC)).then_inc(s_x2T, 1)
            act.wait_ge(s_logit, 1)
            a.activation(bids[:, :, :], bids[:, :, :], ACT.Sigmoid).then_inc(s_sig, 1)
            act.wait_ge(s_dif, 1)
            a.activation(share[:, 0, :], dif[:, :], ACT.Sigmoid).then_inc(s_share, 1)
            a.activation(share[:, 1, :], dif[:, :], ACT.Sigmoid, scale=-1.0).then_inc(s_share, 1)

            act.wait_ge(s_plan, 1)
            act.wait_ge(d_xn, 16 * NB)
            act.wait_ge(s_share, 3)

            def x_hi(j):
                act.wait_ge(s_xT, j + 1)
                if not (isinstance(j, int) and j == 0):
                    act.wait_ge(s_bu, j)
                a.copy(xT_hi[:, :, :].rearrange("p c q -> p (c q)"), pX[:, 0:H]).then_inc(s_xhi, 1)

            def xa_hi(j, first=False):
                act.wait_ge(s_xaT, j + 1)
                if not first:
                    act.wait_ge(s_u, j)
                a.copy(xaT_hi[:, :, :].rearrange("p a q -> p (a q)"), pX[:, 0:2 * P]).then_inc(s_xahi, 1)

            def group(j):
                src = gid[0:1, j:j + 1] if isinstance(j, int) else gid[0:1, bass.ds(j, 1)]
                return act.value_load(src, min_val=0, max_val=G - 1)

            def down_A_group(j, first=False):
                g = group(j)
                if first:
                    act.wait_ge(s_wlo, CH_DA)
                else:
                    act.wait_ge(s_down, j)
                for i, (to, w) in enumerate(((Wd_hi, WdA_hi), (Wd_lo, WdA_lo))):
                    a.copy(to[:, :, H:H + GR], w[:, :, bass.ds(g, 1), :].rearrange("p c a r -> p c (a r)")).then_inc(s_Wd, 1)

            def silu(j, first=False):
                act.wait_ge(s_g, j + 1)
                if not first:
                    act.wait_ge(s_h, j)
                a.activation(sg[:, :].rearrange("p (a i) -> p a i", a=2), pG[:, :, 0:IH], ACT.Silu).then_inc(s_silu, 1)

            def h_hi(j, first=False):
                act.wait_ge(s_hT, j + 1)
                if not first:
                    act.wait_ge(s_down, j)
                a.copy(hT_hi[:, :, :].rearrange("p c q -> p (c q)"),
                       pT[:, :, :].rearrange("p a q -> p (a q)")[:, 0:I]).then_inc(s_hhi, 1)

            def z_hi(j, first=False):
                act.wait_ge(s_zT, j + 1)
                if not first:
                    act.wait_ge(s_y, j)
                a.copy(zT_hi[:, :], pT[:, 1, 3 * P:4 * P]).then_inc(s_zhi, 1)

            def tile(j, back=True, back2=True, last=False):
                if back:
                    h_hi(j - 1, not back2)
                silu(j, not back)
                if not last:
                    x_hi(j + 1)
                down_A_group(j, not back)
                if not last:
                    xa_hi(j + 1)
                if back:
                    z_hi(j - 1, not back2)

            x_hi(0)
            split_hi(NCH - CH_1)
            xa_hi(0, first=True)
            tile(0, back=False)
            tile(1, back2=False)
            with act.Fori(2, PT - 1) as j:
                tile(j)
            tile(PT - 1, last=True)
            h_hi(PT - 1)
            z_hi(PT - 1)

        @block.vector
        def _(dve):
            v = nc.vector

            chains = [0]
            s_chain = sem("s_chain")

            def link(ins):
                ins.then_inc(s_chain, 1)
                chains[0] += 1
                dve.wait_ge(s_chain, chains[0])

            for t in range(NT):
                dve.wait_ge(d_x[t // TB], 16)
                v.bn_stats(bst[:, t, :], xs_all[:, t, :]).then_inc(s_stat, 1)
            for t in range(NT):
                dve.wait_ge(s_stat, t + 1)
                ins = v.bn_aggr(mv[:, t, :], bst[:, t, :])
            link(ins)
            v.tensor_scalar(mv[:, :, 1], mv[:, :, 1], LN_EPS, None, ALU.add).then_inc(s_var, 1)
            for b in range(NB):
                dve.wait_ge(s_wT, b + 1)
                v.tensor_reduce(amx[:, 1, b, :], A[4 + b][:, :].rearrange("p (c s) -> p c s", c=HC), AX_X, ALU.max,
                                apply_absolute_value=True).then_inc(s_wamax, 1)
            dve.wait_ge(s_std, 1)
            v.reciprocal(rstd[:, :], rstd[:, :]).then_inc(s_rstd, 1)
            dve.wait_ge(s_rstd, 1)
            for t in range(NT):
                v.tensor_scalar(q1[:, t // TB, t % TB, :], xs_all[:, t, :], mv[:, t, 0:1], rstd[:, t:t + 1],
                                ALU.subtract, ALU.mult).then_inc(s_xn, 1)
            for b in range(NB):
                dve.wait_ge(s_xT1, b + 1)
                v.tensor_reduce(amx[:, 0, b, :], A[b][:, :].rearrange("p (c s) -> p c s", c=HC), AX_X, ALU.max,
                                apply_absolute_value=True).then_inc(s_xamax, 1)
            dve.wait_ge(s_xamax, NB)
            dve.wait_ge(s_wamax, NB)
            v.tensor_scalar(amx[:, :, :, :], amx[:, :, :, :], EPS, None, ALU.max).then_inc(s_srs, 1)
            dve.wait_ge(s_srs, 1)
            v.reciprocal(tmp8[:, :, :], amx[:, 1]).then_inc(s_srs, 1)
            dve.wait_ge(s_srs, 2)
            v.tensor_tensor(tmp8[:, :, :], amx[:, 0], tmp8[:, :, :], ALU.mult).then_inc(s_ratio, 1)
            dve.wait_ge(s_sq, 1)
            v.tensor_scalar(s_rs[:, 1], s_rs[:, 1], EPS, None, ALU.max).then_inc(s_srs, 1)
            dve.wait_ge(s_srs, 3)
            v.reciprocal(s_rs[:, 0], s_rs[:, 1]).then_inc(s_srs, 1)
            dve.wait_ge(s_srs, 4)

            def smooth(b):
                dve.wait_ge(s_bc, b + 1)
                for w in range(2):
                    dve.wait_ge(s_xn, NT) if w == 0 else dve.wait_ge(d_w[b], 16)
                    qv = q1[:, b, 2 * w:2 * w + 2, :]
                    v.tensor_tensor(qv, qv, A[b][:, w * H:(w + 1) * H].unsqueeze(1).to_broadcast([P, 2, H]),
                                    ALU.mult).then_inc(s_smooth, 1)
                dve.wait_ge(s_smooth, 2 * b + 2)
                v.tensor_reduce(am1[:, b, :], q1[:, b], AX_X, ALU.max, apply_absolute_value=True).then_inc(s_am1, 1)
                dve.wait_ge(s_am1, b + 1)
                scales(am1[:, b, :], inv1[:, b, :], sc1[:, b, :], s_inv1, b)

            def scales(am, inv, sc, s_inv, b):
                link(v.tensor_scalar(am, am, EPS, None, ALU.max))
                v.tensor_scalar(sc, am, 1.0 / QMAX, None, ALU.mult)
                link(v.reciprocal(inv, am))
                v.tensor_scalar(inv, inv, QMAX, None, ALU.mult).then_inc(s_inv, 1)

            for b in range(NB):
                if b >= 1:
                    dve.wait_ge(s_bc, b)
                v.tensor_tensor(diag[:, :, :].rearrange("p (w c) q -> p w c q", w=2),
                                ident[:, :].unsqueeze(1).unsqueeze(1).to_broadcast([P, 2, HC, P]),
                                s_rs[:, :, b, :].unsqueeze(3).to_broadcast([P, 2, HC, P]), ALU.mult).then_inc(s_diag, 1)
                if b >= 1:
                    smooth(b - 1)
            smooth(NB - 1)
            for b in range(NB):
                dve.wait_ge(s_scaled, 4 * b + 4)
                qf = q1[:, b].rearrange("p i h -> p (i h)")
                link(v.tensor_scalar(qf, qf, ROUND, ROUND, ALU.add, ALU.subtract))
                if b >= 2:
                    dve.wait_ge(s_q1Tp, b - 1)
                v.tensor_scalar(q1i[:, b % 2].rearrange("p i h -> p (i h)"), qf, QMAX, -QMAX, ALU.min, ALU.max).then_inc(s_q1i, 1)
                if b >= 1:
                    dve.wait_ge(s_wbc, b)
                v.tensor_tensor(diag[:, 0:2, :], ident[:, :].unsqueeze(1).to_broadcast([P, 2, P]),
                                sc1[:, b, 2:4].unsqueeze(2).to_broadcast([P, 2, P]), ALU.mult).then_inc(s_diagw, 1)
            def deq1(b):
                dve.wait_ge(s_mm1, b + 1)
                dve.wait_ge(s_wrow, b + 1)
                if b >= 2:
                    dve.wait_ge(s_a, b - 1)
                for j in range(TB):
                    ins = v.scalar_tensor_tensor(out=hq[:, b % 2, j, :], in0=A[4 + b % 2][:, j * S:(j + 1) * S],
                                                 scalar=sc1[:, b, j:j + 1], in1=wrow[:, b % 2, :], op0=ALU.mult, op1=ALU.mult)
                ins.then_inc(s_deq1, 1)

            def a_mul(b):
                dve.wait_ge(s_sg, b + 1)
                v.tensor_tensor(q2[:, b, 0:2, :], hq[:, b % 2, :, 0:I2], hq[:, b % 2, :, I2:2 * I2], ALU.mult).then_inc(s_a, 1)

            for b in range(NB):
                deq1(b)
                if b >= 1:
                    a_mul(b - 1)
            a_mul(NB - 1)
            for b in range(NB):
                dve.wait_ge(s_cT, b // 2 + 1)
                v.tensor_reduce(amx2[:, 1, b:b + 1], A[6 + b // 2][:, (b % 2) * S:(b % 2 + 1) * S], AX_X, ALU.max,
                                apply_absolute_value=True)
            for b in range(NB):
                dve.wait_ge(s_aT, b + 1)
                ins = v.tensor_reduce(amx2[:, 0, b:b + 1], A[b][:, 0:S], AX_X, ALU.max, apply_absolute_value=True)
            link(ins)
            link(v.tensor_scalar(amx2[:, :, :], amx2[:, :, :], EPS, None, ALU.max))
            link(v.reciprocal(tmp4[:, :], amx2[:, 1]))
            v.tensor_tensor(tmp4[:, :], amx2[:, 0], tmp4[:, :], ALU.mult).then_inc(s_ratio2, 1)
            dve.wait_ge(s_sq2, 1)
            link(v.tensor_scalar(s_rs2[:, 1], s_rs2[:, 1], EPS, None, ALU.max))
            link(v.reciprocal(s_rs2[:, 0], s_rs2[:, 1]))

            def smooth2(b):
                dve.wait_ge(s_bc2, b + 1)
                dve.wait_ge(d_c, 16 * NB)
                link(v.tensor_tensor(q2[:, b].rearrange("p (w j) q -> p w j q", w=2), q2[:, b].rearrange("p (w j) q -> p w j q", w=2),
                                     A[b][:, 0:2 * I2].rearrange("p (w q) -> p w q", w=2).unsqueeze(2).to_broadcast([P, 2, 2, I2]),
                                     ALU.mult))
                link(v.tensor_reduce(am2[:, b, :], q2[:, b], AX_X, ALU.max, apply_absolute_value=True))
                scales(am2[:, b, :], inv2[:, b, :], sc2[:, b, :], s_inv2, b)

            dve.wait_ge(s_a, NB)
            for b in range(NB):
                if b >= 1:
                    dve.wait_ge(s_bc2, b)
                v.tensor_tensor(diag[:, 0:2, :], ident[:, :].unsqueeze(1).to_broadcast([P, 2, P]),
                                s_rs2[:, :, b].unsqueeze(2).to_broadcast([P, 2, P]), ALU.mult).then_inc(s_diag2, 1)
                if b >= 1:
                    smooth2(b - 1)
            smooth2(NB - 1)
            dve.wait_ge(s_gate, 1)
            dve.wait_ge(s_inv2, NB)
            link(v.tensor_scalar(sc2g[:, :, :], sc2[:, :, 0:2], gates[:, 0:1], None, ALU.mult))
            for b in range(NB):
                dve.wait_ge(s_scaled2, 4 * b + 4)
                qf = q2[:, b].rearrange("p i h -> p (i h)")
                link(v.tensor_scalar(qf, qf, ROUND, ROUND, ALU.add, ALU.subtract))
                if b >= 2:
                    dve.wait_ge(s_q2Tp, b - 1)
                v.tensor_scalar(q2i[:, b % 2].rearrange("p i h -> p (i h)"), qf, QMAX, -QMAX, ALU.min, ALU.max).then_inc(s_q2i, 1)
                if b >= 1:
                    dve.wait_ge(s_cbc, b)
                v.tensor_tensor(diag[:, 0:2, :], ident[:, :].unsqueeze(1).to_broadcast([P, 2, P]),
                                sc2[:, b, 2:4].unsqueeze(2).to_broadcast([P, 2, P]), ALU.mult).then_inc(s_diagc, 1)
            for b in range(NB):
                dve.wait_ge(s_mm2, b + 1)
                dve.wait_ge(s_crow, b + 1)
                for j in range(TB):
                    ins = v.scalar_tensor_tensor(out=hq[:, b % 2, j, :], in0=A[4 + b % 2][:, j * H:(j + 1) * H],
                                                 scalar=sc2g[:, b, j:j + 1], in1=wrow[:, b % 2, :], op0=ALU.mult, op1=ALU.mult)
                ins.then_inc(s_deq2, 1)
                dve.wait_ge(s_deq2, b + 1)
                xv_ = xs_all[:, 2 * b:2 * b + 2, :]
                v.tensor_tensor(xv_, xv_, hq[:, b % 2], ALU.add).then_inc(s_x1, 1)
            for t in range(NT):
                dve.wait_ge(s_x1, t // TB + 1)
                v.bn_stats(bst2[:, t, :], xs_all[:, t, :]).then_inc(s_stat2, 1)
            for t in range(NT):
                dve.wait_ge(s_stat2, t + 1)
                ins = v.bn_aggr(mv2[:, t, :], bst2[:, t, :])
            link(ins)
            v.tensor_scalar(mv2[:, :, 1], mv2[:, :, 1], LN_EPS, None, ALU.add).then_inc(s_var2, 1)
            dve.wait_ge(s_std2, 1)
            link(v.reciprocal(rstd2[:, :], rstd2[:, :]))
            for t in range(NT):
                v.tensor_scalar(q1[:, t // TB, t % TB, :], xs_all[:, t, :], mv2[:, t, 0:1], rstd2[:, t:t + 1],
                                ALU.subtract, ALU.mult).then_inc(s_x2, 1)
            dve.wait_ge(s_cWTp, 1)
            v.tensor_copy(cWT[:, :, :], A[5][:, 0:HC * E].rearrange("p (c e) -> p c e", c=HC)).then_inc(s_cWT, 1)

            def row(r):
                return rows[:, r, :].unsqueeze(1).to_broadcast([P, NT, E])

            def per_tile(ap):
                return ap.unsqueeze(2).to_broadcast([P, NT, E])
            dve.wait_ge(s_conf, 1)
            dve.wait_ge(d_small, 80)
            v.tensor_tensor(bids[:, :, :], A[4][:, 0:NT * E].rearrange("p (t e) -> p t e", t=NT), row(0), ALU.add).then_inc(s_logit, 1)
            dve.wait_ge(s_sig, 1)
            dve.wait_ge(s_down1, E)
            down_b = down[:, :].unsqueeze(1).to_broadcast([P, NT, E])
            link(v.tensor_tensor(bids[:, :, :], bids[:, :, :], row(1), ALU.mult))
            for k in range(K):
                link(v.tensor_reduce(best[:, k, :], bids[:, :, :], AX_X, ALU.max))
                link(v.tensor_tensor(eq[:, :, :], bids[:, :, :], per_tile(best[:, k, :]), ALU.is_equal))
                link(v.tensor_tensor(eq[:, :, :], eq[:, :, :], down_b, ALU.mult))
                link(v.tensor_reduce(key[:, :], eq[:, :, :], AX_X, ALU.max))
                link(v.tensor_tensor(pick[:, k], down_b, per_tile(key[:, :]), ALU.is_equal))
                if k == 0:
                    link(v.scalar_tensor_tensor(out=bids[:, :, :], in0=pick[:, k], scalar=-BIG, in1=bids[:, :, :],
                                                op0=ALU.mult, op1=ALU.add))
                else:
                    v.tensor_tensor(dif[:, :], best[:, 0, :], best[:, 1, :], ALU.subtract).then_inc(s_dif, 1)
            pick_ = pick[:, :, :, :].rearrange("p k t (g a) -> p (k t) g a", a=GE)
            link(v.tensor_reduce(gp[:, :, :], pick_, AX_X, ALU.add))
            v.tensor_copy(pickb[:, :, :], gp[:, :, :]).then_inc(s_pickb, 1)
            v.tensor_reduce(par[:, :], pick_[:, :, :, 1], AX_X, ALU.add)
            dve.wait_ge(s_iota, 3)
            v.tensor_copy(fcol[:, :], icol[:, :])
            v.tensor_copy(frow[:, :], irow[:, :])
            v.tensor_copy(fpad[:, :], ipad[:, :])
            link(v.memset(csum[:, :, :], 0.0))

            dve.wait_ge(s_rank, 1)
            CNT = NG * G

            def floor_of(out_, in_, plus):
                link(v.tensor_scalar(out_, in_, 1.0 / P, plus - 0.5 + 0.5 / P, ALU.mult, ALU.add))
                link(v.tensor_scalar(out_, out_, ROUND, ROUND, ALU.add, ALU.subtract))

            floor_of(tiles_g[:, :], A[6][:, CNT:CNT + G], 1.0 - 1.0 / P)
            link(v.tensor_copy(csum[:, 0, G:2 * G], tiles_g[:, :]))
            for i, d in enumerate((1, 2)):
                link(v.tensor_tensor(csum[:, i + 1, G:2 * G], csum[:, i, G:2 * G], csum[:, i, G - d:2 * G - d], ALU.add))
            ends = csum[:, 2, G:2 * G]
            link(v.tensor_tensor(start_g[:, :], ends, tiles_g[:, :], ALU.subtract))
            link(v.scalar_tensor_tensor(out=place[:, :, :], in0=start_g[:, :].unsqueeze(1).to_broadcast([P, NG, G]), scalar=float(P),
                                        in1=A[6][:, 0:CNT].rearrange("p (g e) -> p g e", g=NG), op0=ALU.mult, op1=ALU.add))
            link(v.tensor_tensor(place[:, :, :], place[:, :, :], gp[:, :, :], ALU.mult))
            link(v.tensor_reduce(placef[:, :], place[:, :, :], AX_X, ALU.add))
            floor_of(ptile[:, :], placef[:, :], 0.0)
            link(v.scalar_tensor_tensor(out=prow[:, :], in0=ptile[:, :], scalar=-float(P), in1=placef[:, :], op0=ALU.mult, op1=ALU.add))
            v.tensor_tensor(atrow, prow[:, :].unsqueeze(2).to_broadcast([P, NG, P]),
                            fcol[:, :].unsqueeze(1).to_broadcast([P, NG, P]), ALU.is_equal).then_inc(s_atrow, 1)
            link(v.tensor_tensor(attile[:, :, :], ptile[:, :].unsqueeze(2).to_broadcast([P, NG, PT]),
                                 fcol[:, 0:PT].unsqueeze(1).to_broadcast([P, NG, PT]), ALU.is_equal))
            v.tensor_tensor(attrib[:, :, 0, :], attile[:, :, :], fcol[:, 0:NG].unsqueeze(2).to_broadcast([P, NG, PT]), ALU.mult)
            v.tensor_scalar(attrib[:, :, 1, :], attile[:, :, :], frow[:, :], None, ALU.mult)
            v.tensor_tensor(attrib[:, :, 2, :], attile[:, :, :], par[:, :].unsqueeze(2).to_broadcast([P, NG, PT]), ALU.mult)
            link(v.tensor_copy(attrib[:, :, 3, :], attile[:, :, :]))
            v.tensor_scalar(fpad[:, :], fpad[:, :], 1.0, None, ALU.mult).then_inc(s_attrib, 1)
            link(v.tensor_tensor(past[:, :, :], fcol[0:1, 0:PT].unsqueeze(2).to_broadcast([1, PT, G]),
                                 ends[0:1].unsqueeze(1).to_broadcast([1, PT, G]), ALU.is_ge))
            link(v.tensor_reduce(gidf[:, :], past[:, :, :], AX_X, ALU.add))
            link(v.tensor_scalar(gidf[:, :], gidf[:, :], float(G - 1), None, ALU.min))
            v.tensor_copy(gid[:, :], gidf[:, :])
            dve.wait_ge(s_sorted, 1)
            link(v.tensor_copy(sorted_[:, :, :], A[7][:, 0:4 * PT].rearrange("p (a j) -> p a j", a=4)))
            v.tensor_scalar(mask[:, :, 1], sorted_[:, 2, :], SCALING, None, ALU.mult)
            v.tensor_scalar(mask[:, :, 0], sorted_[:, 2, :], -SCALING, SCALING, ALU.mult, ALU.add)
            link(v.scalar_tensor_tensor(out=destf[:, :], in0=sorted_[:, 0, :], scalar=float(P), in1=sorted_[:, 1, :],
                                        op0=ALU.mult, op1=ALU.add))
            link(v.tensor_tensor(sorted_[:, 3, :], sorted_[:, 3, :], fpad[:, :], ALU.mult))
            link(v.tensor_tensor(destf[:, :], destf[:, :], fpad[:, :], ALU.add))
            link(v.tensor_tensor(destf[:, :], destf[:, :], sorted_[:, 3, :], ALU.subtract))
            link(v.tensor_copy(dest[:, :], destf[:, :]))
            v.tensor_scalar(tok[:, :], dest[:, :], NT * P - 1, None, ALU.bitwise_and).then_inc(s_plan, 1)
            dve.wait_ge(s_share, 2)
            v.tensor_scalar(share[:, :, :], share[:, :, :], gates[:, 1:2], None, ALU.mult).then_inc(s_share, 1)

            dve.wait_ge(s_plan, 1)
            dve.wait_ge(s_share, 3)
            dve.wait_ge(d_xn, 16 * NB)

            def x_lo(j):
                dve.wait_ge(s_xhi, j + 1)
                v.tensor_tensor(xT_lo[:, :, :].rearrange("p c q -> p (c q)"), pX[:, 0:H],
                                xT_hi[:, :, :].rearrange("p c q -> p (c q)"), ALU.subtract).then_inc(s_xlo, 1)

            def mask_of(j, a):
                m_ = mask[:, j, :] if isinstance(j, int) else mask[:, bass.ds(j, 1), :].rearrange("p a e -> p (a e)")
                if a == 1:
                    return m_.unsqueeze(2).to_broadcast([P, GE, R])
                return m_.unsqueeze(1).unsqueeze(3).to_broadcast([P, a, GE, R])

            def xa_mask(j, first=False):
                dve.wait_ge(s_A, j + 1)
                if not first:
                    dve.wait_ge(s_xaT, j)
                v.tensor_tensor(xa[:, :, :, :], pX[:, H:2 * H].rearrange("p (a e r) -> p a e r", a=2, e=GE), mask_of(j, 2),
                                ALU.mult).then_inc(s_xac, 1)

            def z_mask(j, first=False):
                dve.wait_ge(s_down, j + 1)
                if not first:
                    dve.wait_ge(s_zT, j)
                v.tensor_tensor(zb[:, :, :], pY[:, H:H + GR].rearrange("p (e r) -> p e r", e=GE), mask_of(j, 1),
                                ALU.mult).then_inc(s_zc, 1)

            def xa_lo(j):
                dve.wait_ge(s_xahi, j + 1)
                v.tensor_tensor(xaT_lo[:, :, :].rearrange("p a q -> p (a q)"), pX[:, 0:2 * P],
                                xaT_hi[:, :, :].rearrange("p a q -> p (a q)"), ALU.subtract).then_inc(s_xalo, 1)

            def h_mul(j, first=False):
                dve.wait_ge(s_silu, j + 1)
                dve.wait_ge(s_u, j + 1)
                if not first:
                    dve.wait_ge(s_hT, j)
                v.tensor_tensor(hbuf[:, :].rearrange("p (a i) -> p a i", a=2), pU[:, :, 0:IH],
                                sg[:, :].rearrange("p (a i) -> p a i", a=2), ALU.mult).then_inc(s_h, 1)

            def h_lo(j):
                dve.wait_ge(s_hhi, j + 1)
                v.tensor_tensor(hT_lo[:, :, :].rearrange("p c q -> p (c q)"),
                                pT[:, :, :].rearrange("p a q -> p (a q)")[:, 0:I],
                                hT_hi[:, :, :].rearrange("p c q -> p (c q)"), ALU.subtract).then_inc(s_hlo, 1)

            def z_lo(j):
                dve.wait_ge(s_zhi, j + 1)
                v.tensor_tensor(zT_lo[:, :], pT[:, 1, 3 * P:4 * P], zT_hi[:, :], ALU.subtract).then_inc(s_zlo, 1)

            def y_copy(j, first=False):
                dve.wait_ge(s_y, j + 1)
                if not first:
                    dve.wait_ge(d_y, 16 * j)
                v.tensor_copy(yb[:, :], pY[:, 0:H]).then_inc(s_yc, 1)

            def tile(j, back=True, back2=True, last=False, back3=True):
                if back2:
                    y_copy(j - 2, not back3)
                if back:
                    h_lo(j - 1)
                if not last:
                    x_lo(j + 1)
                if back:
                    z_mask(j - 1, not back2)
                if not last:
                    xa_mask(j + 1)
                h_mul(j, not back)
                if not last:
                    xa_lo(j + 1)
                if back:
                    z_lo(j - 1)

            x_lo(0)
            xa_mask(0, True)
            xa_lo(0)
            tile(0, back=False, back2=False)
            tile(1, back2=False)
            tile(2, back3=False)
            with dve.Fori(3, PT - 1) as j:
                tile(j)
            tile(PT - 1, last=True)
            y_copy(PT - 2)
            h_lo(PT - 1)
            z_mask(PT - 1)
            z_lo(PT - 1)
            y_copy(PT - 1)
            for t in range(NT):
                dve.wait_ge(d_rows[t // TB], 16 * K)
                v.scalar_tensor_tensor(out=xs_all[:, t, :], in0=yr[:, 0, t, :], scalar=share[:, 0, t:t + 1], in1=xs_all[:, t, :],
                                       op0=ALU.mult, op1=ALU.add).then_inc(s_out1, 1)
                dve.wait_ge(s_out1, t + 1)
                v.scalar_tensor_tensor(out=xs_all[:, t, :], in0=yr[:, 1, t, :], scalar=share[:, 1, t:t + 1], in1=xs_all[:, t, :],
                                       op0=ALU.mult, op1=ALU.add).then_inc(s_outr, 1)

        @block.tensor
        def _(pe):
            m = nc.tensor
            pe.wait_ge(s_ident, 1)
            pe.wait_ge(s_identb, 1)
            pe.wait_ge(s_ones, 1)
            for b in range(NB):
                pe.wait_ge(d_w[b], 16)
                for c in range(HC):
                    for j in range(TB):
                        ins = m.transpose(A[4 + b][:, c * S + j * P:c * S + (j + 1) * P], q1[:, b, 2 + j, c * P:(c + 1) * P], ident[:, :])
                ins.then_inc(s_wT, 1)
            for b in range(NB):
                pe.wait_ge(s_xn, TB * (b + 1))
                for c in range(HC):
                    for j in range(TB):
                        ins = m.transpose(A[b][:, c * S + j * P:c * S + (j + 1) * P], q1[:, b, j, c * P:(c + 1) * P], ident[:, :])
                ins.then_inc(s_xT1, 1)
            for b in range(NB):
                pe.wait_ge(d_c, 16 * NB)
                pe.wait_ge(s_wamax, NB)
                for j in range(TB):
                    ins = m.transpose(A[6 + b // 2][:, (b % 2) * S + j * P:(b % 2) * S + (j + 1) * P], q2[:, b, 2 + j, :], ident[:, :])
                if b % 2:
                    ins.then_inc(s_cT, 1)
            pe.wait_ge(s_xamax, NB)
            for b in range(NB):
                pe.wait_ge(s_diag, b + 1)
                m.matmul(A[b][:, :], ones[:, :], diag[:, :, :].rearrange("p a q -> p (a q)"), start=True, stop=True).then_inc(s_bc, 1)
            pe.wait_ge(s_smooth, 2 * NB)

            def products1(b):
                pe.wait_ge(s_q1T, b + 1)
                if b >= 2:
                    pe.wait_ge(s_deq1, b - 1)
                for j in range(TB):
                    for c in range(HC):
                        ins = m.matmul(A[4 + b % 2][:, j * S:(j + 1) * S], q1T[:, b % 2, 0, c, j * P:(j + 1) * P],
                                       q1T[:, b % 2, 1, c, :], start=(c == 0), stop=(c == HC - 1))
                ins.then_inc(s_mm1, 1)

            for b in range(NB):
                pe.wait_ge(s_q1i, b + 1)
                if b >= 2:
                    pe.wait_ge(s_q1T, b - 1)
                for w in range(2):
                    for c in range(HC):
                        for j in range(TB):
                            o = ((w * HC + c) * TB + j) * P
                            ins = m.transpose(Ab[b % 2][:, o:o + P], q1i[:, b % 2, 2 * w + j, c * P:(c + 1) * P], identb[:, :])
                ins.then_inc(s_q1Tp, 1)
                pe.wait_ge(s_diagw, b + 1)
                if b >= 2:
                    pe.wait_ge(s_wrow, b - 1)
                m.matmul(A[2 + b % 2][:, 0:S], ones[:, :], diag[:, 0:2, :].rearrange("p a q -> p (a q)"), start=True, stop=True).then_inc(s_wbc, 1)
                if b >= 1:
                    products1(b - 1)
            products1(NB - 1)
            pe.wait_ge(s_wrow, NB)
            for b in range(NB):
                pe.wait_ge(s_a, b + 1)
                for j in range(TB):
                    ins = m.transpose(A[b][:, j * P:(j + 1) * P], q2[:, b, j, :], ident[:, :])
                ins.then_inc(s_aT, 1)
            for b in range(NB):
                pe.wait_ge(s_diag2, b + 1)
                m.matmul(A[b][:, 0:2 * I2], ones[:, :], diag[:, 0:2, :].rearrange("p a q -> p (a q)"), start=True, stop=True).then_inc(s_bc2, 1)
            pe.wait_ge(s_inv2, NB)

            def products2(b):
                pe.wait_ge(s_q2T, b + 1)
                if b >= 2:
                    pe.wait_ge(s_deq2, b - 1)
                for j in range(TB):
                    ins = m.matmul(A[4 + b % 2][:, j * H:(j + 1) * H], q2T[:, b % 2, 0, j * P:(j + 1) * P], q2T[:, b % 2, 1, :],
                                   start=True, stop=True)
                ins.then_inc(s_mm2, 1)

            for b in range(NB):
                pe.wait_ge(s_q2i, b + 1)
                if b >= 2:
                    pe.wait_ge(s_q2T, b - 1)
                for i in range(4):
                    ins = m.transpose(Ab[b % 2][:, i * P:(i + 1) * P], q2i[:, b % 2, i, :], identb[:, :])
                ins.then_inc(s_q2Tp, 1)
                pe.wait_ge(s_diagc, b + 1)
                if b >= 2:
                    pe.wait_ge(s_crow, b - 1)
                m.matmul(A[2 + b % 2][:, 0:S], ones[:, :], diag[:, 0:2, :].rearrange("p a q -> p (a q)"), start=True, stop=True).then_inc(s_cbc, 1)
                if b >= 1:
                    products2(b - 1)
            products2(NB - 1)
            pe.wait_ge(s_deq2, NB)
            pe.wait_ge(s_crow, NB)
            pe.wait_ge(d_small, 80)
            for c in range(HC):
                ins = m.transpose(A[5][:, c * E:(c + 1) * E], cW[:, c * P:(c + 1) * P], ident[0:E, 0:E])
            ins.then_inc(s_cWTp, 1)
            for b in range(NB):
                pe.wait_ge(s_x2, TB * (b + 1))
                for c in range(HC):
                    for j in range(TB):
                        ins = m.transpose(A[b][:, c * S + j * P:c * S + (j + 1) * P], q1[:, b, j, c * P:(c + 1) * P], ident[:, :])
                ins.then_inc(s_x2Tp, 1)
            pe.wait_ge(s_cWT, 1)
            for t in range(NT):
                pe.wait_ge(s_x2T, t // TB + 1)
                for c in range(HC):
                    ins = m.matmul(A[4][:, t * E:(t + 1) * E], x2T[:, t // TB, c, (t % TB) * P:(t % TB + 1) * P], cWT[:, c, :], start=(c == 0), stop=(c == HC - 1))
            ins.then_inc(s_conf, 1)

            pe.wait_ge(s_pickb, 1)
            pe.wait_ge(s_before, 2)
            pe.wait_ge(s_onesb, 1)
            CNT = NG * G
            pf = pickb[:, :, :].rearrange("p g e -> p (g e)")
            m.matmul(A[6][:, 0:CNT], beforeb[:, :], pf, start=True, stop=True)
            for d in range(1, NG):
                m.matmul(A[6][:, d * G:CNT], onesb[:, :], pf[:, 0:CNT - d * G], start=False, stop=True, skip_group_check=True)
            for g in range(NG):
                ins = m.matmul(A[6][:, CNT:CNT + G], onesb[:, :], pickb[:, g, :], start=False, stop=(g == NG - 1), skip_group_check=True)
            ins.then_inc(s_rank, 1)
            pe.wait_ge(s_atrow, 1)
            pe.wait_ge(s_attrib, 1)
            for g in range(NG):
                ins = m.matmul(A[7][:, 0:4 * PT], atrow[:, g, :], attrib[:, g].rearrange("p a j -> p (a j)"),
                               start=(g == 0), stop=(g == NG - 1))
            ins.then_inc(s_sorted, 1)

            pe.wait_ge(s_plan, 1)

            def group(j):
                src = gid[0:1, j:j + 1] if isinstance(j, int) else gid[0:1, bass.ds(j, 1)]
                return pe.value_load(src, min_val=0, max_val=G - 1)

            def split_product(outs, hi, lo, whi, wlo, first, last, **kw):
                n = len(outs)
                for i in range(n):
                    m.matmul(outs[i], hi, whi[i], start=(first and i in starts(kw, n)), stop=False, skip_group_check=True)
                for i in range(n):
                    m.matmul(outs[i], hi, wlo[i], start=False, stop=False, skip_group_check=True)
                for i in range(n):
                    ins = m.matmul(outs[i], lo, whi[i], start=False, stop=last, skip_group_check=True)
                return ins

            def starts(kw, n):
                return range(1 if kw.get("one_bank") else n)

            def x_T(j, first=False):
                pe.wait_ge(d_xin, 16 * (j + 1))
                if not first:
                    pe.wait_ge(s_xalo, j)
                for c in range(HC):
                    ins = m.transpose(pX[:, c * P:(c + 1) * P], xin[:, c * P:(c + 1) * P], ident[:, :])
                ins.then_inc(s_xT, 1)

            def project_A(j, e, first=False):
                pe.wait_ge(s_xlo, j + 1)
                for c in range(HC):
                    wsl = [w[:, c, :, bass.ds(e, 1), :].rearrange("p a g r -> p a (g r)") for w in (WA_hi, WA_lo)]
                    ins = split_product([pX[:, H:2 * H].rearrange("p (a r) -> p a r", a=2)], xT_hi[:, c, :], xT_lo[:, c, :],
                                        [wsl[0]], [wsl[1]], c == 0, c == HC - 1)
                ins.then_inc(s_A, 1)

            def xa_T(j):
                pe.wait_ge(s_xac, j + 1)
                for gu in range(2):
                    ins = m.transpose(pX[:, gu * P:(gu + 1) * P], xa[:, gu].rearrange("p e r -> p (e r)"), ident[:, :])
                ins.then_inc(s_xaT, 1)

            def base(j, gu, first=False):
                if gu == 0 and not first:
                    pe.wait_ge(s_silu, j)
                pp = (pG, pU)[gu]
                for c in range(HC):
                    if first:
                        pe.wait_ge(s_wlo, CH_A + gu * HC + c + 1)
                    ins = split_product([pp[:, i, 0:IH] for i in range(2)], xT_hi[:, c, :], xT_lo[:, c, :],
                                        [Wbase_hi[:, gu, c, i * IH:(i + 1) * IH] for i in range(2)],
                                        [Wbase_lo[:, gu, c, i * IH:(i + 1) * IH] for i in range(2)], c == 0, False)
                if gu == 1:
                    ins.then_inc(s_bu, 1)

            def expand_B(j, gu, e, first=False):
                if gu == 0:
                    pe.wait_ge(s_xalo, j + 1)
                if first:
                    pe.wait_ge(s_wlo, CH_B)
                pp = (pG, pU)[gu]
                wsl = [[w[:, gu, bass.ds(e, 1), i * IH:(i + 1) * IH].rearrange("p a w -> p (a w)") for i in range(2)] for w in (WB_hi, WB_lo)]
                split_product([pp[:, i, 0:IH] for i in range(2)], xaT_hi[:, gu, :], xaT_lo[:, gu, :],
                              wsl[0], wsl[1], False, True).then_inc((s_g, s_u)[gu], 1)

            def h_T(j, first=False):
                pe.wait_ge(s_h, j + 1)
                if not first:
                    pe.wait_ge(s_hlo, j)
                for c in range(IC):
                    ins = m.transpose(pT[:, c // 4, (c % 4) * P:(c % 4 + 1) * P], hbuf[:, c * P:(c + 1) * P], ident[:, :])
                ins.then_inc(s_hT, 1)

            def down_products(j, first=False):
                pe.wait_ge(s_hlo, j + 1)
                pe.wait_ge(s_Wd, 2 * (j + 1))
                if first:
                    pe.wait_ge(s_wlo, NCH)
                else:
                    pe.wait_ge(s_yc, j)
                for c in range(IC):
                    ins = split_product([pY[:, 0:H + GR]], hT_hi[:, c, :], hT_lo[:, c, :],
                                        [Wd_hi[:, c, :]], [Wd_lo[:, c, :]], c == 0, c == IC - 1)
                ins.then_inc(s_down, 1)

            def z_T(j):
                pe.wait_ge(s_zc, j + 1)
                m.transpose(pT[:, 1, 3 * P:4 * P], zb[:, :, :].rearrange("p e r -> p (e r)"), ident[:, :]).then_inc(s_zT, 1)

            def down_B_products(j, e):
                pe.wait_ge(s_zlo, j + 1)
                wsl = [w[:, bass.ds(e, 1), :].rearrange("p a w -> p (a w)") for w in (WdB_hi, WdB_lo)]
                split_product([pY[:, 0:H]], zT_hi[:, :], zT_lo[:, :], [wsl[0]], [wsl[1]], False, True).then_inc(s_y, 1)

            def tile(j, back=True, back2=True, last=False, back3=True):
                e = group(j)
                base(j, 0, not back)
                if back2:
                    down_B_products(j - 2, group(j - 2))
                if back:
                    h_T(j - 1, not back2)
                if not last:
                    x_T(j + 1)
                expand_B(j, 0, e, not back)
                base(j, 1, not back)
                if back:
                    down_products(j - 1, not back2)
                if not last:
                    project_A(j + 1, group(j + 1))
                expand_B(j, 1, e)
                if not last:
                    xa_T(j + 1)
                if back:
                    z_T(j - 1)

            x_T(0, True)
            pe.wait_ge(s_wlo, CH_A)
            project_A(0, group(0))
            xa_T(0)
            tile(0, back=False, back2=False)
            tile(1, back2=False)
            tile(2, back3=False)
            with pe.Fori(3, PT - 1) as j:
                tile(j)
            tile(PT - 1, last=True)
            down_B_products(PT - 2, group(PT - 2))
            h_T(PT - 1)
            down_products(PT - 1)
            z_T(PT - 1)
            down_B_products(PT - 1, group(PT - 1))


_INS = ['x', 'fside_BxS2xS2_0', 'ctx_1024', 'g_xattn', 'g_ffn', 'L0_ffn_expert_wealth', 'L0_ffn_conf_W', 'L0_ffn_conf_b',
        'L0_ffn_base_gate', 'L0_ffn_base_up', 'L0_ffn_base_down', 'L0_ffn_gate_A', 'L0_ffn_gate_B', 'L0_ffn_up_A',
        'L0_ffn_up_B', 'L0_ffn_down_A', 'L0_ffn_down_B']


def kernel(**inputs):
    import numpy as _np
    import concourse.bacc as _bacc
    from concourse import mybir as _mybir
    from concourse.bass_utils import run_bass_kernel_spmd as _run

    nc = _bacc.Bacc("TRN2", target_bir_lowering=False, num_devices=1)
    arrays, args = {}, []
    for name in _INS:
        a = _np.ascontiguousarray(inputs[name])
        arrays[f"in_{name}_dram"] = a
        args.append(nc.dram_tensor(f"in_{name}_dram", a.shape, _mybir.dt.from_np(a.dtype), kind="ExternalInput").ap())
    shape = inputs['x'].shape
    tokens, pairs = shape[0] * shape[1], 2 * shape[0] * shape[1]
    tiles = pair_tiles(pairs, inputs['L0_ffn_gate_A'].shape[0] // GE)
    for name, rows in (("normed", tokens), ("results", pairs + 128 * tiles)):
        args.append(nc.dram_tensor(name, [rows, shape[2]], _mybir.dt.float32, kind="Internal").ap())
    args.append(nc.dram_tensor("out_0_dram", shape, _mybir.dt.from_np(_np.dtype('float32')), kind="ExternalOutput").ap())
    build(nc, *args)
    r = _run(nc, [arrays], core_ids=[0])
    return r.results[0]["out_0_dram"]
```

```python
from contextlib import ExitStack

import concourse.bass as bass
from concourse import mybir

ALU = mybir.AluOpType
ACT = mybir.ActivationFunctionType
F32 = mybir.dt.float32
F32R = mybir.dt.float32r
I32 = mybir.dt.int32
U32 = mybir.dt.uint32
BF16 = mybir.dt.bfloat16
AX_X = mybir.AxisListType.X

P = 128
EPS = 1e-6
LN_EPS = 1e-5
QMAX = 127.0
ROUND = 1.5 * 2.0 ** 23
BIG = 3.0e38


GE = 2


def pair_tiles(pairs, groups):
    return (pairs + groups * (P - 1)) // P


def products_of(m):
    def split_product(outs, hi, lo, whi, wlo, first, last):
        n = len(outs)
        for i in range(n):
            m.matmul(outs[i], hi, whi[i], start=first, stop=False, skip_group_check=True)
        for i in range(n):
            m.matmul(outs[i], hi, wlo[i], start=False, stop=False, skip_group_check=True)
        for i in range(n):
            ins = m.matmul(outs[i], lo, whi[i], start=False, stop=last, skip_group_check=True)
        return ins

    return split_product


def build(nc, x, fside, ctxw, g_xattn, g_ffn, wealth, conf_W, conf_b,
          base_gate, base_up, base_down, gate_A, gate_B, up_A, up_B, down_A, down_B, xn, gun, yg, out):
    NB, S, H = x.shape
    I2 = ctxw.shape[2]
    E, _, R = gate_A.shape
    I = base_gate.shape[1]
    ER = E * R
    SCALING = 16.0 / 64.0
    TB = S // P
    NT = NB * TB
    HC, EC, IC = H // P, ER // P, I // P
    IH = I // 2
    K = 2
    NG = K * NT
    PAIRS = NG * P
    G = E // GE
    GR = GE * R
    PT = pair_tiles(PAIRS, G)
    assert yg.shape[0] == PAIRS + PT * P and GR == P and NG * P == 2 * NB * S
    assert PT % 2 == 1
    assert TB == 2 and HC == 2 and I2 == P and ER == 512 and IH <= 512 and fside.shape[1] == S

    stack = ExitStack()
    with stack:
        def sem(name):
            return stack.enter_context(nc.semaphore(name))

        def sb(name, shape, dt=F32, scope=stack):
            return scope.enter_context(nc.sbuf_tensor(name, shape, dt))

        def ps(name, shape, dt=F32, scope=stack):
            return scope.enter_context(nc.psum_tensor(name, shape, dt))

        xs_all = sb("x_resid", [P, NT, H])
        ident = sb("ident", [P, P])
        identb = sb("identb", [P, P], BF16)
        WB_hi = sb("WB_hi", [P, 2, G, I], F32R)
        WB_lo = sb("WB_lo", [P, 2, G, I], F32R)
        WA_hi = sb("WA_hi", [P, HC, 2, G, GR], F32R)
        WA_lo = sb("WA_lo", [P, HC, 2, G, GR], F32R)
        WdA_hi = sb("WdA_hi", [P, IC, G, GR], F32R)
        WdA_lo = sb("WdA_lo", [P, IC, G, GR], F32R)
        WdB_hi = sb("WdB_hi", [P, G, H], F32R)
        WdB_lo = sb("WdB_lo", [P, G, H], F32R)
        RING, RW = 4, 512
        raw = sb("raw", [P, RING, RW])
        gid = sb("gid", [1, PT], I32)
        dest = sb("dest", [P, PT], I32)
        tok = sb("tok", [P, PT], I32)
        mask = sb("mask", [P, PT, GE])
        share = sb("share", [P, K, NT])
        warm2 = sb("warm2", [P, 1])
        gates = sb("gates", [P, 2])

        base_scope = ExitStack()
        Wbase_hi = sb("Wbase_hi", [P, 2, HC, I], F32R, base_scope)
        Wbase_lo = sb("Wbase_lo", [P, 2, HC, I], F32R, base_scope)
        part1 = ExitStack()
        with part1:
            def s1(name, shape, dt=F32):
                return sb(name, shape, dt, part1)
            ones = s1("ones", [P, P])
            bst = s1("bst", [P, NT, 6])
            mv = s1("mv", [P, NT, 2])
            rstd = s1("rstd", [P, NT])
            amx = s1("amx", [P, 2, NB, HC])
            s_rs = s1("s_rs", [P, 2, NB, HC])
            tmp8 = s1("tmp8", [P, NB, HC])
            am1 = s1("am1", [P, NB, 4])
            inv1 = s1("inv1", [P, NB, 4])
            sc1 = s1("sc1", [P, NB, 4])
            amx2 = s1("amx2", [P, 2, NB])
            s_rs2 = s1("s_rs2", [P, 2, NB])
            tmp4 = s1("tmp4", [P, NB])
            am2 = s1("am2", [P, NB, 4])
            inv2 = s1("inv2", [P, NB, 4])
            sc2 = s1("sc2", [P, NB, 4])
            sc2g = s1("sc2g", [P, NB, TB])
            bst2 = s1("bst2", [P, NT, 6])
            mv2 = s1("mv2", [P, NT, 2])
            rstd2 = s1("rstd2", [P, NT])
            cW = s1("cW", [E, H])
            cWT_hi = s1("cWT_hi", [P, HC, E], F32R)
            cWT_lo = s1("cWT_lo", [P, HC, E], F32R)
            rows = s1("rows", [P, 2, E])
            gin = s1("gin", [P, 2])
            warm = s1("warm", [P, 1])
            rounder = s1("rounder", [P, 2])
            bids = s1("bids", [P, NT, E])
            eq = s1("eq", [P, NT, E])
            pick = s1("pick", [P, K, NT, E])
            pickb = s1("pickb", [P, NG, G], BF16)
            gp = s1("gp", [P, NG, G])
            par = s1("par", [P, NG])
            before = s1("before", [P, P])
            beforeb = s1("beforeb", [P, P], BF16)
            onesb = s1("onesb", [P, P], BF16)
            place = s1("place", [P, NG, G])
            placef = s1("placef", [P, NG])
            ptile = s1("ptile", [P, NG])
            prow = s1("prow", [P, NG])
            csum = s1("csum", [P, 3, 2 * G])
            tiles_g = s1("tiles_g", [P, G])
            start_g = s1("start_g", [P, G])
            icol = s1("icol", [P, P], I32)
            irow = s1("irow", [P, 1], I32)
            ipad = s1("ipad", [P, PT], I32)
            fcol = s1("fcol", [P, P])
            frow = s1("frow", [P, 1])
            fpad = s1("fpad", [P, PT])
            attile = s1("attile", [P, NG, PT])
            attrib = s1("attrib", [P, NG, 4, PT], BF16)
            sorted_ = s1("sorted", [P, 4, PT])
            destf = s1("destf", [P, PT])
            past = s1("past", [1, PT, G])
            gidf = s1("gidf", [1, PT])
            best = s1("best", [P, 2, NT])
            key = s1("key", [P, NT])
            down = s1("down", [P, E])
            dif = s1("dif", [P, NT])
            quant = ExitStack()
            with quant:
                q1 = sb("q1", [P, 4, NB, H], F32, quant)
                q2 = sb("q2", [P, NB, 4, I2], F32, quant)
                q1i = sb("q1i", [P, 2, 4, H], BF16, quant)
                q1T = sb("q1T", [P, 2, 2, HC, S], BF16, quant)
                q2i = q1i[:, :, 0:2, :].rearrange("p r i (a q) -> p r (i a) q", a=2)
                q2T = q1T[:, :, :, 0, :]
                hq = sb("hq", [P, 2, TB, S], F32, quant)
                wrow = sb("wrow", [P, 2, S], F32, quant)
                diag = sb("diag", [P, 4, P], F32, quant)
            quant = ExitStack()
            with quant:
                sb("x2_rows", [P, 2, NB, H], F32, quant)
                x2T_hi = sb("x2T_hi", [P, NB, HC, S], F32R, quant)
                x2T_lo = sb("x2T_lo", [P, NB, HC, S], F32R, quant)
                brow = sb("brow", [P, 2, 2, I], F32, quant)
                early = ExitStack()
                with early:
                    confT = sb("confT", [E, NB, S], F32, early)
                atrow = sb("atrow", [P, NG, P], BF16, quant)
        part2 = ExitStack()
        with part2:
            def s2(name, shape, dt=F32):
                return sb(name, shape, dt, part2)
            xin = s2("xin", [P, H])
            xT_hi = s2("xT_hi", [P, HC, P], F32R)
            xT_lo = s2("xT_lo", [P, HC, P], F32R)
            xa = s2("xa", [P, 2, GE, R])
            xaT_hi = s2("xaT_hi", [P, 2, P], F32R)
            xaT_lo = s2("xaT_lo", [P, 2, P], F32R)
            Wd_hi = s2("Wd_hi", [P, IC, H + GR], F32R)
            Wd_lo = s2("Wd_lo", [P, IC, H + GR], F32R)
            gb = s2("gb", [P, I])
            hbuf = s2("hbuf", [P, I])
            hT_hi = s2("hT_hi", [P, IC, P], F32R)
            hT_lo = s2("hT_lo", [P, IC, P], F32R)
            zb = s2("zb", [P, GE, R])
            zT_hi = s2("zT_hi", [P, P], F32R)
            zT_lo = s2("zT_lo", [P, P], F32R)
            yb = s2("yb", [P, H])
        base_scope.close()
        bin_scope = ExitStack()
        with bin_scope:
            bin_ = sb("bin", [P, 2, 2, I], F32, bin_scope)
        part3 = ExitStack()
        with part3:
            yr = sb("yr", [P, K, NT, H], F32, part3)

        psum = ExitStack()
        with psum:
            A = [ps(f"bank{i}", [P, 512], F32, psum) for i in range(8)]
        X2 = [A[3], A[4], A[5], A[7]]
        psum = ExitStack()
        with psum:
            Ab = [ps(f"bankb{i}", [P, 1024], BF16, psum) for i in range(8)]
        psum = ExitStack()
        with psum:
            pG = ps("pG", [P, 2, 512], F32, psum)
            pU = ps("pU", [P, 2, 512], F32, psum)
            pT = ps("pT", [P, 2, 512], F32, psum)
            pY = ps("pY", [P, 512], F32, psum)
            pX = ps("pX", [P, 512], F32, psum)

        d_c, d_small = sem("d_c"), sem("d_small")
        d_x, d_w = [sem(f"d_x{b}") for b in range(NB)], [sem(f"d_w{b}") for b in range(NB)]
        d_xn = sem("d_xn")
        d_raw = [sem(f"d_raw{i}") for i in range(RING)]
        s_ident, s_identb, s_ones, s_down1 = sem("s_ident"), sem("s_identb"), sem("s_ones"), sem("s_down0")
        s_whi, s_wlo = sem("s_whi"), sem("s_wlo")
        s_stat, s_var, s_std, s_rstd, s_xn = sem("s_stat"), sem("s_var"), sem("s_std"), sem("s_rstd"), sem("s_xn")
        s_wT, s_xT1, s_cT, s_aT = sem("s_wT"), sem("s_xT1"), sem("s_cT"), sem("s_aT")
        s_wamax, s_xamax, s_camax, s_aamax = sem("s_wamax"), sem("s_xamax"), sem("s_camax"), sem("s_aamax")
        s_ratio, s_sq, s_srs = sem("s_ratio"), sem("s_sq"), sem("s_srs")
        s_diag, s_bc, s_smooth, s_am1, s_inv1 = sem("s_diag"), sem("s_bc"), sem("s_smooth"), sem("s_am1"), sem("s_inv1")
        s_scaled, s_clip, s_q1i, s_q1Tp, s_q1T = sem("s_scaled"), sem("s_clip"), sem("s_q1i"), sem("s_q1Tp"), sem("s_q1T")
        s_diagw, s_wbc, s_wrow, s_mm1, s_deq1 = sem("s_diagw"), sem("s_wbc"), sem("s_wrow"), sem("s_mm1"), sem("s_deq1")
        s_sg, s_a = sem("s_sg"), sem("s_a")
        s_ratio2, s_sq2, s_srs2 = sem("s_ratio2"), sem("s_sq2"), sem("s_srs2")
        s_diag2, s_bc2, s_smooth2, s_am2, s_inv2 = sem("s_diag2"), sem("s_bc2"), sem("s_smooth2"), sem("s_am2"), sem("s_inv2")
        s_scaled2, s_clip2, s_q2i, s_q2Tp, s_q2T = sem("s_scaled2"), sem("s_clip2"), sem("s_q2i"), sem("s_q2Tp"), sem("s_q2T")
        s_diagc, s_cbc, s_crow, s_mm2, s_deq2, s_x1 = sem("s_diagc"), sem("s_cbc"), sem("s_crow"), sem("s_mm2"), sem("s_deq2"), sem("s_x1")
        s_gate, s_sc2g = sem("s_gate"), sem("s_sc2g")
        s_bg, s_bu, s_bgc, s_buc = sem("s_bg"), sem("s_bu"), sem("s_bgc"), sem("s_buc")
        d_bn = [sem("d_bn0"), sem("d_bn1")]
        s_stat2, s_var2, s_std2, s_rstd2, s_x2 = sem("s_stat2"), sem("s_var2"), sem("s_std2"), sem("s_rstd2"), sem("s_x2")
        s_x2Tp, s_x2hi, s_x2lo, s_cWTp, s_cWT, s_confT, s_confTc, s_conf = sem("s_x2Tp"), sem("s_x2hi"), sem("s_x2lo"), sem("s_cWTp"), sem("s_cWT"), sem("s_confT"), sem("s_confTc"), sem("s_conf")
        s_logit, s_sig, s_bids, s_route, s_dif, s_share = sem("s_logit"), sem("s_sig"), sem("s_bids"), sem("s_route"), sem("s_dif"), sem("s_share")
        s_zero, s_warm, s_rounder = sem("s_zero"), sem("s_warm"), sem("s_rounder")
        s_before, s_onesb, s_iota = sem("s_before"), sem("s_onesb"), sem("s_iota")
        s_before0 = sem("s_before0")
        s_pickb, s_rank, s_atrow, s_attrib, s_sorted, s_plan = (sem("s_pickb"), sem("s_rank"), sem("s_atrow"), sem("s_attrib"),
                                                               sem("s_sorted"), sem("s_plan"))
        d_xin, d_y = sem("d_xin"), sem("d_y")
        d_bin = [sem("d_bin0"), sem("d_bin1")]
        s_gadd, s_uadd = sem("s_gadd"), sem("s_uadd")
        s_direct = sem("s_direct")
        s_xT, s_xhi, s_xlo = sem("s_xT"), sem("s_xhi"), sem("s_xlo")
        s_A, s_xac, s_xaT, s_xahi, s_xalo = sem("s_A"), sem("s_xac"), sem("s_xaT"), sem("s_xahi"), sem("s_xalo")
        s_g, s_u, s_silu, s_h = sem("s_g"), sem("s_u"), sem("s_silu"), sem("s_h")
        s_hT, s_hhi, s_hlo = sem("s_hT"), sem("s_hhi"), sem("s_hlo")
        s_Wd = sem("s_Wd")
        s_down, s_zc, s_zT, s_zhi, s_zlo, s_y, s_yc = (sem("s_downp"), sem("s_zc"), sem("s_zT"), sem("s_zhi"), sem("s_zlo"),
                                                       sem("s_y"), sem("s_yc"))
        d_rows = [sem(f"d_rows{b}") for b in range(NB)]
        s_out1, s_second, d_out = sem("s_out1"), sem("s_second"), sem("d_out")
        s_sum = [sem(f"s_sum{b}") for b in range(NB)]

        chunks = []

        def view(n):
            return raw[:, n % RING, :]

        def add(moves, hi, lo, width):
            chunks.append((moves, hi, lo, width))

        def add_rows(source, hi, lo):
            for i in range(2):
                cols = slice(i * IH, (i + 1) * IH)
                add([(view(len(chunks))[:, 0:IH], source[:, cols])], hi[:, cols], lo[:, cols], IH)

        for gu, w in enumerate((base_gate, base_up)):
            for c in range(HC):
                add_rows(w[c * P:(c + 1) * P, :], Wbase_hi[:, gu, c, :], Wbase_lo[:, gu, c, :])
        CH_BASE = len(chunks)
        for c in range(HC):
            for gu, w in enumerate((gate_A, up_A)):
                add([(view(len(chunks)).rearrange("p (e r) -> p e r", e=E), w[:, c * P:(c + 1) * P, :].rearrange("e h r -> h e r"))],
                    WA_hi[:, c, gu].rearrange("p g r -> p (g r)"), WA_lo[:, c, gu].rearrange("p g r -> p (g r)"), ER)
        CH_A = len(chunks)
        for gu, w in enumerate((gate_B, up_B)):
            for g in range(G):
                add_rows(w[GE * g:GE * (g + 1)].rearrange("e r i -> (e r) i"), WB_hi[:, gu, g, :], WB_lo[:, gu, g, :])
        CH_B = len(chunks)
        for c in range(IC):
            add([(view(len(chunks)).rearrange("p (e r) -> p e r", e=E), down_A[:, c * P:(c + 1) * P, :].rearrange("e i r -> i e r"))],
                WdA_hi[:, c].rearrange("p g r -> p (g r)"), WdA_lo[:, c].rearrange("p g r -> p (g r)"), ER)
        CH_DA = len(chunks)
        for g in range(0, G, 2):
            add([(view(len(chunks)).rearrange("p (g h) -> p g h", g=2), down_B[GE * g:GE * (g + 2)].rearrange("(g a) r h -> (a r) g h", a=GE))],
                WdB_hi[:, g:g + 2, :].rearrange("p g h -> p (g h)"), WdB_lo[:, g:g + 2, :].rearrange("p g h -> p (g h)"), 2 * H)
        CH_1 = len(chunks)
        for c0 in range(0, IC, 2):
            c1 = min(c0 + 2, IC)
            w = (c1 - c0) * H
            add([(view(len(chunks))[:, 0:w].rearrange("p (c h) -> p c h", h=H),
                  base_down[c0 * P:c1 * P, :].rearrange("(c p) h -> p c h", p=P))],
                Wd_hi[:, c0:c1, 0:H], Wd_lo[:, c0:c1, 0:H], w)
        NCH = len(chunks)
        landed = []
        for n in range(NCH):
            landed.append((landed[n - RING] if n >= RING else 0) + 16 * len(chunks[n][0]))

        PRE = NT - 2

        def results(b, k):
            g0 = (k * NT + TB * b) * P
            return yg[g0:g0 + TB * P, :].rearrange("(t p) h -> p t h", p=P)

        def factors_bank(b, w):
            return A[4] if b == 0 and w == 1 else A[b]

        block = stack.enter_context(nc.Block())

        @block.sync
        def _(sp):
            xv = x.rearrange("b (j p) h -> p (b j) h", p=P)
            for b in range(NB):
                sp.dma_start(xs_all[:, 2 * b:2 * b + 2, :], xv[:, 2 * b:2 * b + 2, :]).then_inc(d_x[b], 16)
            for n, (moves, _, _, _) in enumerate(chunks):
                if n >= RING:
                    sp.wait_ge(s_wlo, n - RING + 1)
                for dst, src in moves:
                    sp.dma_start(dst, src).then_inc(d_raw[n % RING], 16)
            sp.wait_ge(d_y, 16 * PT)
            for b in range(NB):
                for k in range(K):
                    sp.dma_start(yr[:, k, TB * b:TB * (b + 1), :], results(b, k)).then_inc(d_rows[b], 16)
            ov = out.rearrange("b (j p) h -> b p j h", p=P)
            for b in range(NB):
                sp.wait_ge(s_sum[b], 1)
                sp.dma_start(ov[b], xs_all[:, TB * b:TB * (b + 1), :]).then_inc(d_out, 16)
            sp.wait_ge(d_out, 16 * NB)

        @block.gpsimd
        def _(pool):
            g = nc.gpsimd
            g.memset(ident[:, :], 0.0).then_inc(s_zero, 1)
            g.memset(ones[:, :], 1.0).then_inc(s_ones, 1)
            pool.wait_ge(s_zero, 1)
            g.affine_select(out=ident[:, :], in_=ident[:, :], compare_op=ALU.not_equal, fill=1.0, base=0,
                            pattern=[[-1, P]], channel_multiplier=1).then_inc(s_ident, 1)
            pool.wait_ge(s_ident, 1)
            g.tensor_copy(identb[:, :], ident[:, :]).then_inc(s_identb, 1)
            g.memset(before[:, :], 1.0).then_inc(s_before0, 1)
            pool.wait_ge(s_before0, 1)
            g.affine_select(out=before[:, :], in_=before[:, :], compare_op=ALU.is_ge, fill=0.0, base=-1,
                            pattern=[[1, P]], channel_multiplier=-1).then_inc(s_before, 1)
            pool.wait_ge(s_before, 1)
            g.tensor_copy(beforeb[:, :], before[:, :]).then_inc(s_before, 1)
            g.memset(onesb[:, :], 1.0).then_inc(s_onesb, 1)
            for i, value in enumerate((ROUND, -ROUND)):
                g.memset(rounder[:, i:i + 1], value).then_inc(s_rounder, 1)
            for e in range(E):
                g.memset(down[:, e:e + 1], float(E - e)).then_inc(s_down1, 1)
            g.iota(icol[:, :], pattern=[[1, P]], base=0, channel_multiplier=0).then_inc(s_iota, 1)
            g.iota(irow[:, :], pattern=[[1, 1]], base=0, channel_multiplier=1).then_inc(s_iota, 1)
            g.iota(ipad[:, :], pattern=[[P, PT]], base=PAIRS, channel_multiplier=1).then_inc(s_iota, 1)

            def split_lo(n):
                _, hi, lo, width = chunks[n]
                src = raw[:, n % RING, 0:width]
                if n >= CH_1:
                    src = src.rearrange("p (c h) -> p c h", h=H)
                pool.wait_ge(s_whi, n + 1)
                g.tensor_tensor(lo, src, hi, ALU.subtract).then_inc(s_wlo, 1)

            lo_done = [0]

            def lo(count):
                for _ in range(count):
                    split_lo(lo_done[0])
                    lo_done[0] += 1

            def spread(n, factors):
                return (diag[:, 0:n, :], ident[:, :].unsqueeze(1).to_broadcast([P, n, P]), factors.unsqueeze(2).to_broadcast([P, n, P]),
                        ALU.mult)

            lo(4)
            pool.wait_ge(s_srs, 4)
            for b in range(NB):
                for w in range(2):
                    if b >= 1:
                        pool.wait_ge(s_bc, 2 * b - 1 + w)
                    g.tensor_tensor(diag[:, 2 * w:2 * w + 2, :], ident[:, :].unsqueeze(1).to_broadcast([P, HC, P]),
                                    s_rs[:, w, b, :].unsqueeze(2).to_broadcast([P, HC, P]), ALU.mult).then_inc(s_diag, 1)
            lo(4)
            for b in range(NB):
                pool.wait_ge(s_inv1, b + 1)
                if b == 0:
                    pool.wait_ge(s_bc, 2 * NB)
                else:
                    pool.wait_ge(s_wbc, b)
                g.tensor_tensor(*spread(2, sc1[:, b, 2:4])).then_inc(s_diagw, 1)
                lo((1, 1, 2, 2)[b])
            for b in range(NB):
                pool.wait_ge(s_sg, b + 1)
                g.tensor_tensor(q2[:, b, 0:2, :], hq[:, b % 2, :, 0:I2], hq[:, b % 2, :, I2:2 * I2], ALU.mult).then_inc(s_a, 1)
            lo(2)
            pool.wait_ge(s_wbc, NB)
            pool.wait_ge(s_srs2, 1)
            for b in range(NB):
                if b >= 1:
                    pool.wait_ge(s_bc2, b)
                g.tensor_tensor(*spread(2, s_rs2[:, :, b])).then_inc(s_diag2, 1)
            lo(2)
            for b in range(NB):
                pool.wait_ge(s_inv2, b + 1)
                if b == 0:
                    pool.wait_ge(s_bc2, NB)
                else:
                    pool.wait_ge(s_cbc, b)
                g.tensor_tensor(*spread(2, sc2[:, b, 2:4])).then_inc(s_diagc, 1)
                lo(1)
            lo(CH_1 - lo_done[0])

            def gather(j):
                if j:
                    pool.wait_ge(s_xT, j)
                g.indirect_dma_start(out=xin[:, :], out_offset=None, in_=xn,
                                     in_offset=bass.IndirectOffsetOnAxis(ap=tok[:, j:j + 1], axis=0)).then_inc(d_xin, 16)

            def gather_base(j):
                if j >= 3:
                    pool.wait_ge(s_gadd, j - 1)
                    pool.wait_ge(s_uadd, j - 1)
                g.indirect_dma_start(out=bin_[:, j % 2].rearrange("p a i -> p (a i)"), out_offset=None, in_=gun,
                                     in_offset=bass.IndirectOffsetOnAxis(ap=tok[:, j:j + 1], axis=0)).then_inc(d_bin[j % 2], 16)

            def scatter(j):
                pool.wait_ge(s_yc, j + 1)
                g.indirect_dma_start(out=yg, out_offset=bass.IndirectOffsetOnAxis(ap=dest[:, j:j + 1], axis=0),
                                     in_=yb[:, :], in_offset=None).then_inc(d_y, 16)

            pool.wait_ge(s_plan, 1)
            pool.wait_ge(d_xn, 16 * NB)
            pool.wait_ge(s_share, 3)
            gather(0)
            gather(1)
            for i in range(2):
                pool.wait_ge(d_bn[i], 16 * NT // 2)
            pool.wait_ge(s_direct, 1)
            gather_base(1)
            gather_base(2)
            for n in range(CH_1, NCH):
                split_lo(n)
            for j in range(1, PT + 3):
                if 2 <= j < PT:
                    gather(j)
                if 3 <= j < PT:
                    gather_base(j)
                if j >= 3:
                    scatter(j - 3)
            for b in range(0, NB, 2):
                pool.wait_ge(s_out1, TB * (b + 1))
                pool.wait_ge(s_second, TB * (b + 1))
                bt = slice(TB * b, TB * (b + 1))
                g.tensor_tensor(xs_all[:, bt, :], xs_all[:, bt, :], yr[:, 1, bt, :], ALU.add).then_inc(s_sum[b], 1)

        @block.scalar
        def _(act):
            a = nc.scalar
            wv = fside.rearrange("b (j p) h -> p b j h", p=P)
            cv = ctxw.rearrange("b (j p) h -> p b j h", p=P)
            for b in range(NB):
                a.dma_start(q1[:, 2:4, b, :], wv[:, b]).then_inc(d_w[b], 16)
            for b in range(NB):
                a.dma_start(q2[:, b, 2:4, :], cv[:, b]).then_inc(d_c, 16)
            a.dma_start(cW[:, :], conf_W).then_inc(d_small, 16)
            a.dma_start(rows[:, 0, :], conf_b.rearrange("(a e) -> a e", a=1).to_broadcast([P, E])).then_inc(d_small, 16)
            a.dma_start(rows[:, 1, :], wealth.rearrange("(a e) -> a e", a=1).to_broadcast([P, E])).then_inc(d_small, 16)
            a.dma_start(gin[:, 0:1], g_xattn.rearrange("(a e) -> a e", a=1).to_broadcast([P, 1])).then_inc(d_small, 16)
            a.dma_start(gin[:, 1:2], g_ffn.rearrange("(a e) -> a e", a=1).to_broadcast([P, 1])).then_inc(d_small, 16)

            def split(count, end=CH_1):
                for _ in range(count):
                    if done[0] >= end:
                        break
                    n = done[0]
                    _, hi, _, width = chunks[n]
                    src = raw[:, n % RING, 0:width]
                    if n >= CH_1:
                        src = src.rearrange("p (c h) -> p c h", h=H)
                    act.wait_ge(d_raw[n % RING], landed[n])
                    a.copy(hi, src).then_inc(s_whi, 1)
                    done[0] += 1

            done = [0]
            act.wait_ge(s_var, 1)
            a.activation(rstd[:, :], mv[:, :, 1], ACT.Sqrt).then_inc(s_std, 1)
            split(4)
            act.wait_ge(s_ratio, 1)
            a.activation(s_rs[:, 1], tmp8[:, :, :], ACT.Sqrt).then_inc(s_sq, 1)
            split(4)
            def integers(b, clip, read, made, to, frm):
                act.wait_ge(clip, b + 1)
                if b >= 2:
                    act.wait_ge(read, b - 1)
                a.activation(to, frm, ACT.Identity, bias=rounder[:, 1:2]).then_inc(made, 1)

            def row_copy(b, made, used, copied):
                act.wait_ge(made, b + 1)
                if b >= 2:
                    act.wait_ge(used, b - 1)
                a.copy(wrow[:, b % 2, :], A[6 + b % 2][:, 0:S]).then_inc(copied, 1)

            act.wait_ge(s_rounder, 2)
            a.activation(warm[:, :], ones[:, 0:1], ACT.Silu).then_inc(s_warm, 1)
            for step in range(NB + 2):
                if step < NB:
                    for i in range(4):
                        act.wait_ge(s_inv1, step + 1)
                        a.activation(q1[:, i, step, :], q1[:, i, step, :], ACT.Identity, scale=inv1[:, step, i:i + 1],
                                     bias=rounder[:, 0:1]).then_inc(s_scaled, 1)
                b = step - 1
                if 0 <= b < NB:
                    integers(b, s_clip, s_q1Tp, s_q1i, q1i[:, b % 2], q1[:, :, b, :])
                    split(1)
                b = step - 2
                if 0 <= b < NB:
                    row_copy(b, s_wbc, s_deq1, s_wrow)
                    if b < 3:
                        split(1)
            for b in range(NB):
                act.wait_ge(s_deq1, b + 1)
                a.activation(hq[:, b % 2, :, 0:I2], hq[:, b % 2, :, 0:I2], ACT.Silu).then_inc(s_sg, 1)
            act.wait_ge(d_small, 80)
            a.activation(gates[:, :], gin[:, :], ACT.Tanh).then_inc(s_gate, 1)
            split(3)
            act.wait_ge(s_ratio2, 1)
            a.activation(s_rs2[:, 1], tmp4[:, :], ACT.Sqrt).then_inc(s_sq2, 1)
            for step in range(NB + 2):
                if step < NB:
                    for i in range(4):
                        act.wait_ge(s_inv2, step + 1)
                        a.activation(q2[:, step, i, :], q2[:, step, i, :], ACT.Identity, scale=inv2[:, step, i:i + 1],
                                     bias=rounder[:, 0:1]).then_inc(s_scaled2, 1)
                b = step - 1
                if 0 <= b < NB:
                    integers(b, s_clip2, s_q2Tp, s_q2i, q2i[:, b % 2], q2[:, b])
                b = step - 2
                if 0 <= b < NB:
                    act.wait_ge(s_q2Tp, b + 1)
                    if b >= 2:
                        act.wait_ge(s_mm2, b - 1)
                    a.copy(q2T[:, b % 2], Ab[b % 2][:, 0:2 * S].rearrange("p (a s) -> p a s", a=2)).then_inc(s_q2T, 1)
                    row_copy(b, s_cbc, s_deq2, s_crow)
                    if b < 2:
                        split(2)

            def x2_hi(b):
                act.wait_ge(s_x2Tp, b + 1)
                a.dma_start(xn[b * S:(b + 1) * S, :].rearrange("(t p) h -> p t h", p=P), q1[:, 0:2, b, :]).then_inc(d_xn, 16)
                a.copy(x2T_hi[:, b].rearrange("p c s -> p (c s)"), X2[b][:, :]).then_inc(s_x2hi, 1)

            act.wait_ge(s_q2i, NB)
            for b in range(NB):
                act.wait_ge(s_var2, b + 1)
                a.activation(rstd2[:, TB * b:TB * (b + 1)], mv2[:, TB * b:TB * (b + 1), 1], ACT.Sqrt).then_inc(s_std2, 1)
                if b >= 1:
                    x2_hi(b - 1)
                split(2)
            def base_out(t):
                for gu, (made, copied, pp) in enumerate(((s_bg, s_bgc, pG), (s_bu, s_buc, pU))):
                    act.wait_ge(made, t + 1)
                    if t >= 2 and gu == 0:
                        act.wait_ge(d_bn[t % 2], 16 * (t // 2))
                    elif t == 0 and gu == 0:
                        act.wait_ge(s_x1, NB)
                    a.copy(brow[:, t % 2, gu].rearrange("p (a i) -> p a i", a=2), pp[:, :, 0:IH]).then_inc(copied, 1)
                act.wait_ge(s_bgc, t + 1)
                act.wait_ge(s_buc, t + 1)
                a.dma_start(gun[t * P:(t + 1) * P, :], brow[:, t % 2].rearrange("p a i -> p (a i)")).then_inc(d_bn[t % 2], 16)

            x2_hi(NB - 1)
            base_out(0)
            for b in range(NB):
                act.wait_ge(s_confT, b + 1)
                a.copy(confT[:, b, :], A[6 - b % 2][0:E, 0:S]).then_inc(s_confTc, 1)
            act.wait_ge(s_logit, 1)
            a.activation(bids[:, :, :], bids[:, :, :], ACT.Sigmoid).then_inc(s_sig, 1)
            split(2)
            base_out(1)
            split(2)
            base_out(2)
            act.wait_ge(s_dif, 1)
            a.activation(share[:, 0, :], dif[:, :], ACT.Sigmoid).then_inc(s_share, 1)
            a.activation(share[:, 1, :], dif[:, :], ACT.Sigmoid, scale=-1.0).then_inc(s_share, 1)
            for t in range(3, PRE):
                split(3)
                base_out(t)
            split(CH_1)

            act.wait_ge(s_plan, 1)
            act.wait_ge(d_xn, 16 * NB)
            act.wait_ge(s_share, 3)

            def x_hi(j):
                act.wait_ge(s_xT, j + 1)
                if not (isinstance(j, int) and j == 0):
                    act.wait_ge(s_A, j)
                if isinstance(j, int) and j == 1:
                    act.wait_ge(s_direct, 1)
                a.copy(xT_hi[:, :, :].rearrange("p c q -> p (c q)"), pX[:, 0:H]).then_inc(s_xhi, 1)

            def xa_hi(j, first=False):
                act.wait_ge(s_xaT, j + 1)
                if not first:
                    act.wait_ge(s_u, j)
                a.copy(xaT_hi[:, :, :].rearrange("p a q -> p (a q)"), pX[:, H:H + 2 * P]).then_inc(s_xahi, 1)

            def group(j):
                src = gid[0:1, j:j + 1] if isinstance(j, int) else gid[0:1, bass.ds(j, 1)]
                return act.value_load(src, min_val=0, max_val=G - 1)

            def down_A_group(j, i, g):
                if isinstance(j, int) and j == 0:
                    act.wait_ge(s_wlo, CH_DA)
                else:
                    act.wait_ge(s_down, j)
                to, w = ((Wd_hi, WdA_hi), (Wd_lo, WdA_lo))[i]
                a.copy(to[:, :, H:H + GR], w[:, :, bass.ds(g, 1), :].rearrange("p c a r -> p c (a r)")).then_inc(s_Wd, 1)

            def silu(j):
                act.wait_ge(s_gadd, j + 1)
                a.activation(gb[:, :], gb[:, :], ACT.Silu).then_inc(s_silu, 1)

            def h_hi(j, first=False):
                act.wait_ge(s_hT, j + 1)
                if not first:
                    act.wait_ge(s_down, j)
                a.copy(hT_hi[:, :, :].rearrange("p c q -> p (c q)"),
                       pT[:, :, :].rearrange("p a q -> p (a q)")[:, 0:I]).then_inc(s_hhi, 1)

            def z_hi(j, first=False):
                act.wait_ge(s_zT, j + 1)
                if not first:
                    act.wait_ge(s_y, j)
                a.copy(zT_hi[:, :], pX[:, 0:P]).then_inc(s_zhi, 1)

            def tile(j, back=True, back2=True, back3=True, last=False):
                if back:
                    g = group(j - 1)
                    h_hi(j - 1, not back2)
                if back2:
                    z_hi(j - 2, not back3)
                if back:
                    down_A_group(j - 1, 0, g)
                    down_A_group(j - 1, 1, g)
                if not last:
                    x_hi(j + 1)
                silu(j)
                if not last:
                    xa_hi(j + 1)

            x_hi(0)
            for t in range(PRE, NT):
                base_out(t)
            xa_hi(0, first=True)
            a.activation(warm2[:, :], gates[:, 0:1], ACT.Silu).then_inc(s_warm, 1)
            x_hi(1)
            for i in range(2):
                act.wait_ge(d_bn[i], 16 * NT // 2)
            split(NCH - CH_1, NCH)
            silu(0)
            xa_hi(1)
            tile(1, back2=False)
            tile(2, back3=False)
            with act.Fori(3, PT - 1) as j:
                tile(j)
            tile(PT - 1, last=True)
            g = group(PT - 1)
            h_hi(PT - 1)
            z_hi(PT - 2)
            down_A_group(PT - 1, 0, g)
            down_A_group(PT - 1, 1, g)
            z_hi(PT - 1)
            for t in range(NT):
                act.wait_ge(d_rows[t // TB], 16 * K)
                a.activation(yr[:, 1, t, :], yr[:, 1, t, :], ACT.Copy, scale=share[:, 1, t:t + 1]).then_inc(s_second, 1)

        @block.vector
        def _(dve):
            v = nc.vector

            chains = [0]
            s_chain = sem("s_chain")

            def link(ins):
                ins.then_inc(s_chain, 1)
                chains[0] += 1
                dve.wait_ge(s_chain, chains[0])

            for t in range(NT):
                dve.wait_ge(d_x[t // TB], 16)
                v.bn_stats(bst[:, t, :], xs_all[:, t, :]).then_inc(s_stat, 1)
            for t in range(NT):
                dve.wait_ge(s_stat, t + 1)
                ins = v.bn_aggr(mv[:, t, :], bst[:, t, :])
            link(ins)
            v.tensor_scalar(mv[:, :, 1], mv[:, :, 1], LN_EPS, None, ALU.add).then_inc(s_var, 1)
            for b in range(NB):
                dve.wait_ge(s_wT, b + 1)
                v.tensor_reduce(amx[:, 1, b, :], A[4 + b][:, :].rearrange("p (c s) -> p c s", c=HC), AX_X, ALU.max,
                                apply_absolute_value=True).then_inc(s_wamax, 1)
            dve.wait_ge(s_std, 1)
            v.reciprocal(rstd[:, :], rstd[:, :]).then_inc(s_rstd, 1)
            dve.wait_ge(s_rstd, 1)
            for t in range(NT):
                v.tensor_scalar(q1[:, t % TB, t // TB, :], xs_all[:, t, :], mv[:, t, 0:1], rstd[:, t:t + 1],
                                ALU.subtract, ALU.mult).then_inc(s_xn, 1)
            for b in range(NB):
                dve.wait_ge(s_xT1, b + 1)
                v.tensor_reduce(amx[:, 0, b, :], A[b][:, :].rearrange("p (c s) -> p c s", c=HC), AX_X, ALU.max,
                                apply_absolute_value=True).then_inc(s_xamax, 1)
            dve.wait_ge(s_xamax, NB)
            dve.wait_ge(s_wamax, NB)
            v.tensor_scalar(amx[:, :, :, :], amx[:, :, :, :], EPS, None, ALU.max).then_inc(s_srs, 1)
            dve.wait_ge(s_srs, 1)
            v.reciprocal(tmp8[:, :, :], amx[:, 1]).then_inc(s_srs, 1)
            dve.wait_ge(s_srs, 2)
            v.tensor_tensor(tmp8[:, :, :], amx[:, 0], tmp8[:, :, :], ALU.mult).then_inc(s_ratio, 1)
            for b in range(NB):
                dve.wait_ge(s_cT, b // 2 + 1)
                v.tensor_reduce(amx2[:, 1, b:b + 1], A[6 + b // 2][:, (b % 2) * S:(b % 2 + 1) * S], AX_X, ALU.max,
                                apply_absolute_value=True).then_inc(s_camax, 1)
            dve.wait_ge(s_sq, 1)
            v.tensor_scalar(s_rs[:, 1], s_rs[:, 1], EPS, None, ALU.max).then_inc(s_srs, 1)
            dve.wait_ge(s_srs, 3)
            v.reciprocal(s_rs[:, 0], s_rs[:, 1]).then_inc(s_srs, 1)
            dve.wait_ge(s_srs, 4)

            def smooth(b):
                dve.wait_ge(s_xn, NT)
                dve.wait_ge(d_w[b], 16)
                for w in range(2):
                    dve.wait_ge(s_bc, 2 * b + 1 + w if b == 0 else 2 * b + 2)
                    qv = q1[:, 2 * w:2 * w + 2, b, :]
                    v.tensor_tensor(qv, qv, factors_bank(b, w)[:, w * H:(w + 1) * H].unsqueeze(1).to_broadcast([P, 2, H]), ALU.mult).then_inc(s_smooth, 1)
                dve.wait_ge(s_smooth, 2 * b + 2)
                v.tensor_reduce(am1[:, b, :], q1[:, :, b, :], AX_X, ALU.max, apply_absolute_value=True).then_inc(s_am1, 1)
                dve.wait_ge(s_am1, b + 1)
                scales(am1[:, b, :], inv1[:, b, :], sc1[:, b, :], s_inv1, b)

            def scales(am, inv, sc, s_inv, b):
                link(v.tensor_scalar(am, am, EPS, None, ALU.max))
                v.tensor_scalar(sc, am, 1.0 / QMAX, None, ALU.mult)
                link(v.reciprocal(inv, am))
                v.tensor_scalar(inv, inv, QMAX, None, ALU.mult).then_inc(s_inv, 1)

            def clip1(b):
                dve.wait_ge(s_scaled, 4 * b + 4)
                qf = q1[:, :, b, :]
                v.tensor_scalar(qf, qf, ROUND + QMAX, ROUND - QMAX, ALU.min, ALU.max).then_inc(s_clip, 1)

            def q1T_copy(b):
                dve.wait_ge(s_q1Tp, b + 1)
                if b >= 2:
                    dve.wait_ge(s_mm1, b - 1)
                v.tensor_copy(q1T[:, b % 2].rearrange("p a c s -> p (a c s)"), Ab[b % 2][:, :]).then_inc(s_q1T, 1)

            def deq1(b):
                dve.wait_ge(s_mm1, b + 1)
                dve.wait_ge(s_wrow, b + 1)
                if b >= 2:
                    dve.wait_ge(s_a, b - 1)
                for j in range(TB):
                    ins = v.scalar_tensor_tensor(out=hq[:, b % 2, j, :], in0=A[4 + b % 2][:, j * S:(j + 1) * S],
                                                 scalar=sc1[:, b, j:j + 1], in1=wrow[:, b % 2, :], op0=ALU.mult, op1=ALU.mult)
                ins.then_inc(s_deq1, 1)

            for step in range(NB + 3):
                if step < NB:
                    smooth(step)
                if 0 <= step - 1 < NB:
                    clip1(step - 1)
                if 0 <= step - 2 < NB:
                    q1T_copy(step - 2)
                if 0 <= step - 3 < NB:
                    deq1(step - 3)
            for b in range(NB):
                dve.wait_ge(s_aT, b + 1)
                ins = v.tensor_reduce(amx2[:, 0, b:b + 1], A[b][:, 0:S], AX_X, ALU.max, apply_absolute_value=True)
            link(ins)
            dve.wait_ge(s_camax, NB)
            link(v.tensor_scalar(amx2[:, :, :], amx2[:, :, :], EPS, None, ALU.max))
            link(v.reciprocal(tmp4[:, :], amx2[:, 1]))
            v.tensor_tensor(tmp4[:, :], amx2[:, 0], tmp4[:, :], ALU.mult).then_inc(s_ratio2, 1)
            dve.wait_ge(s_sq2, 1)
            link(v.tensor_scalar(s_rs2[:, 1], s_rs2[:, 1], EPS, None, ALU.max))
            v.reciprocal(s_rs2[:, 0], s_rs2[:, 1]).then_inc(s_srs2, 1)

            def smooth2(b):
                dve.wait_ge(s_bc2, b + 1)
                dve.wait_ge(d_c, 16 * NB)
                link(v.tensor_tensor(q2[:, b].rearrange("p (w j) q -> p w j q", w=2), q2[:, b].rearrange("p (w j) q -> p w j q", w=2),
                                     A[b][:, 0:2 * I2].rearrange("p (w q) -> p w q", w=2).unsqueeze(2).to_broadcast([P, 2, 2, I2]),
                                     ALU.mult))
                link(v.tensor_reduce(am2[:, b, :], q2[:, b], AX_X, ALU.max, apply_absolute_value=True))
                scales(am2[:, b, :], inv2[:, b, :], sc2[:, b, :], s_inv2, b)
                dve.wait_ge(s_inv2, b + 1)
                v.tensor_scalar(sc2g[:, b, :], sc2[:, b, 0:2], gates[:, 0:1], None, ALU.mult).then_inc(s_sc2g, 1)

            dve.wait_ge(s_a, NB)
            dve.wait_ge(s_gate, 1)
            def clip2(b):
                dve.wait_ge(s_scaled2, 4 * b + 4)
                qf = q2[:, b].rearrange("p i h -> p (i h)")
                v.tensor_scalar(qf, qf, ROUND + QMAX, ROUND - QMAX, ALU.min, ALU.max).then_inc(s_clip2, 1)

            def x1_norm(b):
                dve.wait_ge(s_std2, b + 1)
                rs = rstd2[:, TB * b:TB * (b + 1)]
                link(v.reciprocal(rs, rs))
                for t in range(TB * b, TB * (b + 1)):
                    v.tensor_scalar(q1[:, t % TB, t // TB, :], xs_all[:, t, :], mv2[:, t, 0:1], rstd2[:, t:t + 1],
                                    ALU.subtract, ALU.mult).then_inc(s_x2, 1)

            def x2_lo(b):
                dve.wait_ge(s_x2hi, b + 1)
                v.tensor_tensor(x2T_lo[:, b].rearrange("p c s -> p (c s)"), X2[b][:, :],
                                x2T_hi[:, b].rearrange("p c s -> p (c s)"), ALU.subtract).then_inc(s_x2lo, 1)

            def x1_rows(b):
                dve.wait_ge(s_mm2, b + 1)
                dve.wait_ge(s_crow, b + 1)
                dve.wait_ge(s_sc2g, b + 1)
                for j in range(TB):
                    ins = v.scalar_tensor_tensor(out=hq[:, b % 2, j, :], in0=A[4 + b % 2][:, j * H:(j + 1) * H],
                                                 scalar=sc2g[:, b, j:j + 1], in1=wrow[:, b % 2, :], op0=ALU.mult, op1=ALU.mult)
                ins.then_inc(s_deq2, 1)
                dve.wait_ge(s_deq2, b + 1)
                xv_ = xs_all[:, 2 * b:2 * b + 2, :]
                v.tensor_tensor(xv_, xv_, hq[:, b % 2], ALU.add).then_inc(s_x1, 1)
                dve.wait_ge(s_x1, b + 1)
                for t in range(TB * b, TB * (b + 1)):
                    ins = v.bn_stats(bst2[:, t, :], xs_all[:, t, :])
                link(ins)
                for t in range(TB * b, TB * (b + 1)):
                    ins = v.bn_aggr(mv2[:, t, :], bst2[:, t, :])
                link(ins)
                vs = mv2[:, TB * b:TB * (b + 1), 1]
                v.tensor_scalar(vs, vs, LN_EPS, None, ALU.add).then_inc(s_var2, 1)

            for step in range(NB + 5):
                if step < NB:
                    smooth2(step)
                if 0 <= step - 1 < NB:
                    clip2(step - 1)
                if 0 <= step - 3 < NB:
                    x1_rows(step - 3)
                if 0 <= step - 4 < NB:
                    x1_norm(step - 4)
                if step == 5:
                    dve.wait_ge(s_cWTp, 1)
                    pc = A[2][:, 0:HC * E].rearrange("p (c e) -> p c e", c=HC)
                    link(v.tensor_copy(cWT_hi[:, :, :], pc))
                    v.tensor_tensor(cWT_lo[:, :, :], pc, cWT_hi[:, :, :], ALU.subtract).then_inc(s_cWT, 1)
                if 0 <= step - 5:
                    x2_lo(step - 5)

            def row(r):
                return rows[:, r, :].unsqueeze(1).to_broadcast([P, NT, E])

            def per_tile(ap):
                return ap.unsqueeze(2).to_broadcast([P, NT, E])
            dve.wait_ge(s_conf, 1)
            dve.wait_ge(d_small, 80)
            v.tensor_tensor(bids[:, :, :], A[4][:, 0:NT * E].rearrange("p (t e) -> p t e", t=NT), row(0), ALU.add).then_inc(s_logit, 1)
            dve.wait_ge(s_sig, 1)
            dve.wait_ge(s_down1, E)
            down_b = down[:, :].unsqueeze(1).to_broadcast([P, NT, E])
            link(v.tensor_tensor(bids[:, :, :], bids[:, :, :], row(1), ALU.mult))
            for k in range(K):
                link(v.tensor_reduce(best[:, k, :], bids[:, :, :], AX_X, ALU.max))
                link(v.tensor_tensor(eq[:, :, :], bids[:, :, :], per_tile(best[:, k, :]), ALU.is_equal))
                link(v.tensor_tensor(eq[:, :, :], eq[:, :, :], down_b, ALU.mult))
                link(v.tensor_reduce(key[:, :], eq[:, :, :], AX_X, ALU.max))
                link(v.tensor_tensor(pick[:, k], down_b, per_tile(key[:, :]), ALU.is_equal))
                if k == 0:
                    link(v.scalar_tensor_tensor(out=bids[:, :, :], in0=pick[:, k], scalar=-BIG, in1=bids[:, :, :],
                                                op0=ALU.mult, op1=ALU.add))
                else:
                    v.tensor_tensor(dif[:, :], best[:, 0, :], best[:, 1, :], ALU.subtract).then_inc(s_dif, 1)
            pick_ = pick[:, :, :, :].rearrange("p k t (g a) -> p (k t) g a", a=GE)
            link(v.tensor_reduce(gp[:, :, :], pick_, AX_X, ALU.add))
            v.tensor_copy(pickb[:, :, :], gp[:, :, :]).then_inc(s_pickb, 1)
            v.tensor_reduce(par[:, :], pick_[:, :, :, 1], AX_X, ALU.add)
            dve.wait_ge(s_iota, 3)
            v.tensor_copy(fcol[:, :], icol[:, :])
            v.tensor_copy(frow[:, :], irow[:, :])
            v.tensor_copy(fpad[:, :], ipad[:, :])
            link(v.memset(csum[:, :, :], 0.0))

            dve.wait_ge(s_rank, 1)
            CNT = NG * G

            def floor_of(out_, in_, plus):
                link(v.tensor_scalar(out_, in_, 1.0 / P, plus - 0.5 + 0.5 / P, ALU.mult, ALU.add))
                link(v.tensor_scalar(out_, out_, ROUND, ROUND, ALU.add, ALU.subtract))

            floor_of(tiles_g[:, :], A[7][:, CNT:CNT + G], 1.0 - 1.0 / P)
            link(v.tensor_copy(csum[:, 0, G:2 * G], tiles_g[:, :]))
            for i, d in enumerate((1, 2)):
                link(v.tensor_tensor(csum[:, i + 1, G:2 * G], csum[:, i, G:2 * G], csum[:, i, G - d:2 * G - d], ALU.add))
            ends = csum[:, 2, G:2 * G]
            link(v.tensor_tensor(start_g[:, :], ends, tiles_g[:, :], ALU.subtract))
            link(v.scalar_tensor_tensor(out=place[:, :, :], in0=start_g[:, :].unsqueeze(1).to_broadcast([P, NG, G]), scalar=float(P),
                                        in1=A[7][:, 0:CNT].rearrange("p (g e) -> p g e", g=NG), op0=ALU.mult, op1=ALU.add))
            link(v.tensor_tensor(place[:, :, :], place[:, :, :], gp[:, :, :], ALU.mult))
            link(v.tensor_reduce(placef[:, :], place[:, :, :], AX_X, ALU.add))
            floor_of(ptile[:, :], placef[:, :], 0.0)
            link(v.scalar_tensor_tensor(out=prow[:, :], in0=ptile[:, :], scalar=-float(P), in1=placef[:, :], op0=ALU.mult, op1=ALU.add))
            v.tensor_tensor(atrow[:, :, :], prow[:, :].unsqueeze(2).to_broadcast([P, NG, P]),
                            fcol[:, :].unsqueeze(1).to_broadcast([P, NG, P]), ALU.is_equal).then_inc(s_atrow, 1)
            link(v.tensor_tensor(attile[:, :, :], ptile[:, :].unsqueeze(2).to_broadcast([P, NG, PT]),
                                 fcol[:, 0:PT].unsqueeze(1).to_broadcast([P, NG, PT]), ALU.is_equal))
            v.tensor_tensor(attrib[:, :, 0, :], attile[:, :, :], fcol[:, 0:NG].unsqueeze(2).to_broadcast([P, NG, PT]), ALU.mult)
            v.tensor_scalar(attrib[:, :, 1, :], attile[:, :, :], frow[:, :], None, ALU.mult)
            v.tensor_tensor(attrib[:, :, 2, :], attile[:, :, :], par[:, :].unsqueeze(2).to_broadcast([P, NG, PT]), ALU.mult)
            link(v.tensor_copy(attrib[:, :, 3, :], attile[:, :, :]))
            v.tensor_scalar(fpad[:, :], fpad[:, :], 1.0, None, ALU.mult).then_inc(s_attrib, 1)
            link(v.tensor_tensor(past[:, :, :], fcol[0:1, 0:PT].unsqueeze(2).to_broadcast([1, PT, G]),
                                 ends[0:1].unsqueeze(1).to_broadcast([1, PT, G]), ALU.is_ge))
            link(v.tensor_reduce(gidf[:, :], past[:, :, :], AX_X, ALU.add))
            link(v.tensor_scalar(gidf[:, :], gidf[:, :], float(G - 1), None, ALU.min))
            v.tensor_copy(gid[:, :], gidf[:, :])
            dve.wait_ge(s_sorted, 1)
            link(v.tensor_copy(sorted_[:, :, :], A[6][:, 0:4 * PT].rearrange("p (a j) -> p a j", a=4)))
            v.tensor_scalar(mask[:, :, 1], sorted_[:, 2, :], SCALING, None, ALU.mult)
            v.tensor_scalar(mask[:, :, 0], sorted_[:, 2, :], -SCALING, SCALING, ALU.mult, ALU.add)
            link(v.scalar_tensor_tensor(out=destf[:, :], in0=sorted_[:, 0, :], scalar=float(P), in1=sorted_[:, 1, :],
                                        op0=ALU.mult, op1=ALU.add))
            link(v.tensor_tensor(sorted_[:, 3, :], sorted_[:, 3, :], fpad[:, :], ALU.mult))
            link(v.tensor_tensor(destf[:, :], destf[:, :], fpad[:, :], ALU.add))
            link(v.tensor_tensor(destf[:, :], destf[:, :], sorted_[:, 3, :], ALU.subtract))
            link(v.tensor_copy(dest[:, :], destf[:, :]))
            v.tensor_scalar(tok[:, :], dest[:, :], NT * P - 1, None, ALU.bitwise_and).then_inc(s_plan, 1)
            dve.wait_ge(s_share, 2)
            v.tensor_scalar(share[:, :, :], share[:, :, :], gates[:, 1:2], None, ALU.mult).then_inc(s_share, 1)

            dve.wait_ge(s_plan, 1)
            dve.wait_ge(s_share, 3)
            dve.wait_ge(d_xn, 16 * NB)

            def x_lo(j):
                dve.wait_ge(s_xhi, j + 1)
                v.tensor_tensor(xT_lo[:, :, :].rearrange("p c q -> p (c q)"), pX[:, 0:H],
                                xT_hi[:, :, :].rearrange("p c q -> p (c q)"), ALU.subtract).then_inc(s_xlo, 1)

            def mask_of(j, a):
                m_ = mask[:, j, :] if isinstance(j, int) else mask[:, bass.ds(j, 1), :].rearrange("p a e -> p (a e)")
                if a == 1:
                    return m_.unsqueeze(2).to_broadcast([P, GE, R])
                return m_.unsqueeze(1).unsqueeze(3).to_broadcast([P, a, GE, R])

            def xa_mask(j, first=False):
                dve.wait_ge(s_A, j + 1)
                if not first:
                    dve.wait_ge(s_xaT, j)
                v.tensor_tensor(xa[:, :, :, :], pX[:, H:2 * H].rearrange("p (a e r) -> p a e r", a=2, e=GE), mask_of(j, 2),
                                ALU.mult).then_inc(s_xac, 1)

            def z_mask(j, first=False):
                dve.wait_ge(s_down, j + 1)
                if not first:
                    dve.wait_ge(s_zT, j)
                v.tensor_tensor(zb[:, :, :], pY[:, H:H + GR].rearrange("p (e r) -> p e r", e=GE), mask_of(j, 1),
                                ALU.mult).then_inc(s_zc, 1)

            def xa_lo(j):
                dve.wait_ge(s_xahi, j + 1)
                v.tensor_tensor(xaT_lo[:, :, :].rearrange("p a q -> p (a q)"), pX[:, H:H + 2 * P],
                                xaT_hi[:, :, :].rearrange("p a q -> p (a q)"), ALU.subtract).then_inc(s_xalo, 1)

            def halves(ap):
                return ap.rearrange("p (a i) -> p a i", a=2)

            def g_add(j, slot, first=False):
                dve.wait_ge(s_g, j + 1)
                if first:
                    v.tensor_copy(halves(gb[:, :]), pG[:, :, 0:IH]).then_inc(s_gadd, 1)
                    return
                dve.wait_ge(d_bin[slot], 8 * j + (0, 8)[slot])
                dve.wait_ge(s_h, j)
                v.tensor_tensor(halves(gb[:, :]), pG[:, :, 0:IH], halves(bin_[:, slot, 0, :]), ALU.add).then_inc(s_gadd, 1)

            def u_add(j, slot, first=False):
                dve.wait_ge(s_u, j + 1)
                if first:
                    v.tensor_copy(halves(hbuf[:, :]), pU[:, :, 0:IH]).then_inc(s_uadd, 1)
                    return
                dve.wait_ge(s_hT, j)
                v.tensor_tensor(halves(hbuf[:, :]), pU[:, :, 0:IH], halves(bin_[:, slot, 1, :]), ALU.add).then_inc(s_uadd, 1)

            def h_mul(j):
                dve.wait_ge(s_silu, j + 1)
                dve.wait_ge(s_uadd, j + 1)
                v.tensor_tensor(hbuf[:, :], hbuf[:, :], gb[:, :], ALU.mult).then_inc(s_h, 1)

            def h_lo(j):
                dve.wait_ge(s_hhi, j + 1)
                v.tensor_tensor(hT_lo[:, :, :].rearrange("p c q -> p (c q)"),
                                pT[:, :, :].rearrange("p a q -> p (a q)")[:, 0:I],
                                hT_hi[:, :, :].rearrange("p c q -> p (c q)"), ALU.subtract).then_inc(s_hlo, 1)

            def z_lo(j):
                dve.wait_ge(s_zhi, j + 1)
                v.tensor_tensor(zT_lo[:, :], pX[:, 0:P], zT_hi[:, :], ALU.subtract).then_inc(s_zlo, 1)

            def y_copy(j, first=False):
                dve.wait_ge(s_y, j + 1)
                if not first:
                    dve.wait_ge(d_y, 16 * j)
                v.tensor_copy(yb[:, :], pY[:, 0:H]).then_inc(s_yc, 1)

            def tile(j, slot, back=True, back2=True, back3=True, last=False):
                if back2:
                    z_lo(j - 2)
                if back:
                    h_lo(j - 1)
                if back2:
                    y_copy(j - 2, not back3)
                g_add(j, slot, not back)
                if not last:
                    x_lo(j + 1)
                u_add(j, slot, not back)
                h_mul(j)
                if not last:
                    xa_mask(j + 1)
                    xa_lo(j + 1)
                if back:
                    z_mask(j - 1, not back2)

            x_lo(0)
            xa_mask(0, True)
            xa_lo(0)
            x_lo(1)
            for i in range(2):
                dve.wait_ge(d_bn[i], 16 * NT // 2)
            g_add(0, 0, True)
            xa_mask(1)
            u_add(0, 0, True)
            xa_lo(1)
            h_mul(0)
            tile(1, 1, back2=False)
            tile(2, 0, back3=False)
            tile(3, 1)
            with dve.Fori(4, PT - 2, 2) as j:
                tile(j, 0)
                tile(j + 1, 1)
            tile(PT - 1, (PT - 1) % 2, last=True)
            z_lo(PT - 2)
            h_lo(PT - 1)
            y_copy(PT - 2)
            z_mask(PT - 1)
            z_lo(PT - 1)
            y_copy(PT - 1)
            for b in range(NB):
                dve.wait_ge(d_rows[b], 16 * K)
                for t in range(TB * b, TB * (b + 1)):
                    v.scalar_tensor_tensor(out=xs_all[:, t, :], in0=yr[:, 0, t, :], scalar=share[:, 0, t:t + 1],
                                           in1=xs_all[:, t, :], op0=ALU.mult, op1=ALU.add).then_inc(s_out1, 1)
                if b % 2:
                    dve.wait_ge(s_out1, TB * (b + 1))
                    dve.wait_ge(s_second, TB * (b + 1))
                    bt = slice(TB * b, TB * (b + 1))
                    v.tensor_tensor(xs_all[:, bt, :], xs_all[:, bt, :], yr[:, 1, bt, :], ALU.add).then_inc(s_sum[b], 1)

        @block.tensor
        def _(pe):
            m = nc.tensor
            pe.wait_ge(s_ident, 1)
            pe.wait_ge(s_identb, 1)
            pe.wait_ge(s_ones, 1)
            for b in range(NB):
                pe.wait_ge(d_w[b], 16)
                for c in range(HC):
                    for j in range(TB):
                        ins = m.transpose(A[4 + b][:, c * S + j * P:c * S + (j + 1) * P], q1[:, 2 + j, b, c * P:(c + 1) * P], ident[:, :])
                ins.then_inc(s_wT, 1)
            for b in range(NB):
                pe.wait_ge(s_xn, TB * (b + 1))
                for c in range(HC):
                    for j in range(TB):
                        ins = m.transpose(A[b][:, c * S + j * P:c * S + (j + 1) * P], q1[:, j, b, c * P:(c + 1) * P], ident[:, :])
                ins.then_inc(s_xT1, 1)
            for b in range(NB):
                pe.wait_ge(d_c, 16 * NB)
                pe.wait_ge(s_wamax, NB)
                for j in range(TB):
                    ins = m.transpose(A[6 + b // 2][:, (b % 2) * S + j * P:(b % 2) * S + (j + 1) * P], q2[:, b, 2 + j, :], ident[:, :])
                if b % 2:
                    ins.then_inc(s_cT, 1)
            pe.wait_ge(s_xamax, NB)
            for b in range(NB):
                for w in range(2):
                    pe.wait_ge(s_diag, 2 * b + w + 1)
                    m.matmul(factors_bank(b, w)[:, w * H:(w + 1) * H], ones[:, :], diag[:, 2 * w:2 * w + 2, :].rearrange("p a q -> p (a q)"),
                             start=True, stop=True).then_inc(s_bc, 1)
            pe.wait_ge(s_camax, NB)

            def products1(b):
                pe.wait_ge(s_q1T, b + 1)
                if b >= 2:
                    pe.wait_ge(s_deq1, b - 1)
                for j in range(TB):
                    for c in range(HC):
                        ins = m.matmul(A[4 + b % 2][:, j * S:(j + 1) * S], q1T[:, b % 2, 0, c, j * P:(j + 1) * P],
                                       q1T[:, b % 2, 1, c, :], start=(c == 0), stop=(c == HC - 1))
                ins.then_inc(s_mm1, 1)

            for b in range(NB):
                pe.wait_ge(s_q1i, b + 1)
                if b >= 2:
                    pe.wait_ge(s_q1T, b - 1)
                for w in range(2):
                    for c in range(HC):
                        for j in range(TB):
                            o = ((w * HC + c) * TB + j) * P
                            ins = m.transpose(Ab[b % 2][:, o:o + P], q1i[:, b % 2, 2 * w + j, c * P:(c + 1) * P], identb[:, :])
                ins.then_inc(s_q1Tp, 1)
                if b >= 1:
                    products1(b - 1)
                pe.wait_ge(s_diagw, b + 1)
                if b >= 2:
                    pe.wait_ge(s_wrow, b - 1)
                m.matmul(A[6 + b % 2][:, 0:S], ones[:, :], diag[:, 0:2, :].rearrange("p a q -> p (a q)"), start=True, stop=True).then_inc(s_wbc, 1)
            products1(NB - 1)
            pe.wait_ge(s_wrow, NB)
            pe.wait_ge(s_q1T, NB)
            for b in range(NB):
                pe.wait_ge(s_a, b + 1)
                for j in range(TB):
                    ins = m.transpose(A[b][:, j * P:(j + 1) * P], q2[:, b, j, :], ident[:, :])
                ins.then_inc(s_aT, 1)
            for b in range(NB):
                pe.wait_ge(s_diag2, b + 1)
                m.matmul(A[b][:, 0:2 * I2], ones[:, :], diag[:, 0:2, :].rearrange("p a q -> p (a q)"), start=True, stop=True).then_inc(s_bc2, 1)

            def products2(b):
                pe.wait_ge(s_q2T, b + 1)
                if b >= 2:
                    pe.wait_ge(s_deq2, b - 1)
                for j in range(TB):
                    ins = m.matmul(A[4 + b % 2][:, j * H:(j + 1) * H], q2T[:, b % 2, 0, j * P:(j + 1) * P], q2T[:, b % 2, 1, :],
                                   start=True, stop=True)
                ins.then_inc(s_mm2, 1)

            for b in range(NB):
                pe.wait_ge(s_q2i, b + 1)
                if b >= 2:
                    pe.wait_ge(s_q2T, b - 1)
                for i in range(4):
                    ins = m.transpose(Ab[b % 2][:, i * P:(i + 1) * P], q2i[:, b % 2, i, :], identb[:, :])
                ins.then_inc(s_q2Tp, 1)
                if b >= 1:
                    products2(b - 1)
                pe.wait_ge(s_diagc, b + 1)
                if b >= 2:
                    pe.wait_ge(s_crow, b - 1)
                m.matmul(A[6 + b % 2][:, 0:S], ones[:, :], diag[:, 0:2, :].rearrange("p a q -> p (a q)"), start=True, stop=True).then_inc(s_cbc, 1)
            products2(NB - 1)
            pe.wait_ge(d_small, 80)
            pe.wait_ge(s_inv2, NB)
            for c in range(HC):
                ins = m.transpose(A[2][:, c * E:(c + 1) * E], cW[:, c * P:(c + 1) * P], ident[0:E, 0:E])
            ins.then_inc(s_cWTp, 1)
            split_product = products_of(m)

            def logits(b):
                if b >= 2:
                    pe.wait_ge(s_confTc, b - 1)
                else:
                    pe.wait_ge(s_cWT, 1)
                for c in range(HC):
                    ins = split_product([A[6 - b % 2][0:E, 0:S]], cWT_hi[:, c, :], cWT_lo[:, c, :],
                                        [x2T_hi[:, b, c, :]], [x2T_lo[:, b, c, :]], c == 0, c == HC - 1)
                ins.then_inc(s_confT, 1)

            def x2_T(b):
                if b == 3:
                    pe.wait_ge(s_crow, NB)
                elif b >= 1:
                    pe.wait_ge(s_deq2, NB - 2 + b)
                pe.wait_ge(s_x2, TB * (b + 1))
                for c in range(HC):
                    for j in range(TB):
                        ins = m.transpose(X2[b][:, c * S + j * P:c * S + (j + 1) * P], q1[:, j, b, c * P:(c + 1) * P], ident[:, :])
                ins.then_inc(s_x2Tp, 1)

            def base_product(gu, c, x_hi, x_lo, last):
                pp = (pG, pU)[gu]
                return split_product([pp[:, i, 0:IH] for i in range(2)], x_hi, x_lo,
                                     [Wbase_hi[:, gu, c, i * IH:(i + 1) * IH] for i in range(2)],
                                     [Wbase_lo[:, gu, c, i * IH:(i + 1) * IH] for i in range(2)], c == 0, last)

            def base(t):
                b, q = t // TB, slice((t % TB) * P, (t % TB + 1) * P)
                for gu, (made, copied) in enumerate(((s_bg, s_bgc), (s_bu, s_buc))):
                    if t >= 1:
                        pe.wait_ge(copied, t)
                    for c in range(HC):
                        if t == 0:
                            pe.wait_ge(s_wlo, 2 * (gu * HC + c + 1))
                        ins = base_product(gu, c, x2T_hi[:, b, c, q], x2T_lo[:, b, c, q], c == HC - 1)
                    ins.then_inc(made, 1)

            for b in range(NB):
                x2_T(b)
            pe.wait_ge(s_q2T, NB)
            pe.wait_ge(s_cWT, 1)
            pe.wait_ge(s_x2lo, 1)
            base(0)
            for b in range(NB):
                pe.wait_ge(s_x2lo, max(b + 1, 3) if b % 2 else b + 1)
                logits(b)
            pe.wait_ge(s_confTc, NB)
            for t in range(NT):
                q = (t % TB) * P
                ins = m.transpose(A[4][:, t * E:(t + 1) * E], confT[:, t // TB, q:q + P], ident[0:E, 0:E])
            ins.then_inc(s_conf, 1)
            base(1)

            pe.wait_ge(s_pickb, 1)
            pe.wait_ge(s_before, 2)
            pe.wait_ge(s_onesb, 1)
            CNT = NG * G
            pf = pickb[:, :, :].rearrange("p g e -> p (g e)")
            m.matmul(A[7][:, 0:CNT], beforeb[:, :], pf, start=True, stop=True)
            for d in range(1, NG):
                m.matmul(A[7][:, d * G:CNT], onesb[:, :], pf[:, 0:CNT - d * G], start=False, stop=True, skip_group_check=True)
            for g in range(NG):
                ins = m.matmul(A[7][:, CNT:CNT + G], onesb[:, :], pickb[:, g, :], start=False, stop=(g == NG - 1), skip_group_check=True)
            ins.then_inc(s_rank, 1)
            base(2)
            base(3)
            pe.wait_ge(s_atrow, 1)
            pe.wait_ge(s_attrib, 1)
            for g in range(NG):
                ins = m.matmul(A[6][:, 0:4 * PT], atrow[:, g, :], attrib[:, g].rearrange("p a j -> p (a j)"),
                               start=(g == 0), stop=(g == NG - 1))
            ins.then_inc(s_sorted, 1)
            for t in range(4, PRE):
                base(t)

            pe.wait_ge(s_plan, 1)

            def group(j):
                src = gid[0:1, j:j + 1] if isinstance(j, int) else gid[0:1, bass.ds(j, 1)]
                return pe.value_load(src, min_val=0, max_val=G - 1)

            def x_T(j, first=False):
                pe.wait_ge(d_xin, 16 * (j + 1))
                for c in range(HC):
                    ins = m.transpose(pX[:, c * P:(c + 1) * P], xin[:, c * P:(c + 1) * P], ident[:, :])
                ins.then_inc(s_xT, 1)

            def project_A(j, e, first=False):
                pe.wait_ge(s_xlo, j + 1)
                for c in range(HC):
                    wsl = [w[:, c, :, bass.ds(e, 1), :].rearrange("p a g r -> p a (g r)") for w in (WA_hi, WA_lo)]
                    ins = split_product([pX[:, H:2 * H].rearrange("p (a r) -> p a r", a=2)], xT_hi[:, c, :], xT_lo[:, c, :],
                                        [wsl[0]], [wsl[1]], c == 0, c == HC - 1)
                ins.then_inc(s_A, 1)

            def xa_T(j):
                pe.wait_ge(s_xac, j + 1)
                for gu in range(2):
                    ins = m.transpose(pX[:, H + gu * P:H + (gu + 1) * P], xa[:, gu].rearrange("p e r -> p (e r)"), ident[:, :])
                ins.then_inc(s_xaT, 1)

            def expand_B(j, gu, halves_, e, first=False):
                if halves_[0] == 0:
                    if gu == 0:
                        pe.wait_ge(s_xalo, j + 1)
                    if first:
                        pe.wait_ge(s_wlo, CH_B)
                    else:
                        pe.wait_ge((s_gadd, s_uadd)[gu], j)
                pp = (pG, pU)[gu]
                for i in halves_:
                    wsl = [w[:, gu, bass.ds(e, 1), i * IH:(i + 1) * IH].rearrange("p a w -> p (a w)") for w in (WB_hi, WB_lo)]
                    ins = split_product([pp[:, i, 0:IH]], xaT_hi[:, gu, :], xaT_lo[:, gu, :], [wsl[0]], [wsl[1]], not first, True)
                if i == 1:
                    ins.then_inc((s_g, s_u)[gu], 1)

            def h_T(j, first=False):
                pe.wait_ge(s_h, j + 1)
                if not first:
                    pe.wait_ge(s_hlo, j)
                for c in range(IC):
                    ins = m.transpose(pT[:, c // 4, (c % 4) * P:(c % 4 + 1) * P], hbuf[:, c * P:(c + 1) * P], ident[:, :])
                ins.then_inc(s_hT, 1)

            def down_products(j, chunks_, first=False):
                if chunks_[0] == 0:
                    pe.wait_ge(s_hlo, j + 1)
                    pe.wait_ge(s_Wd, 2 * (j + 1))
                    if first:
                        pe.wait_ge(s_wlo, NCH)
                    else:
                        pe.wait_ge(s_yc, j)
                        pe.wait_ge(s_zc, j)
                for c in chunks_:
                    ins = split_product([pY[:, 0:H + GR]], hT_hi[:, c, :], hT_lo[:, c, :],
                                        [Wd_hi[:, c, :]], [Wd_lo[:, c, :]], c == 0, c == IC - 1)
                if c == IC - 1:
                    ins.then_inc(s_down, 1)

            def z_T(j):
                pe.wait_ge(s_zc, j + 1)
                m.transpose(pX[:, 0:P], zb[:, :, :].rearrange("p e r -> p (e r)"), ident[:, :]).then_inc(s_zT, 1)

            def down_B_products(j, e):
                pe.wait_ge(s_zlo, j + 1)
                wsl = [w[:, bass.ds(e, 1), :].rearrange("p a w -> p (a w)") for w in (WdB_hi, WdB_lo)]
                split_product([pY[:, 0:H]], zT_hi[:, :], zT_lo[:, :], [wsl[0]], [wsl[1]], False, True).then_inc(s_y, 1)

            def tile(j, back2=True, last=False):
                e = group(j)
                expand_B(j, 0, (0,), e)
                if back2:
                    z_T(j - 2)
                expand_B(j, 0, (1,), e)
                expand_B(j, 1, (0,), e)
                if back2:
                    down_B_products(j - 2, group(j - 2))
                expand_B(j, 1, (1,), e)
                if not last:
                    x_T(j + 1)
                down_products(j - 1, range(0, 3), not back2)
                if not last:
                    project_A(j + 1, group(j + 1))
                down_products(j - 1, range(3, IC - 1), not back2)
                if not last:
                    xa_T(j + 1)
                down_products(j - 1, range(IC - 1, IC), not back2)
                h_T(j)

            x_T(0)
            base(PRE)
            pe.wait_ge(s_wlo, CH_A)
            project_A(0, group(0))
            base(PRE + 1)
            xa_T(0)
            for gu, copied in enumerate((s_bgc, s_buc)):
                pe.wait_ge(copied, NT)
                for c in range(HC):
                    ins = base_product(gu, c, xT_hi[:, c, :], xT_lo[:, c, :], False)
            ins.then_inc(s_direct, 1)
            pe.wait_ge(s_xalo, 1)
            x_T(1)
            e = group(0)
            expand_B(0, 0, (0, 1), e, True)
            project_A(1, group(1))
            expand_B(0, 1, (0, 1), e, True)
            xa_T(1)
            h_T(0, True)
            tile(1, back2=False)
            tile(2)
            tile(3)
            with pe.Fori(4, PT - 2, 2) as j:
                tile(j)
                tile(j + 1)
            tile(PT - 1, last=True)
            z_T(PT - 2)
            down_B_products(PT - 2, group(PT - 2))
            down_products(PT - 1, range(IC))
            z_T(PT - 1)
            down_B_products(PT - 1, group(PT - 1))


_INS = ['x', 'fside_BxS2xS2_0', 'ctx_1024', 'g_xattn', 'g_ffn', 'L0_ffn_expert_wealth', 'L0_ffn_conf_W', 'L0_ffn_conf_b',
        'L0_ffn_base_gate', 'L0_ffn_base_up', 'L0_ffn_base_down', 'L0_ffn_gate_A', 'L0_ffn_gate_B', 'L0_ffn_up_A',
        'L0_ffn_up_B', 'L0_ffn_down_A', 'L0_ffn_down_B']


def kernel(**inputs):
    import numpy as _np
    import concourse.bacc as _bacc
    from concourse import mybir as _mybir
    from concourse.bass_utils import run_bass_kernel_spmd as _run

    nc = _bacc.Bacc("TRN2", target_bir_lowering=False, num_devices=1)
    arrays, args = {}, []
    for name in _INS:
        a = _np.ascontiguousarray(inputs[name])
        arrays[f"in_{name}_dram"] = a
        args.append(nc.dram_tensor(f"in_{name}_dram", a.shape, _mybir.dt.from_np(a.dtype), kind="ExternalInput").ap())
    shape = inputs['x'].shape
    tokens, pairs = shape[0] * shape[1], 2 * shape[0] * shape[1]
    tiles = pair_tiles(pairs, inputs['L0_ffn_gate_A'].shape[0] // GE)
    for name, rows, cols in (("normed", tokens, shape[2]), ("base_products", tokens, 2 * inputs['L0_ffn_base_gate'].shape[1]),
                             ("results", pairs + 128 * tiles, shape[2])):
        args.append(nc.dram_tensor(name, [rows, cols], _mybir.dt.float32, kind="Internal").ap())
    args.append(nc.dram_tensor("out_0_dram", shape, _mybir.dt.from_np(_np.dtype('float32')), kind="ExternalOutput").ap())
    build(nc, *args)
    r = _run(nc, [arrays], core_ids=[0])
    return r.results[0]["out_0_dram"]
```
